# Optimizing a Trainium2 kernel written in Bass

```python
import numpy as np
import jax
import jax.numpy as jnp

def _softmax(x, axis=-1):
    return jax.nn.softmax(x, axis=axis)

def _gelu(x):
    return jax.nn.gelu(x, approximate=True)

def _silu(x):
    return jax.nn.silu(x)

def _sigmoid(x):
    return jax.nn.sigmoid(x)

def _layernorm(x, axis=-1, eps=1e-05):
    m = jnp.mean(x, axis=axis, keepdims=True)
    v = jnp.var(x, axis=axis, keepdims=True)
    return (x - m) / jnp.sqrt(v + eps)

def _scatter_add(tgt, idx, src, axis=0):
    return tgt.at[idx].add(src)

def _segment_sum(src, seg, n):
    return jax.ops.segment_sum(src, seg, n)
kernel_name = 'mk_xattn_ffn_d2_seqx_r4_38fad4'

def setup_inputs(seed: int=0):
    np.random.seed(seed)
    _w = jnp.asarray

    def _rec_inputs():
        import jax
        import jax.numpy as jnp
        _rk = jax.random.key(seed)
        x = -0.0002928 + 1 * jax.random.normal(jax.random.fold_in(_rk, 1), (16, 256, 256), jnp.float32)
        _lenS = 256 - jax.random.randint(jax.random.fold_in(_rk, 7), (16,), 0, max(1, 256 // 4) + 1, jnp.int32)
        _lenS2 = 256 - jax.random.randint(jax.random.fold_in(_rk, 8), (16,), 0, max(1, 256 // 4) + 1, jnp.int32)
        _ctx_1024P = jax.random.normal(jax.random.fold_in(_rk, 11), (16, 16, 256), jnp.float32)
        _ctx_1024c = jax.random.dirichlet(jax.random.fold_in(_rk, 511), 0.3 * jnp.ones((16,), jnp.float32), (16, 256))
        _ctx_1024t = jnp.einsum('bsk,bkd->bsd', _ctx_1024c, _ctx_1024P)
        _ctx_1024t = _ctx_1024t * jax.lax.rsqrt(jnp.mean(jnp.square(_ctx_1024t)) + 1e-12) * 0.953939
        ctx_1024 = -1.39393e-06 + 0.999914 * (_ctx_1024t + 0.3 * jax.random.normal(jax.random.fold_in(_rk, 611), (16, 256, 256), jnp.float32))
        _validS = jnp.arange(256)[None, :] < _lenS[:, None]
        _validS2 = jnp.arange(256)[None, :] < _lenS2[:, None]
        _causal = jnp.tril(jnp.ones((256, 256), dtype=bool))
        mask_Bx1xSxS2_ik1 = jnp.where(jnp.broadcast_to(_validS2[:, None, None, :], (16, 1, 256, 256)), 1, 0).astype(jnp.int32)
        return (x, ctx_1024, mask_Bx1xSxS2_ik1)
    x, ctx_1024, mask_Bx1xSxS2_ik1 = _rec_inputs()

    def _L0_xattn_setup():
        import jax, jax.numpy as jnp
        import numpy as np
        D_MODEL = 256
        N_HEADS = 16
        D_HEAD = D_MODEL // N_HEADS
        WINDOW = 128

        def _attn(q, k, v, Wq, bq, Wk, bk, Wv, bv, Wo, bo):
            B, L, D = q.shape
            H, Dh = (N_HEADS, D_HEAD)
            qh = (q @ Wq.T + bq).reshape(B, L, H, Dh).transpose(0, 2, 1, 3)
            kh = (k @ Wk.T + bk).reshape(B, L, H, Dh).transpose(0, 2, 1, 3)
            vh = (v @ Wv.T + bv).reshape(B, L, H, Dh).transpose(0, 2, 1, 3)
            scale = jnp.sqrt(jnp.asarray(Dh, q.dtype))
            scores = jnp.einsum('bhqd,bhkd->bhqk', qh, kh) / scale
            pos = jnp.arange(L)
            band = jnp.abs(pos[:, None] - pos[None, :]) <= WINDOW
            scores = jnp.where(band[None, None], scores, -jnp.inf)
            w = jax.nn.softmax(scores, axis=-1)
            out = jnp.einsum('bhqk,bhkd->bhqd', w, vh)
            out = out.transpose(0, 2, 1, 3).reshape(B, L, D)
            return out @ Wo.T + bo
        key = jax.random.key(seed)
        ks = jax.random.split(key, 11)
        B, L = (2, 512)
        s = 1.0 / np.sqrt(D_MODEL)
        inp = {'q': jax.random.normal(ks[0], (B, L, D_MODEL), jnp.float32), 'k': jax.random.normal(ks[1], (B, L, D_MODEL), jnp.float32), 'v': jax.random.normal(ks[2], (B, L, D_MODEL), jnp.float32), 'Wq': jax.random.normal(ks[3], (D_MODEL, D_MODEL), jnp.float32) * s, 'bq': jnp.zeros((D_MODEL,), jnp.float32), 'Wk': jax.random.normal(ks[4], (D_MODEL, D_MODEL), jnp.float32) * s, 'bk': jnp.zeros((D_MODEL,), jnp.float32), 'Wv': jax.random.normal(ks[5], (D_MODEL, D_MODEL), jnp.float32) * s, 'bv': jnp.zeros((D_MODEL,), jnp.float32), 'Wo': jax.random.normal(ks[6], (D_MODEL, D_MODEL), jnp.float32) * s, 'bo': jnp.zeros((D_MODEL,), jnp.float32)}
        return inp
    _L0_xattn_all = _L0_xattn_setup()
    _L0_xattn_in = {k: v for k, v in _L0_xattn_all.items() if k in ('Wq', 'bq', 'Wk', 'bk', 'Wv', 'bv', 'Wo', 'bo')}
    del _L0_xattn_all

    def _L0_ffn_setup():
        import jax, jax.numpy as jnp
        import numpy as np
        DIM = 256

        def _reference_tuple_inner(x, W_r, W_k, W_v, mu_r, mu_k):
            B, T, C = x.shape
            x_prev = jnp.concatenate([jnp.zeros((B, 1, C), x.dtype), x[:, :-1, :]], axis=1)
            xr = mu_r * x + (1.0 - mu_r) * x_prev
            xk = mu_k * x + (1.0 - mu_k) * x_prev
            r = jax.nn.sigmoid(jnp.einsum('btc,dc->btd', xr, W_r))
            k = jnp.einsum('btc,dc->btd', xk, W_k)
            k_act = jnp.square(jax.nn.relu(k))
            out = r * jnp.einsum('btc,dc->btd', k_act, W_v)
            new_state = x[:, -1, :]
            return (out, new_state)
        key = jax.random.key(seed)
        ks = jax.random.split(key, 6)
        B, T, C = (8, 512, DIM)
        x = jax.random.normal(ks[0], (B, T, C), dtype=jnp.float32)
        s = 1.0 / np.sqrt(C)
        W_r = jax.random.uniform(ks[1], (C, C), jnp.float32, -s, s)
        W_k = jax.random.uniform(ks[2], (C, C), jnp.float32, -s, s)
        W_v = jax.random.uniform(ks[3], (C, C), jnp.float32, -s, s)
        mu_r = jax.random.uniform(ks[4], (C,), jnp.float32)
        mu_k = jax.random.uniform(ks[5], (C,), jnp.float32)
        return {'x': x, 'W_r': W_r, 'W_k': W_k, 'W_v': W_v, 'mu_r': mu_r, 'mu_k': mu_k}
    _L0_ffn_all = _L0_ffn_setup()
    _L0_ffn_in = {k: v for k, v in _L0_ffn_all.items() if k in ('W_r', 'W_k', 'W_v', 'mu_r', 'mu_k')}
    del _L0_ffn_all

    def _L1_xattn_setup():
        import jax, jax.numpy as jnp
        import numpy as np
        HEADS = 16
        EMBED_DIM = 256
        HEAD_DIM = EMBED_DIM // HEADS
        N, Q_LEN, KV_LEN = (4, 512, 512)
        key = jax.random.key(seed)
        k1, k2, k3, k4, k5, k6 = jax.random.split(key, 6)
        query = jax.random.normal(k1, (N, Q_LEN, EMBED_DIM), dtype=jnp.float32)
        key_t = jax.random.normal(k2, (N, KV_LEN, EMBED_DIM), dtype=jnp.float32)
        value = jax.random.normal(k3, (N, KV_LEN, EMBED_DIM), dtype=jnp.float32)
        mask = jax.random.randint(k4, (N, 1, Q_LEN, KV_LEN), 0, 2, dtype=jnp.int32)
        W_out = jax.random.normal(k5, (EMBED_DIM, EMBED_DIM), dtype=jnp.float32) / np.sqrt(EMBED_DIM)
        b_out = jax.random.normal(k6, (EMBED_DIM,), dtype=jnp.float32) * 0.01
        return {'query': query, 'key': key_t, 'value': value, 'mask': mask, 'W_out': W_out, 'b_out': b_out}
    _L1_xattn_all = _L1_xattn_setup()
    _L1_xattn_in = {k: v for k, v in _L1_xattn_all.items() if k in ('W_out', 'b_out')}
    del _L1_xattn_all

    def _L1_ffn_setup():
        import jax, jax.numpy as jnp
        import numpy as np
        BLOCK = 32
        W_BITS = 4
        ACT_BITS = 16

        def act_qdq(x):
            qmax = 2.0 ** (ACT_BITS - 1) - 1.0
            scale = jnp.maximum(jnp.max(jnp.abs(x)) / qmax, 1e-12)
            return jnp.clip(jnp.round(x / scale), -qmax - 1.0, qmax) * scale

        def fixed_qdq_u16(x):
            scale = 1.0 / 65536.0
            return jnp.clip(jnp.round(x / scale), 0.0, 65535.0) * scale

        def lpbq_dequant(w):
            O, I = w.shape
            qmax = 2.0 ** (W_BITS - 1) - 1.0
            wb = w.reshape(O, I // BLOCK, BLOCK)
            s = jnp.maximum(jnp.max(jnp.abs(wb), axis=-1, keepdims=True) / qmax, 1e-12)
            wq = jnp.clip(jnp.round(wb / s), -qmax - 1.0, qmax) * s
            return wq.reshape(O, I)
        key = jax.random.key(seed)
        k1, k2, k3, k4 = jax.random.split(key, 4)
        B, S, H, I = (2, 1024, 256, 768)
        x = jax.random.normal(k1, (B, S, H), jnp.float32)
        w_gate = jax.random.normal(k2, (I, H), jnp.float32) * 0.02
        w_up = jax.random.normal(k3, (I, H), jnp.float32) * 0.02
        w_down = jax.random.normal(k4, (H, I), jnp.float32) * 0.02
        return {'x': x, 'w_gate': w_gate, 'w_up': w_up, 'w_down': w_down}
    _L1_ffn_all = _L1_ffn_setup()
    _L1_ffn_in = {k: v for k, v in _L1_ffn_all.items() if k in ('w_gate', 'w_up', 'w_down')}
    del _L1_ffn_all
    return {'x': x, 'ctx_1024': ctx_1024, 'mask_Bx1xSxS2_ik1': mask_Bx1xSxS2_ik1, 'L0_xattn_Wq': _L0_xattn_in['Wq'], 'L0_xattn_bq': _L0_xattn_in['bq'], 'L0_xattn_Wk': _L0_xattn_in['Wk'], 'L0_xattn_bk': _L0_xattn_in['bk'], 'L0_xattn_Wv': _L0_xattn_in['Wv'], 'L0_xattn_bv': _L0_xattn_in['bv'], 'L0_xattn_Wo': _L0_xattn_in['Wo'], 'L0_xattn_bo': _L0_xattn_in['bo'], 'L0_ffn_W_r': _L0_ffn_in['W_r'], 'L0_ffn_W_k': _L0_ffn_in['W_k'], 'L0_ffn_W_v': _L0_ffn_in['W_v'], 'L0_ffn_mu_r': _L0_ffn_in['mu_r'], 'L0_ffn_mu_k': _L0_ffn_in['mu_k'], 'L1_xattn_W_out': _L1_xattn_in['W_out'], 'L1_xattn_b_out': _L1_xattn_in['b_out'], 'L1_ffn_w_gate': _L1_ffn_in['w_gate'], 'L1_ffn_w_up': _L1_ffn_in['w_up'], 'L1_ffn_w_down': _L1_ffn_in['w_down']}

def reference(x, ctx_1024, mask_Bx1xSxS2_ik1, L0_xattn_Wq, L0_xattn_bq, L0_xattn_Wk, L0_xattn_bk, L0_xattn_Wv, L0_xattn_bv, L0_xattn_Wo, L0_xattn_bo, L0_ffn_W_r, L0_ffn_W_k, L0_ffn_W_v, L0_ffn_mu_r, L0_ffn_mu_k, L1_xattn_W_out, L1_xattn_b_out, L1_ffn_w_gate, L1_ffn_w_up, L1_ffn_w_down):
    import jax
    import jax.numpy as jnp

    def _L0_xattn_ref(q, k, v, Wq, bq, Wk, bk, Wv, bv, Wo, bo):
        import jax, jax.numpy as jnp
        import numpy as np
        D_MODEL = 256
        N_HEADS = 16
        D_HEAD = D_MODEL // N_HEADS
        WINDOW = 128

        def _attn(q, k, v, Wq, bq, Wk, bk, Wv, bv, Wo, bo):
            B, L, D = q.shape
            H, Dh = (N_HEADS, D_HEAD)
            qh = (q @ Wq.T + bq).reshape(B, L, H, Dh).transpose(0, 2, 1, 3)
            kh = (k @ Wk.T + bk).reshape(B, L, H, Dh).transpose(0, 2, 1, 3)
            vh = (v @ Wv.T + bv).reshape(B, L, H, Dh).transpose(0, 2, 1, 3)
            scale = jnp.sqrt(jnp.asarray(Dh, q.dtype))
            scores = jnp.einsum('bhqd,bhkd->bhqk', qh, kh) / scale
            pos = jnp.arange(L)
            band = jnp.abs(pos[:, None] - pos[None, :]) <= WINDOW
            scores = jnp.where(band[None, None], scores, -jnp.inf)
            w = jax.nn.softmax(scores, axis=-1)
            out = jnp.einsum('bhqk,bhkd->bhqd', w, vh)
            out = out.transpose(0, 2, 1, 3).reshape(B, L, D)
            return out @ Wo.T + bo
        return _attn(q, k, v, Wq, bq, Wk, bk, Wv, bv, Wo, bo)

    def _L0_ffn_ref(x, W_r, W_k, W_v, mu_r, mu_k):
        import jax, jax.numpy as jnp
        import numpy as np
        DIM = 256

        def _reference_tuple_inner(x, W_r, W_k, W_v, mu_r, mu_k):
            B, T, C = x.shape
            x_prev = jnp.concatenate([jnp.zeros((B, 1, C), x.dtype), x[:, :-1, :]], axis=1)
            xr = mu_r * x + (1.0 - mu_r) * x_prev
            xk = mu_k * x + (1.0 - mu_k) * x_prev
            r = jax.nn.sigmoid(jnp.einsum('btc,dc->btd', xr, W_r))
            k = jnp.einsum('btc,dc->btd', xk, W_k)
            k_act = jnp.square(jax.nn.relu(k))
            out = r * jnp.einsum('btc,dc->btd', k_act, W_v)
            new_state = x[:, -1, :]
            return (out, new_state)
        return _reference_tuple_inner(x, W_r, W_k, W_v, mu_r, mu_k)[0]

    def _L1_xattn_ref(query, key, value, mask, W_out, b_out):
        import jax, jax.numpy as jnp
        import numpy as np
        HEADS = 16
        EMBED_DIM = 256
        HEAD_DIM = EMBED_DIM // HEADS
        N, Q_LEN, KV_LEN = (4, 512, 512)
        n, q_len, _ = query.shape
        k_len = key.shape[1]
        q = query.reshape(n, q_len, HEADS, HEAD_DIM)
        k = key.reshape(n, k_len, HEADS, HEAD_DIM)
        v = value.reshape(n, k_len, HEADS, HEAD_DIM)
        scores = jnp.einsum('nqhd,nkhd->nhqk', q, k)
        scores = jnp.where(mask == 0, jnp.float32(-1000000000.0), scores)
        attn = jax.nn.softmax(scores / jnp.sqrt(jnp.float32(EMBED_DIM)), axis=3)
        out = jnp.einsum('nhql,nlhd->nqhd', attn, v).reshape(n, q_len, HEADS * HEAD_DIM)
        return out @ W_out.T + b_out

    def _L1_ffn_ref(x, w_gate, w_up, w_down):
        import jax, jax.numpy as jnp
        import numpy as np
        BLOCK = 32
        W_BITS = 4
        ACT_BITS = 16

        def act_qdq(x):
            qmax = 2.0 ** (ACT_BITS - 1) - 1.0
            scale = jnp.maximum(jnp.max(jnp.abs(x)) / qmax, 1e-12)
            return jnp.clip(jnp.round(x / scale), -qmax - 1.0, qmax) * scale

        def fixed_qdq_u16(x):
            scale = 1.0 / 65536.0
            return jnp.clip(jnp.round(x / scale), 0.0, 65535.0) * scale

        def lpbq_dequant(w):
            O, I = w.shape
            qmax = 2.0 ** (W_BITS - 1) - 1.0
            wb = w.reshape(O, I // BLOCK, BLOCK)
            s = jnp.maximum(jnp.max(jnp.abs(wb), axis=-1, keepdims=True) / qmax, 1e-12)
            wq = jnp.clip(jnp.round(wb / s), -qmax - 1.0, qmax) * s
            return wq.reshape(O, I)
        x = act_qdq(x)
        up = act_qdq(x @ lpbq_dequant(w_up).T)
        gate = act_qdq(x @ lpbq_dequant(w_gate).T)
        sig = fixed_qdq_u16(jax.nn.sigmoid(gate))
        gate = act_qdq(gate * sig)
        o = act_qdq(gate * up)
        return o @ lpbq_dequant(w_down).T
    x = x + _L0_xattn_ref(_layernorm(x, axis=-1), ctx_1024, ctx_1024, L0_xattn_Wq, L0_xattn_bq, L0_xattn_Wk, L0_xattn_bk, L0_xattn_Wv, L0_xattn_bv, L0_xattn_Wo, L0_xattn_bo)
    x = x + _L0_ffn_ref(_layernorm(x, axis=-1), L0_ffn_W_r, L0_ffn_W_k, L0_ffn_W_v, L0_ffn_mu_r, L0_ffn_mu_k)
    x = x + _L1_xattn_ref(_layernorm(x, axis=-1), ctx_1024, ctx_1024, mask_Bx1xSxS2_ik1, L1_xattn_W_out, L1_xattn_b_out)
    x = x + _L1_ffn_ref(_layernorm(x, axis=-1), L1_ffn_w_gate, L1_ffn_w_up, L1_ffn_w_down)
    return x

_drawn_inputs = setup_inputs


def setup_inputs(seed=0):
    import zlib

    import numpy as np

    out = dict(_drawn_inputs(seed))
    spreads = {'L0_xattn_bq': (0.0, 0.422),
     'L0_xattn_bk': (0.0, 0.8),
     'L0_xattn_bv': (0.0, 0.1),
     'L0_xattn_bo': (0.0, 0.1)}
    factors = {'L0_ffn_W_r': 3.434, 'L0_ffn_mu_r': 8.0, 'L1_xattn_b_out': 6.814}
    for name, (base, spread) in spreads.items():
        noise = np.random.default_rng([zlib.crc32(name.encode()), seed]).standard_normal(out[name].shape)
        drawn = base * np.exp(spread * noise) if base else spread * noise
        out[name] = jnp.asarray(drawn.astype(out[name].dtype))
    for name, factor in factors.items():
        out[name] = (out[name] * factor).astype(out[name].dtype)
    return out
```

```python
from contextlib import ExitStack

import concourse.bass as bass
from concourse import mybir
from concourse.alu_op_type import AluOpType as ALU

F32 = mybir.dt.float32
F16 = mybir.dt.float16
I16 = mybir.dt.int16
U16 = mybir.dt.uint16
I32 = mybir.dt.int32
ACT = mybir.ActivationFunctionType
AX = mybir.AxisListType
RMAX = bass.bass_isa.ReduceOp.max

P = 128
B, L, D = 16, 256, 256
H, DH = 16, 16
TT = L // P
CT = D // P
LANES = 2
VW = 32
NEG = -60000.0
EPS = 1e-5
ROW_M = 3 * DH

MATS = ["q", "k", "v", "o", "r", "kk", "kv", "out"]

ORDER = [(l, part) for l in range(LANES) for part in ("prep0", "max0", "exp0", "ffn0", "prep1", "max1", "exp1", "end1")]

SPARE = {
    "prep0": ["xnT0", "q", "k", "v"],
    "max0": ["mT0"],
    "exp0": ["po0", "po1"],
    "ffn0": ["oN0", "oN1", "oT0", "ao0", "xnT1", "r", "kk", "kv"],
    "prep1": ["mbT", "xnT2"],
    "max1": ["mT1"],
    "exp1": ["po2", "po3"],
    "end1": ["oN2", "oN3", "oT1", "ao1", "xnT3"],
}
USES = [(l, u) for l, part in ORDER for u in SPARE[part]]
PER_BANK = len(USES) // 2
assert len(USES) % 2 == 0
HIS = ["c", "xn0", "q", "k", "o0", "xr", "xk", "ka", "xn2", "o1"]
LINKS = 2 * 18


def build(nc, x, ctxN, ctxT, mask, WT, COLS, ROWS, wg, wu, wd, out):
    scr = nc.dram_tensor("stack_scratch", [LANES, 6, D, L], F16)
    x3 = nc.dram_tensor("x3_scratch", [B, L, D], F32)
    with ExitStack() as whole:
        xnT_all = whole.enter_context(nc.sbuf_tensor("xnT_all", [P, CT, B * L], F32))
        amax = whole.enter_context(nc.sbuf_tensor("amax", [P, B], F32))
        ident = whole.enter_context(nc.sbuf_tensor("ident", [P, P], F32))
        with ExitStack() as ctx:
            layers(nc, ctx, scr, xnT_all, amax, ident, x, ctxN, ctxT, mask, WT, COLS, ROWS, x3)
        with ExitStack() as ctx:
            quantized_ffn(nc, ctx, xnT_all, amax, ident, x3, wg, wu, wd, out)


def layers(nc, ctx, scr, xnT_all, amax, ident, x, ctxN, ctxT, mask, WT, COLS, ROWS, x3):
    def sb(name, shape, dt=F32):
        return ctx.enter_context(nc.sbuf_tensor(name, shape, dt))

    def sb2(name, shape, dt=F32):
        return [sb(f"{name}{l}", shape, dt) for l in range(LANES)]

    def sem(name):
        return ctx.enter_context(nc.semaphore(name))

    def sem2(name):
        return [sem(f"{name}{l}") for l in range(LANES)]

    ident16 = sb("ident16", [P, P], F16)
    band = sb("band", [P, 2, P], F16)
    w_hi = sb("w_hi", [P, len(MATS), CT, D], F16)
    w_lo = sb("w_lo", [P, len(MATS), CT, D], F16)
    cols = sb("cols", [P, 4, CT])
    bias_q, bias_k, mu = cols[:, 0], cols[:, 1], cols[:, 2:4]
    omu = sb("omu", [P, 2, CT])
    rows = sb("rows", [P, 3, D])
    bvB, boB, boutB = rows[:, 0], rows[:, 1], rows[:, 2]
    zrow = sb("zrow", [P, H * L // P], F16)
    mhalf = sb("mhalf", [P, TT])
    xin, ctT, ctN, mk = sb2("xin", [P, TT, D]), sb2("ctT", [P, CT, L]), sb2("ctN", [P, TT, D]), sb2("mk", [P, TT, L], I32)
    xres, xb, xn = sb2("xres", [P, TT, D]), sb2("xb", [P, TT, D]), sb2("xn", [P, TT, D])
    st, mv, ve, rs = sb2("st", [P, TT, 6]), sb2("mv", [P, TT, 2]), sb2("ve", [P, TT]), sb2("rs", [P, TT])
    xh, xl = sb2("xh", [P, CT, L], F16), sb2("xl", [P, CT, L], F16)
    ch, cl = sb2("ch", [P, CT, L], F16), sb2("cl", [P, CT, L], F16)
    qh, ql = sb2("qh", [P, CT, L], F16), sb2("ql", [P, CT, L], F16)
    kh, kl = sb2("kh", [P, CT, L], F16), sb2("kl", [P, CT, L], F16)
    qst, kst0, kst1 = sb2("qst", [P, H, L], F16), sb2("kst0", [P, H, L], F16), sb2("kst1", [P, H, L], F16)
    val0, val1 = sb2("val0", [P, TT, H, VW]), sb2("val1", [P, TT, H, VW])
    anyk, anyn, mb, mbT = sb2("anyk", [P, TT]), sb2("anyn", [P, TT]), sb2("mb", [P, TT, L], F16), sb2("mbT", [P, TT, L], F16)
    mx, nm = sb2("mx", [P, TT, H]), sb2("nm", [H, L], F16)
    rc, on = sb2("rc", [P, TT, H]), sb2("on", [P, TT, D])
    xT, tm = sb2("xT", [P, CT, L + 1]), sb2("tm", [P, 2, CT, L])
    oT = [b[:, :, :, :].rearrange("p m t n -> p (m t) n") for b in tm]
    kr = sb2("kr", [P, CT, L])
    pT = sb("pT", [P, 4, 2, TT, L])
    stage = pT[:, :, :, :, :].rearrange("p u h t n -> p (u h t n)").rearrange("p (m t n) -> p m t n", m=len(MATS), t=CT)

    score_ps = [ctx.enter_context(nc.psum_tensor(f"score_ps{j}", [P, 2, TT, L], F32)) for j in range(2)]
    max_ps = [ctx.enter_context(nc.psum_tensor(f"max_ps{j}", [P, 2, L], F32)) for j in range(2)]
    spare_ps = [ctx.enter_context(nc.psum_tensor(f"spare_ps{j}", [P, 512], F32)) for j in range(2)]

    setup_loaded, id_set, id_done, band_set, consts_ready = sem("setup_loaded"), sem("id_set"), sem("id_done"), sem("band_set"), sem("consts_ready")
    w_hi_ready, w_lo_ready, cast_done, zero_set = sem("w_hi_ready"), sem("w_lo_ready"), sem("cast_done"), sem("zero_set")
    x_loaded, cT_loaded, cN_loaded, mk_loaded = sem2("x_loaded"), sem2("cT_loaded"), sem2("cN_loaded"), sem2("mk_loaded")
    used_act, used_dve, used_pool = sem2("used_act"), sem2("used_dve"), sem2("used_pool")
    var_ready, rstd_ready, xn_ready = sem2("var_ready"), sem2("rstd_ready"), sem2("xn_ready")
    hi_ready, cl_ready, val_ready, xb_ready, mb_ready = sem2("hi_ready"), sem2("cl_ready"), sem2("val_ready"), sem2("xb_ready"), sem2("mb_ready")
    lo_ready, mixed_ready, past_ready, kr_ready, x2_ready = sem2("lo_ready"), sem2("mixed_ready"), sem2("past_ready"), sem2("kr_ready"), sem2("x2_ready")
    scr_q, scr_k, scr_c = sem2("scr_q"), sem2("scr_k"), sem2("scr_c")
    q_stacked, k_stacked, c_stacked = sem2("q_stacked"), sem2("k_stacked"), sem2("c_stacked")
    max_full, max_free, score_full, exp_done, pv_done = sem("max_full"), sem("max_free"), sem("score_full"), sem("exp_done"), sem("pv_done")
    max_done = sem2("max_done")
    x3_ready, x3_stored = sem2("x3_ready"), sem2("x3_stored")
    spare_full, spare_free = [sem("spare_full0"), sem("spare_full1")], [sem("spare_free0"), sem("spare_free1")]
    dve_step, stats_ready = sem("dve_step"), sem("stats_ready")

    SETUP_DMAS = len(MATS) + 2

    def spare(l, use):
        n = USES.index((l, use))
        return spare_ps[n % 2], n % 2, n // 2

    def wait_full(eng, i, l, use):
        _, j, k = spare(l, use)
        eng.wait_ge(spare_full[j], i * PER_BANK + k + 1)

    def wait_evacuated(eng, i, l, use):
        _, j, k = spare(l, use)
        eng.wait_ge(spare_free[j], i * PER_BANK + k + 2)

    def wait_hi(eng, i, l, name):
        eng.wait_ge(hi_ready[l], i * len(HIS) + HIS.index(name) + 1)

    block = ctx.enter_context(nc.Block())

    @block.sync
    def _(sp):
        for m, name in enumerate(MATS):
            sp.dma_start(stage[:, m], WT[m].rearrange("(t p) d -> p t d", p=P)).then_inc(setup_loaded, 16)
        sp.dma_start(cols[:, :, :], COLS).then_inc(setup_loaded, 16)
        sp.dma_start(rows[:, :, :], ROWS.partition_broadcast(P)).then_inc(setup_loaded, 16)
        sp.wait_ge(zero_set, 2)

        def prep0(i, l):
            e = i * LANES + l
            sp.wait_ge(used_act[l], i + 1)
            sp.wait_ge(used_dve[l], i + 1)
            sp.wait_ge(used_pool[l], i + 1)
            sp.dma_start(xin[l][:, :, :], x[e].rearrange("(t p) d -> p t d", p=P)).then_inc(x_loaded[l], 16)
            sp.dma_start(ctT[l][:, :, :], ctxT[e].rearrange("(t p) n -> p t n", p=P)).then_inc(cT_loaded[l], 16)
            sp.dma_start(mk[l][:, :, :], mask[e].rearrange("(t p) n -> p t n", p=P)).then_inc(mk_loaded[l], 16)
            sp.dma_start(ctN[l][:, :, :], ctxN[e].rearrange("(t p) d -> p t d", p=P)).then_inc(cN_loaded[l], 16)
            wait_hi(sp, i, l, "c")
            to_scratch(l, 4, ch[l], scr_c[l])
            sp.wait_ge(cl_ready[l], i + 1)
            to_scratch(l, 5, cl[l], scr_c[l])
            wait_hi(sp, i, l, "q")
            to_scratch(l, 0, qh[l], scr_q[l])
            wait_evacuated(sp, i, l, "q")
            to_scratch(l, 1, ql[l], scr_q[l])
            sp.wait_ge(scr_q[l], i * 64 + 32)
            stack_q(l)
            wait_hi(sp, i, l, "k")
            to_scratch(l, 2, kh[l], scr_k[l])
            wait_evacuated(sp, i, l, "k")
            to_scratch(l, 3, kl[l], scr_k[l])
            sp.wait_ge(scr_k[l], i * 32 + 32)
            stack_k(l, 2, kst0[l], k_stacked[l])
            sp.wait_ge(scr_c[l], i * 32 + 32)
            stack_k(l, 4, kst1[l], c_stacked[l])

        def to_scratch(l, n, src, signal):
            sp.dma_start(scr[l, n].rearrange("(t p) n -> p t n", p=P), src[:, :, :]).then_inc(signal, 16)

        def stack_q(l):
            for row, n in ((0, 0), (DH, 0), (2 * DH, 1)):
                sp.dma_start(qst[l][row:row + DH, :, :], scr[l, n].rearrange("(h d) n -> d h n", d=DH)).then_inc(q_stacked[l], 16)
            sp.dma_start(qst[l][ROW_M:ROW_M + 1, :, :], zrow[:, :]).then_inc(q_stacked[l], 16)

        def stack_k(l, first, dst, signal):
            for row, n in ((0, first), (DH, first + 1), (2 * DH, first)):
                sp.dma_start(dst[row:row + DH, :, :], scr[l, n].rearrange("(h d) n -> d h n", d=DH)).then_inc(signal, 16)

        def max_row(i, l, use):
            wait_evacuated(sp, i, l, use)
            sp.dma_start(qst[l][ROW_M:ROW_M + 1, :, :], nm[l][:, :]).then_inc(q_stacked[l], 16)

        def prep1(i, l):
            wait_hi(sp, i, l, "xn2")
            to_scratch(l, 0, xh[l], scr_q[l])
            wait_evacuated(sp, i, l, "xnT2")
            to_scratch(l, 1, xl[l], scr_q[l])
            sp.wait_ge(scr_q[l], i * 64 + 64)
            stack_q(l)

        def end1(i, l):
            sp.wait_ge(x3_ready[l], i + 1)
            sp.dma_start(x3[i * LANES + l].rearrange("(t p) d -> p t d", p=P), xres[l][:, :, :]).then_inc(x3_stored[l], 16)

        with sp.Fori(0, B // LANES) as i:
            for l, part in ORDER:
                if part == "prep0":
                    prep0(i, l)
                if part == "max0":
                    max_row(i, l, "mT0")
                if part == "prep1":
                    prep1(i, l)
                if part == "max1":
                    max_row(i, l, "mT1")
                if part == "end1":
                    end1(i, l)
        for l in range(LANES):
            sp.wait_ge(x3_stored[l], 16 * (B // LANES))

    @block.gpsimd
    def _(pool):
        pool.memset(ident[:, :], 0.0).then_inc(id_set, 1)
        pool.memset(band[:, :, :], 0.0).then_inc(band_set, 1)
        pool.wait_ge(id_set, 1)
        pool.affine_select(out=ident[:, :], in_=ident[:, :], compare_op=ALU.not_equal, fill=1.0, base=0,
                           pattern=[[-1, P]], channel_multiplier=1).then_inc(id_done, 1)
        pool.wait_ge(band_set, 1)
        pool.affine_select(out=band[:, 0, :], in_=band[:, 0, :], compare_op=ALU.is_ge, fill=NEG, base=0,
                           pattern=[[-1, P]], channel_multiplier=1).then_inc(band_set, 1)
        pool.affine_select(out=band[:, 1, :], in_=band[:, 1, :], compare_op=ALU.is_ge, fill=NEG, base=0,
                           pattern=[[1, P]], channel_multiplier=-1).then_inc(band_set, 1)
        for l in range(LANES):
            pool.memset(val1[l][:, :, :, :], 0.0).then_inc(band_set, 1)
        pool.memset(mhalf[:, :], -0.5).then_inc(band_set, 1)
        pool.wait_ge(band_set, 4 + LANES)
        for l in range(LANES):
            pool.memset(val1[l][:, :, :, DH:DH + 1], 1.0).then_inc(band_set, 1)
            pool.sem_inc(used_pool[l], 1)
        pool.wait_ge(band_set, 4 + 2 * LANES)
        pool.wait_ge(setup_loaded, 16 * SETUP_DMAS)

        def rstd(i, l, n, per=4):
            pool.wait_ge(var_ready[l], i * per + n + 1)
            pool.tensor_tensor(rs[l][:, :], ve[l][:, :], mhalf[:, :], ALU.pow).then_inc(rstd_ready[l], 1)

        def prep0(i, l):
            rstd(i, l, 0)
            wait_hi(pool, i, l, "c")
            pool.tensor_tensor(cl[l][:, :, :], ctT[l][:, :, :], ch[l][:, :, :], ALU.subtract).then_inc(cl_ready[l], 1)
            pool.wait_ge(cN_loaded[l], i * 16 + 16)
            pool.tensor_tensor(xb[l][:, :, :], xin[l][:, :, :], boB[:, :].unsqueeze(1).to_broadcast([P, TT, D]),
                               ALU.add).then_inc(xb_ready[l], 1)
            for t in range(TT):
                ins = pool.tensor_copy(val1[l][:, t, :, 0:DH], ctN[l][:, t, :].rearrange("p (h d) -> p h d", d=DH))
                if t == TT - 1:
                    ins.then_inc(val_ready[l], 1)
            pool.wait_ge(val_ready[l], i + 1)
            pool.sem_inc(used_pool[l], 1)

        with pool.Fori(0, B // LANES) as i:
            for l, part in ORDER:
                if part == "prep0":
                    prep0(i, l)
                if part == "ffn0":
                    rstd(i, l, 1)
                if part == "prep1":
                    pool.wait_ge(x2_ready[l], i + 1)
                    pool.tensor_tensor(xb[l][:, :, :], xres[l][:, :, :], boutB[:, :].unsqueeze(1).to_broadcast([P, TT, D]),
                                       ALU.add).then_inc(xb_ready[l], 1)
                    rstd(i, l, 2)
                if part == "end1":
                    rstd(i, l, 3)

    @block.scalar
    def _(act):
        act.wait_ge(setup_loaded, 16 * SETUP_DMAS)
        act.activation(w_hi[:, :, :, :].rearrange("p m t n -> p (m t n)"), stage.rearrange("p m t n -> p (m t n)"),
                       ACT.Copy).then_inc(w_hi_ready, 1)
        for l in range(LANES):
            act.sem_inc(used_act[l], 1)

        def high(i, l, src, dst, name):
            ins = act.activation(dst, src, ACT.Copy)
            ins.then_inc(hi_ready[l], 1)

        def transposed_high(i, l, use, dst, name):
            wait_full(act, i, l, use)
            act.activation(dst[l][:, :, :].rearrange("p t n -> p (t n)"), spare(l, use)[0][:, :], ACT.Copy).then_inc(hi_ready[l], 1)

        def prep0(i, l):
            act.wait_ge(cT_loaded[l], i * 16 + 16)
            act.activation(ch[l][:, :, :], ctT[l][:, :, :], ACT.Copy).then_inc(hi_ready[l], 1)
            act.wait_ge(hi_ready[l], i * len(HIS) + 1)
            act.sem_inc(used_act[l], 1)
            transposed_high(i, l, "xnT0", xh, "xn0")
            for use, dst, bias in (("q", qh[l], bias_q), ("k", kh[l], bias_k)):
                wait_full(act, i, l, use)
                for t in range(CT):
                    ins = act.activation(dst[:, t, :], spare(l, use)[0][:, t * L:(t + 1) * L], ACT.Identity, bias=bias[:, t:t + 1])
                ins.then_inc(hi_ready[l], 1)

        def minus_max(i, l, use):
            _, j, _ = spare(l, use)
            wait_full(act, i, l, use)
            act.activation(nm[l][:, :], spare_ps[j][0:H, 0:L], ACT.Copy, scale=-1.0).then_inc(spare_free[j], 1)

        def exps(i, l, layer):
            scale = 1.0 / DH ** 0.5 if layer == 0 else 1.0 / D ** 0.5
            at = ORDER_EXP.index((l, layer)) * 8
            for u in range(8):
                act.wait_ge(score_full, i * 8 * len(ORDER_EXP) + at + u + 1)
                if u % 2 == 0:
                    act.wait_ge(pv_done, i * 4 * len(ORDER_EXP) + (at + u) // 2 + 1)
                act.activation(pT[:, u % 4], score_ps[u % 2][:, :, :, :], ACT.Exp, scale=scale).then_inc(exp_done, 1)

        def ffn0(i, l):
            transposed_high(i, l, "oT0", xh, "o0")
            ps, j, _ = spare(l, "xnT1")
            wait_full(act, i, l, "xnT1")
            act.activation(xT[l][:, :, 1:L + 1], ps[:, :].rearrange("p (t n) -> p t n", t=CT), ACT.Copy).then_inc(spare_free[j], 1)
            wait_evacuated(act, i, l, "xnT1")
            for m in range(2):
                for t in range(CT):
                    ins = act.activation(tm[l][:, m, t, :], xT[l][:, t, 0:L], ACT.Identity, scale=omu[:, m, t:t + 1])
                ins.then_inc(past_ready[l], 1)
            for m, dst in ((0, qh[l]), (1, kh[l])):
                act.wait_ge(mixed_ready[l], i * 2 + m + 1)
                act.activation(dst[:, :, :], tm[l][:, m], ACT.Copy).then_inc(hi_ready[l], 1)
            ps, j, _ = spare(l, "r")
            wait_full(act, i, l, "r")
            act.activation(on[l][:, :, :].rearrange("p t n -> p (t n)"), ps[:, :], ACT.Tanh, scale=0.5).then_inc(spare_free[j], 1)
            ps, j, _ = spare(l, "kk")
            wait_full(act, i, l, "kk")
            act.activation(kr[l][:, :, :].rearrange("p t n -> p (t n)"), ps[:, :], ACT.Relu).then_inc(kr_ready[l], 1)
            wait_evacuated(act, i, l, "kk")
            act.activation(xh[l][:, :, :], kr[l][:, :, :], ACT.Copy).then_inc(hi_ready[l], 1)

        def prep1(i, l):
            ps, j, _ = spare(l, "mbT")
            wait_full(act, i, l, "mbT")
            act.activation(mbT[l][:, :, :].rearrange("p t n -> p (t n)"), ps[:, :].bitcast(F16)[:, 0:TT * L], ACT.Copy).then_inc(spare_free[j], 1)
            transposed_high(i, l, "xnT2", xh, "xn2")

        def end1(i, l):
            transposed_high(i, l, "oT1", xh, "o1")
            ps, j, _ = spare(l, "xnT3")
            wait_full(act, i, l, "xnT3")
            act.activation(xnT_all[:, :, bass.ds((i * LANES + l) * L, L)], ps[:, :].rearrange("p (t n) -> p t n", t=CT),
                           ACT.Copy).then_inc(spare_free[j], 1)

        with act.Fori(0, B // LANES) as i:
            for l, part in ORDER:
                if part == "prep0":
                    prep0(i, l)
                if part == "max0":
                    minus_max(i, l, "mT0")
                if part == "exp0":
                    exps(i, l, 0)
                if part == "ffn0":
                    ffn0(i, l)
                if part == "prep1":
                    prep1(i, l)
                if part == "max1":
                    minus_max(i, l, "mT1")
                if part == "exp1":
                    exps(i, l, 1)
                if part == "end1":
                    end1(i, l)

    @block.tensor
    def _(pe):
        pe.wait_ge(id_done, 1)
        pe.wait_ge(consts_ready, 1)
        pe.wait_ge(w_lo_ready, 1)
        pe.wait_ge(band_set, 4 + 2 * LANES)

        def claim(i, l, use):
            ps, j, k = spare(l, use)
            pe.wait_ge(spare_free[j], i * PER_BANK + k + 1)
            return ps, spare_full[j]

        def transposes(i, l, src, use):
            ps, full = claim(i, l, use)
            for t in range(TT):
                for c in range(CT):
                    ins = pe.transpose(ps[:, c * L + t * P:c * L + (t + 1) * P], src[:, t, c * P:(c + 1) * P], ident[:, :])
            ins.then_inc(full, 1)

        def product(i, l, m, hi, lo, use, weights_first):
            ps, full = claim(i, l, use)
            for t in range(2):
                n = 0
                for c in range(CT):
                    for a, w in ((hi, w_hi), (hi, w_lo), (lo, w_hi)):
                        if weights_first:
                            lhsT, rhs = w[:, m, c, t * P:(t + 1) * P], a[:, c, :]
                        else:
                            lhsT, rhs = a[:, c, t * P:(t + 1) * P], w[:, m, c, :]
                        ins = pe.matmul(ps[:, t * L:(t + 1) * L], lhsT, rhs, start=(n == 0), stop=(n == 3 * CT - 1))
                        n += 1
            ins.then_inc(full, 1)

        def prep0(i, l):
            pe.wait_ge(xn_ready[l], i * 4 + 1)
            transposes(i, l, xn[l], "xnT0")
            wait_hi(pe, i, l, "xn0")
            wait_evacuated(pe, i, l, "xnT0")
            product(i, l, MATS.index("q"), xh[l], xl[l], "q", True)
            wait_hi(pe, i, l, "c")
            pe.wait_ge(cl_ready[l], i + 1)
            product(i, l, MATS.index("k"), ch[l], cl[l], "k", True)
            product(i, l, MATS.index("v"), ch[l], cl[l], "v", False)

        def maxima(i, l, layer):
            kst = (kst0 if layer == 0 else kst1)[l]
            pe.wait_ge(q_stacked[l], i * 160 + 80 * layer + 64)
            pe.wait_ge((k_stacked if layer == 0 else c_stacked)[l], i * 48 + 48)
            if layer == 1:
                pe.wait_ge(mb_ready[l], i + 1)
            at = ORDER_EXP.index((l, layer)) * 16
            for n in range(16):
                t, h = n // 8, n % 8 * 2
                ps = max_ps[n % 2]
                pe.wait_ge(max_free, i * 16 * len(ORDER_EXP) + at + n + 1)
                if layer == 0:
                    off = (1 - t) * P
                    pe.matmul(ps[:, :, off:off + P], ident16[:, :], band[:, t, :].unsqueeze(1).to_broadcast([P, 2, P]),
                              start=True, stop=False, skip_group_check=True)
                else:
                    pe.matmul(ps[:, :, :], ident16[:, :], mb[l][:, t, :].unsqueeze(1).to_broadcast([P, 2, L]),
                              start=True, stop=False, skip_group_check=True)
                for a in range(2):
                    ins = pe.matmul(ps[:, a, :], qst[l][:, h + a, t * P:(t + 1) * P], kst[:, h + a, :],
                                    start=False, stop=(a == 1), skip_group_check=True)
                ins.then_inc(max_full, 1)
            use = f"mT{layer}"
            ps, full = claim(i, l, use)
            pe.wait_ge(max_done[l], i * 2 + layer + 1)
            for t in range(TT):
                ins = pe.transpose(ps[0:H, t * P:(t + 1) * P], mx[l][:, t, :], ident[:, :])
            ins.then_inc(full, 1)

        def attend(i, l, layer):
            kst, val = (kst0 if layer == 0 else kst1)[l], (val0 if layer == 0 else val1)[l]
            pe.wait_ge(q_stacked[l], i * 160 + 80 * layer + 80)
            if layer == 0:
                wait_evacuated(pe, i, l, "v")
            else:
                pe.wait_ge(val_ready[l], i + 1)
                wait_evacuated(pe, i, l, "mbT")
            at = ORDER_EXP.index((l, layer)) * 8
            for u in range(8):
                ps = score_ps[u % 2]
                pe.wait_ge(exp_done, i * 8 * len(ORDER_EXP) + at + u + 1)
                for a in range(2):
                    if layer == 0:
                        pe.matmul(ps[:, a].rearrange("p t n -> p (t n)")[:, P:3 * P], ident16[:, :],
                                  band[:, :, :].rearrange("p a n -> p (a n)"), start=True, stop=False, skip_group_check=True)
                    else:
                        pe.matmul(ps[:, a].rearrange("p t n -> p (t n)"), ident16[:, :],
                                  mbT[l][:, :, :].rearrange("p t n -> p (t n)"), start=True, stop=False, skip_group_check=True)
                    for t in range(TT):
                        ins = pe.matmul(ps[:, a, t, :], kst[:, 2 * u + a, t * P:(t + 1) * P], qst[l][:, 2 * u + a, :],
                                        start=False, stop=(t == TT - 1), skip_group_check=True)
                ins.then_inc(score_full, 1)
                if u >= 3 and u % 2 == 1:
                    weigh(i, l, layer, (u - 3) // 2, val)
            weigh(i, l, layer, 3, val)

        def weigh(i, l, layer, g, val):
            use = f"po{2 * layer + g // 2}"
            ps, full = claim(i, l, use) if g % 2 == 0 else (spare(l, use)[0], spare_full[spare(l, use)[1]])
            at = ORDER_EXP.index((l, layer)) * 8
            pe.wait_ge(exp_done, i * 8 * len(ORDER_EXP) + at + 2 * g + 2 + 2)
            for t in range(TT):
                for r in range(4):
                    ins = pe.matmul(ps[VW * r:VW * (r + 1), g % 2 * L:(g % 2 + 1) * L], val[:, t, 4 * g + r, :],
                                    pT[:, (2 * g + r // 2) % 4, r % 2, t, :], start=(t == 0), stop=(t == TT - 1),
                                    skip_group_check=True, tile_position=(0, VW * r))
            ins.then_inc(pv_done, 1)
            if g % 2 == 1:
                pe.drain().then_inc(full, 1)

        def project(i, l, layer, m):
            wait_evacuated(pe, i, l, f"po{2 * layer}")
            wait_evacuated(pe, i, l, f"po{2 * layer + 1}")
            for t in range(TT):
                ps, full = claim(i, l, f"oN{2 * layer + t}")
                for g in range(4):
                    ins = pe.transpose(ps[:, g * P:(g + 1) * P], oT[l][:, g, t * P:(t + 1) * P], ident[:, :])
                ins.then_inc(full, 1)
            wait_evacuated(pe, i, l, f"oN{2 * layer}")
            wait_evacuated(pe, i, l, f"oN{2 * layer + 1}")
            transposes(i, l, on[l], f"oT{layer}")
            wait_hi(pe, i, l, f"o{layer}")
            wait_evacuated(pe, i, l, f"oT{layer}")
            product(i, l, m, xh[l], xl[l], f"ao{layer}", False)

        def ffn0(i, l):
            project(i, l, 0, MATS.index("o"))
            pe.wait_ge(xn_ready[l], i * 4 + 2)
            transposes(i, l, xn[l], "xnT1")
            wait_hi(pe, i, l, "xr")
            pe.wait_ge(lo_ready[l], i * 3 + 1)
            product(i, l, MATS.index("r"), qh[l], ql[l], "r", False)
            wait_hi(pe, i, l, "xk")
            pe.wait_ge(lo_ready[l], i * 3 + 2)
            product(i, l, MATS.index("kk"), kh[l], kl[l], "kk", True)
            wait_hi(pe, i, l, "ka")
            pe.wait_ge(lo_ready[l], i * 3 + 3)
            product(i, l, MATS.index("kv"), xh[l], xl[l], "kv", False)

        def prep1(i, l):
            pe.wait_ge(mb_ready[l], i + 1)
            ps, full = claim(i, l, "mbT")
            for k in range(TT):
                for t in range(TT):
                    ins = pe.transpose(ps[:, :].bitcast(F16)[:, k * L + t * P:k * L + (t + 1) * P], mb[l][:, t, k * P:(k + 1) * P], ident16[:, :])
            ins.then_inc(full, 1)
            pe.wait_ge(xn_ready[l], i * 4 + 3)
            transposes(i, l, xn[l], "xnT2")

        def end1(i, l):
            project(i, l, 1, MATS.index("out"))
            pe.wait_ge(xn_ready[l], i * 4 + 4)
            transposes(i, l, xn[l], "xnT3")

        with pe.Fori(0, B // LANES) as i:
            for l, part in ORDER:
                if part == "prep0":
                    prep0(i, l)
                if part == "max0":
                    maxima(i, l, 0)
                if part == "exp0":
                    attend(i, l, 0)
                if part == "ffn0":
                    ffn0(i, l)
                if part == "prep1":
                    prep1(i, l)
                if part == "max1":
                    maxima(i, l, 1)
                if part == "exp1":
                    attend(i, l, 1)
                if part == "end1":
                    end1(i, l)

    @block.vector
    def _(dve):
        dve.memset(zrow[:, :], 0.0).then_inc(zero_set, 1)
        for l in range(LANES):
            dve.memset(qst[l][:, :, :], 0.0)
            for kst in (kst0[l], kst1[l]):
                dve.memset(kst[:, :, :], 0.0)
            dve.memset(xT[l][:, :, 0:1], 0.0)
            dve.memset(val0[l][:, :, :, :], 0.0)
        dve.memset(amax[:, :], 0.0).then_inc(zero_set, 1)
        dve.wait_ge(zero_set, 2)
        for l in range(LANES):
            for kst in (kst0[l], kst1[l]):
                dve.memset(kst[32:64, :, :], 1.0)
            dve.memset(val0[l][:, :, :, DH:DH + 1], 1.0)
        dve.wait_ge(id_done, 1)
        dve.tensor_copy(ident16[:, :], ident[:, :]).then_inc(consts_ready, 1)
        dve.wait_ge(consts_ready, 1)
        for j in range(2):
            dve.sem_inc(spare_free[j], 1)
        dve.sem_inc(max_free, 2)
        dve.sem_inc(exp_done, 2)
        dve.sem_inc(pv_done, 1)
        for l in range(LANES):
            dve.sem_inc(used_dve[l], 1)
        dve.wait_ge(setup_loaded, 16 * SETUP_DMAS)
        dve.tensor_scalar(omu[:, :, :], mu[:, :, :], -1.0, 1.0, ALU.mult, ALU.add)
        dve.wait_ge(w_hi_ready, 1)
        dve.tensor_tensor(w_lo[:, :, :, :].rearrange("p m t n -> p (m t n)"), stage.rearrange("p m t n -> p (m t n)"),
                          w_hi[:, :, :, :].rearrange("p m t n -> p (m t n)"), ALU.subtract).then_inc(w_lo_ready, 1)
        dve.wait_ge(w_lo_ready, 1)

        with dve.Fori(0, B // LANES) as i:
            steps = [0]

            def link(ins):
                steps[0] += 1
                ins.then_inc(dve_step, 1)
                dve.wait_ge(dve_step, i * LINKS + steps[0])

            def norm(l, n, src):
                for t in range(TT):
                    ins = dve.bn_stats(st[l][:, t, :], src[:, t, :])
                link(ins)
                dve.sem_inc(stats_ready, 1)
                for t in range(TT):
                    ins = dve.bn_aggr(mv[l][:, t, :], st[l][:, t, :])
                link(ins)
                dve.tensor_scalar(ve[l][:, :], mv[l][:, :, 1], EPS, None, ALU.add).then_inc(var_ready[l], 1)
                dve.wait_ge(rstd_ready[l], i * 4 + n + 1)
                if n == 2:
                    link(dve.tensor_tensor(rs[l][:, :], rs[l][:, :], anyk[l][:, :], ALU.mult))
                for t in range(TT):
                    ins = dve.tensor_scalar(xn[l][:, t, :], src[:, t, :], mv[l][:, t, 0:1], rs[l][:, t:t + 1], ALU.subtract, ALU.mult)
                ins.then_inc(xn_ready[l], 1)

            def low(l, use, hi, lo, name):
                ps, j, _ = spare(l, use)
                wait_full(dve, i, l, use)
                wait_hi(dve, i, l, name)
                dve.tensor_tensor(lo[l][:, :, :].rearrange("p t n -> p (t n)"), ps[:, :],
                                  hi[l][:, :, :].rearrange("p t n -> p (t n)"), ALU.subtract).then_inc(spare_free[j], 1)

            def prep0(l):
                dve.wait_ge(x_loaded[l], i * 16 + 16)
                norm(l, 0, xin[l])
                dve.wait_ge(mk_loaded[l], i * 16 + 16)
                link(dve.tensor_scalar(kr[l][:, :, :], mk[l][:, :, :], 0.0, None, ALU.not_equal))
                link(dve.tensor_reduce(anyk[l][:, :], kr[l][:, :, :], AX.X, ALU.max))
                link(dve.tensor_scalar(anyn[l][:, :], anyk[l][:, :], NEG, None, ALU.mult))
                for t in range(TT):
                    ins = dve.tensor_scalar(mb[l][:, t, :], mk[l][:, t, :], 0.0, anyn[l][:, t:t + 1], ALU.is_equal, ALU.mult)
                ins.then_inc(mb_ready[l], 1)
                dve.wait_ge(mb_ready[l], i + 1)
                dve.wait_ge(xn_ready[l], i * 4 + 1)
                dve.sem_inc(used_dve[l], 1)
                low(l, "xnT0", xh, xl, "xn0")
                for use, hi, lo, bias in (("q", qh[l], ql[l], bias_q), ("k", kh[l], kl[l], bias_k)):
                    ps, j, _ = spare(l, use)
                    wait_full(dve, i, l, use)
                    wait_hi(dve, i, l, use)
                    for t in range(CT):
                        ins = dve.scalar_tensor_tensor(out=lo[:, t, :], in0=ps[:, t * L:(t + 1) * L], scalar=bias[:, t:t + 1],
                                                       in1=hi[:, t, :], op0=ALU.add, op1=ALU.subtract)
                    ins.then_inc(spare_free[j], 1)
                ps, j, _ = spare(l, "v")
                wait_full(dve, i, l, "v")
                for t in range(TT):
                    ins = dve.tensor_tensor(val0[l][:, t, :, 0:DH], ps[:, t * D:(t + 1) * D].rearrange("p (h d) -> p h d", d=DH),
                                            bvB[:, :].rearrange("p (h d) -> p h d", d=DH), ALU.add)
                ins.then_inc(spare_free[j], 1)

            def maxima(l, layer):
                at = ORDER_EXP.index((l, layer)) * 16
                for n in range(16):
                    t, h = n // 8, n % 8 * 2
                    dve.wait_ge(max_full, i * 16 * len(ORDER_EXP) + at + n + 1)
                    dve.tensor_reduce(mx[l][:, t, h:h + 2], max_ps[n % 2][:, :, :], AX.X, ALU.max).then_inc(max_free, 1)
                dve.wait_ge(max_free, i * 16 * len(ORDER_EXP) + at + 16 + 2)
                dve.sem_inc(max_done[l], 1)

            def gather(l, layer):
                for a in range(2):
                    use = f"po{2 * layer + a}"
                    ps, j, _ = spare(l, use)
                    wait_full(dve, i, l, use)
                    dve.tensor_copy(oT[l][:, 2 * a:2 * a + 2, :].rearrange("p g n -> p (g n)"), ps[:, :]).then_inc(spare_free[j], 1)

            def divide(l, layer):
                for t in range(TT):
                    use = f"oN{2 * layer + t}"
                    ps, j, _ = spare(l, use)
                    wait_full(dve, i, l, use)
                    heads = ps[:, :].rearrange("p (h w) -> p h w", w=VW)
                    link(dve.reciprocal(rc[l][:, t, :], heads[:, :, DH]))
                    dve.tensor_tensor(on[l][:, t, :].rearrange("p (h d) -> p h d", d=DH), heads[:, :, 0:DH],
                                      rc[l][:, t, :].unsqueeze(2).to_broadcast([P, H, DH]), ALU.mult).then_inc(spare_free[j], 1)
                low(l, f"oT{layer}", xh, xl, f"o{layer}")
                use = f"ao{layer}"
                ps, j, _ = spare(l, use)
                wait_full(dve, i, l, use)
                dve.wait_ge(xb_ready[l], i * 2 + layer + 1)
                dve.tensor_tensor(xres[l][:, :, :].rearrange("p t n -> p (t n)"), ps[:, :],
                                  xb[l][:, :, :].rearrange("p t n -> p (t n)"), ALU.add).then_inc(spare_free[j], 1)
                wait_evacuated(dve, i, l, use)

            def ffn0(l):
                divide(l, 0)
                norm(l, 1, xres[l])
                for m in range(2):
                    dve.wait_ge(past_ready[l], i * 2 + m + 1)
                    for t in range(CT):
                        ins = dve.scalar_tensor_tensor(out=tm[l][:, m, t, :], in0=xT[l][:, t, 1:L + 1], scalar=mu[:, m, t:t + 1],
                                                       in1=tm[l][:, m, t, :], op0=ALU.mult, op1=ALU.add)
                    ins.then_inc(mixed_ready[l], 1)
                for m, (hi, lo) in enumerate(((qh, ql), (kh, kl))):
                    wait_hi(dve, i, l, ("xr", "xk")[m])
                    dve.wait_ge(mixed_ready[l], i * 2 + m + 1)
                    dve.tensor_tensor(lo[l][:, :, :], tm[l][:, m], hi[l][:, :, :], ALU.subtract).then_inc(lo_ready[l], 1)
                ps, j, _ = spare(l, "kk")
                dve.wait_ge(kr_ready[l], i + 1)
                dve.scalar_tensor_tensor(out=kr[l][:, :, :].rearrange("p t n -> p (t n)"), in0=ps[:, :], scalar=0.0,
                                         in1=kr[l][:, :, :].rearrange("p t n -> p (t n)"), op0=ALU.max, op1=ALU.mult).then_inc(spare_free[j], 1)
                wait_evacuated(dve, i, l, "r")
                link(dve.tensor_scalar(on[l][:, :, :], on[l][:, :, :], 0.5, 0.5, ALU.mult, ALU.add))
                wait_hi(dve, i, l, "ka")
                wait_evacuated(dve, i, l, "kk")
                dve.tensor_tensor(xl[l][:, :, :], kr[l][:, :, :], xh[l][:, :, :], ALU.subtract).then_inc(lo_ready[l], 1)
                ps, j, _ = spare(l, "kv")
                wait_full(dve, i, l, "kv")
                dve.tensor_tensor(on[l][:, :, :].rearrange("p t n -> p (t n)"), ps[:, :],
                                  on[l][:, :, :].rearrange("p t n -> p (t n)"), ALU.mult).then_inc(spare_free[j], 1)
                wait_evacuated(dve, i, l, "kv")
                dve.tensor_tensor(xres[l][:, :, :], xres[l][:, :, :], on[l][:, :, :], ALU.add).then_inc(x2_ready[l], 1)
                dve.wait_ge(x2_ready[l], i + 1)

            def end1(l):
                divide(l, 1)
                dve.sem_inc(x3_ready[l], 1)
                norm(l, 3, xres[l])
                dve.wait_ge(xn_ready[l], i * 4 + 4)
                link(dve.tensor_reduce(amax[:, bass.ds(i * LANES + l, 1)], xn[l][:, :, :], AX.XY, ALU.max, apply_absolute_value=True))

            for l, part in ORDER:
                if part == "prep0":
                    prep0(l)
                if part == "max0":
                    maxima(l, 0)
                if part == "exp0":
                    gather(l, 0)
                if part == "ffn0":
                    ffn0(l)
                if part == "prep1":
                    norm(l, 2, xres[l])
                    low(l, "xnT2", xh, xl, "xn2")
                if part == "max1":
                    maxima(l, 1)
                if part == "exp1":
                    gather(l, 1)
                if part == "end1":
                    end1(l)
            assert steps[0] == LINKS, steps[0]


ORDER_EXP = [(l, int(part[-1])) for l, part in ORDER if part.startswith("exp")]


I = 768
OT = I // P
PAIRS = OT // 2
BLK = 32
N = B * L
CH = 512
NCH = N // CH
QA, QW = 32767.0, 7.0


def quantized_ffn(nc, ctx, xnT_all, amax, ident, x3, wg, wu, wd, out):
    def sb(name, shape, dt=F32):
        return ctx.enter_context(nc.sbuf_tensor(name, shape, dt))

    def sem(name):
        return ctx.enter_context(nc.semaphore(name))

    hid = sb("hid", [P, OT, N])
    x_hi, x_lo = sb("x_hi", [P, CT, N], F16), sb("x_lo", [P, CT, N], F16)
    wT_hi = [sb(f"wT_hi{m}", [P, CT * I], F16) for m in range(3)]
    wT_lo = [sb(f"wT_lo{m}", [P, CT * I], F16) for m in range(3)]
    steps16 = sb("steps16", [P, 2, OT, CH], I16)
    blk_s, blk_r = sb("blk_s", [P, 3, I * CT // BLK]), sb("blk_r", [P, 3, I * CT // BLK])
    sc = sb("sc", [P, 32])
    g_max, p_max, u_max, q_max = sb("g_max", [P, NCH]), sb("p_max", [P, NCH]), sb("u_max", [P, NCH, PAIRS]), sb("q_max", [P, NCH])

    w_nat = [hid[:, m, 0:CT * I] for m in range(3)]
    w_step = [hid[:, 3, m * CT * I // 2:(m + 1) * CT * I // 2].bitcast(I16) for m in range(2)] + [hid[:, 4, 0:CT * I // 2].bitcast(I16)]
    work = xnT_all[:, :, :].rearrange("p t n -> p (t n)")
    sig = work[:, 0:OT * CH].rearrange("p (o n) -> p o n", o=OT)
    half = [work[:, OT * CH + j * OT * CH // 2:OT * CH + (j + 1) * OT * CH // 2] for j in range(2)]
    sig16 = [h.bitcast(U16).rearrange("p (o n) -> p o n", o=OT) for h in half]
    up16 = [h.bitcast(I16).rearrange("p (o n) -> p o n", o=OT) for h in half]
    rest = work[:, 2 * OT * CH:2 * OT * CH + 4 * 2 * D].rearrange("p (j t d) -> p j t d", j=4, d=D)
    x3_in, y_out = [rest[:, j] for j in range(2)], [rest[:, 2 + j] for j in range(2)]
    tokens = x_hi[:, :, :].rearrange("p t n -> p (t n)"), x_lo[:, :, :].rearrange("p t n -> p (t n)")
    o_hi, o_lo = [[half[:, j * OT * CH:(j + 1) * OT * CH].rearrange("p (o n) -> p o n", o=OT) for j in range(2)] for half in tokens]
    xq = [steps16[:, 0, 2 * j:2 * j + 2, :] for j in range(2)]
    x32 = [steps16[:, 1, 2 * j:2 * j + 2, :] for j in range(2)]

    s_x, c_x, s_gate, c_gate, s_gated, c_gated, s_up, c_up, s_o, c_o = [sc[:, 12 + k:13 + k] for k in range(10)]
    u_sig, u_o, tmp = [sc[:, 22 + k:23 + k] for k in range(3)]

    unit_ps = [ctx.enter_context(nc.psum_tensor(f"unit_ps{j}", [P, 2, CH], F32)) for j in range(PAIRS)]
    down_ps = [ctx.enter_context(nc.psum_tensor(f"down_ps{j}", [P, 2, D], F32)) for j in range(2)]

    w_loaded, w_quantized, wT_full, wT_hi_done, wT_free = sem("w_loaded"), sem("w_quantized"), sem("wT_full"), sem("wT_hi_done"), sem("wT_free")
    amax_ready, max_in, max_out, scale_step = sem("amax_ready"), sem("max_in"), sem("max_out"), sem("scale_step")
    x32_ready, x_hi_ready, x_lo_ready = sem("x32_ready"), sem("x_hi_ready"), sem("x_lo_ready")
    unit_full, unit_free, gate_kept, gate_max_done = sem("unit_full"), sem("unit_free"), sem("gate_kept"), sem("gate_max_done")
    gate_scale, gate16_ready, sig_ready, sig16_ready, prod_ready = sem("gate_scale"), sem("gate16_ready"), sem("sig_ready"), sem("sig16_ready"), sem("prod_ready")
    up_scale, up16_ready, gated16_ready, both_ready = sem("up_scale"), sem("up16_ready"), sem("gated16_ready"), sem("both_ready")
    o16_ready, o32_ready, o_hi_ready, o_lo_ready = sem("o16_ready"), sem("o32_ready"), sem("o_hi_ready"), sem("o_lo_ready")
    down_full, down_free, down_done = sem("down_full"), sem("down_free"), sem("down_done")
    x3_loaded, y_stored = [sem("x3_loaded0"), sem("x3_loaded1")], [sem("y_stored0"), sem("y_stored1")]

    x3_v = x3.rearrange("b l d -> (b l) d").rearrange("(g t p) d -> g p t d", t=2, p=P)
    out_v = out.rearrange("b l d -> (b l) d").rearrange("(g t p) d -> g p t d", t=2, p=P)

    block = ctx.enter_context(nc.Block())

    @block.sync
    def _(sp):
        for m, w in enumerate((wg, wu)):
            sp.dma_start(w_nat[m].rearrange("p (t c) -> p t c", c=D), w.rearrange("(t p) c -> p t c", p=P)).then_inc(w_loaded, 16)
        sp.dma_start(w_nat[2].rearrange("p (t c) -> p t c", c=I), wd.rearrange("(t p) c -> p t c", p=P)).then_inc(w_loaded, 16)
        with sp.Fori(0, NCH) as n:
            for g in range(2):
                sp.wait_ge(down_free, n * 2 + g + 3)
                sp.dma_start(out_v[n * 2 + g], y_out[g]).then_inc(y_stored[g], 16)
        for g in range(2):
            sp.wait_ge(y_stored[g], 16 * NCH + 16)

    @block.gpsimd
    def _(pool):
        for k in range(5):
            pool.wait_ge(max_in, k + 1)
            pool.partition_all_reduce(sc[:, 2 * k + 1:2 * k + 2], sc[:, 2 * k:2 * k + 1], P, RMAX).then_inc(max_out, 1)
        with pool.Fori(0, NCH) as n:
            for g in range(2):
                pool.wait_ge(down_free, n * 2 + g + 1)
                pool.dma_start(x3_in[g], x3_v[n * 2 + g]).then_inc(x3_loaded[g], 16)

    def weight_block(m, k):
        if m < 2:
            o, c = k // CT, k % CT
            return w_nat[m][:, o * D + c * P:o * D + (c + 1) * P], c * I + o * P
        h, t = k % CT, k // CT
        return w_nat[m][:, h * I + t * P:h * I + (t + 1) * P], t * D + h * P

    def weight_dst(w, m, k):
        _, at = weight_block(m, k)
        return w[m][:, at:at + P]

    @block.scalar
    def _(act):
        for n in range(9):
            m, ps = n // 3, unit_ps[n % 3]
            act.wait_ge(wT_full, n + 1)
            for j in range(4):
                ins = act.activation(weight_dst(wT_hi, m, n % 3 * 4 + j), ps[:, 0, j * P:(j + 1) * P], ACT.Copy)
            ins.then_inc(wT_hi_done, 1)
        with act.Fori(0, NCH // 2) as n2:
            for a in range(2):
                n = n2 * 2 + a
                act.wait_ge(x32_ready, n + 1)
                act.activation(x_hi[:, :, bass.ds(n * CH, CH)], x32[a], ACT.Copy, scale=32.0).then_inc(x_hi_ready, 1)
                for j in range(PAIRS):
                    act.wait_ge(unit_full, n * PAIRS + j + 1)
                    act.activation(hid[:, 2 * j:2 * j + 2, bass.ds(n * CH, CH)], unit_ps[j][:, :, :], ACT.Copy).then_inc(gate_kept, 1)
        act.wait_ge(gate_scale, 1)
        with act.Fori(0, NCH // 2) as n2:
            for a in range(2):
                n = n2 * 2 + a
                act.wait_ge(prod_ready, n + 1)
                act.activation(steps16[:, a], hid[:, :, bass.ds(n * CH, CH)], ACT.Identity, scale=c_gate).then_inc(gate16_ready, 1)
                act.wait_ge(gate16_ready, n + 1)
                act.wait_ge(sig16_ready, n + 1)
                act.activation(sig, steps16[:, a], ACT.Sigmoid, scale=s_gate).then_inc(sig_ready, 1)
        act.wait_ge(up_scale, 1)
        with act.Fori(0, NCH // 2) as n2:
            for a in range(2):
                n = n2 * 2 + a
                act.wait_ge(both_ready, n + 1)
                for j in range(PAIRS):
                    act.wait_ge(unit_full, n * PAIRS + j + 1 + 2 * NCH * PAIRS)
                    act.activation(up16[a][:, 2 * j:2 * j + 2, :], unit_ps[j][:, :, :], ACT.Identity, scale=c_up).then_inc(up16_ready, 1)
        with act.Fori(0, NCH // 2) as n2:
            for a in range(2):
                n = n2 * 2 + a
                act.wait_ge(o32_ready, n + 1)
                act.wait_ge(down_done, n + 1)
                act.activation(o_hi[a], up16[a], ACT.Copy, scale=32.0).then_inc(o_hi_ready, 1)

    @block.tensor
    def _(pe):
        for n in range(9):
            m, ps = n // 3, unit_ps[n % 3]
            pe.wait_ge(w_quantized, m + 1)
            if n >= 3:
                pe.wait_ge(wT_free, n - 2)
            for j in range(4):
                src, _ = weight_block(m, n % 3 * 4 + j)
                ins = pe.transpose(ps[:, 0, j * P:(j + 1) * P], src, ident[:, :])
            ins.then_inc(wT_full, 1)
        pe.wait_ge(wT_free, 9)

        def units(n, m, first):
            for j in range(PAIRS):
                done_before = first + j
                pe.wait_ge(unit_free, n * PAIRS + done_before + 1)
                for a in range(2):
                    o, k = 2 * j + a, 0
                    for c in range(CT):
                        for w, xx in ((wT_hi, x_hi), (wT_lo, x_hi), (wT_hi, x_lo)):
                            ins = pe.matmul(unit_ps[j][:, a, :], w[m][:, c * I + o * P:c * I + (o + 1) * P],
                                            xx[:, c, bass.ds(n * CH, CH)], start=(k == 0), stop=(k == 3 * CT - 1))
                            k += 1
                ins.then_inc(unit_full, 1)

        for p, m in enumerate((0, 1, 1)):
            with pe.Fori(0, NCH) as n:
                if p == 0:
                    pe.wait_ge(x_hi_ready, n + 1)
                    pe.wait_ge(x_lo_ready, n + 1)
                units(n, m, p * NCH * PAIRS)
        with pe.Fori(0, NCH // 2) as n2:
            for a in range(2):
                n = n2 * 2 + a
                pe.wait_ge(o_hi_ready, n + 1)
                pe.wait_ge(o_lo_ready, n + 1)
                for g in range(2):
                    pe.wait_ge(down_free, n * 2 + g + 1)
                    for t in range(2):
                        k = 0
                        tok = slice((2 * g + t) * P, (2 * g + t + 1) * P)
                        for o in range(OT):
                            for w, hh in ((wT_hi, o_hi), (wT_lo, o_hi), (wT_hi, o_lo)):
                                ins = pe.matmul(down_ps[g][:, t, :], hh[a][:, o, tok], w[2][:, o * D:(o + 1) * D],
                                                start=(k == 0), stop=(k == 3 * OT - 1))
                                k += 1
                    ins.then_inc(down_full, 1)
                pe.drain().then_inc(down_done, 1)

    @block.vector
    def _(dve):
        for s, v in ((y_stored[0], 16), (y_stored[1], 16), (unit_free, PAIRS), (prod_ready, 2), (sig16_ready, 1), (both_ready, 2), (down_done, 2), (down_free, 2)):
            dve.sem_inc(s, v)
        steps = [0]

        def link(ins):
            steps[0] += 1
            ins.then_inc(scale_step, 1)
            dve.wait_ge(scale_step, steps[0])

        def whole_max(k, parts):
            dve.tensor_reduce(sc[:, 2 * k:2 * k + 1], parts, AX.X if len(parts.shape) == 2 else AX.XY, ALU.max).then_inc(max_in, 1)

        def scales(k, unit, s, c):
            dve.wait_ge(max_out, k + 1)
            if unit is None:
                link(dve.tensor_scalar(s, sc[:, 2 * k + 1:2 * k + 2], 1.0 / QA, 1e-12, ALU.mult, ALU.max))
                link(dve.reciprocal(c, s))
                return
            link(dve.tensor_tensor(tmp, sc[:, 2 * k + 1:2 * k + 2], unit, ALU.mult))
            link(dve.tensor_scalar(s, tmp, 1.0 / QA, 1e-12, ALU.mult, ALU.max))
            link(dve.reciprocal(tmp, s))
            link(dve.tensor_tensor(c, tmp, unit, ALU.mult))

        whole_max(0, amax[:, :])
        dve.wait_ge(w_loaded, 48)
        nb = CT * I // BLK
        for m in range(3):
            blocks = w_nat[m].rearrange("p (b e) -> p b e", e=BLK)
            s, r = blk_s[:, m], blk_r[:, m]
            link(dve.tensor_reduce(r, blocks, AX.X, ALU.max, apply_absolute_value=True))
            link(dve.tensor_scalar(s, r, 1.0 / QW, 1e-12, ALU.mult, ALU.max))
            link(dve.reciprocal(r, s))
            step = w_step[m].rearrange("p (b e) -> p b e", e=BLK)
            link(dve.tensor_tensor(step, blocks, r.unsqueeze(2).to_broadcast([P, nb, BLK]), ALU.mult))
            link(dve.tensor_scalar(w_step[m], w_step[m], QW, -QW - 1.0, ALU.min, ALU.max))
            dve.tensor_tensor(blocks, step, s.unsqueeze(2).to_broadcast([P, nb, BLK]), ALU.mult).then_inc(w_quantized, 1)
        scales(0, None, s_x, c_x)
        for n in range(9):
            m, ps = n // 3, unit_ps[n % 3]
            dve.wait_ge(wT_hi_done, n + 1)
            for j in range(4):
                ins = dve.tensor_tensor(weight_dst(wT_lo, m, n % 3 * 4 + j), ps[:, 0, j * P:(j + 1) * P],
                                        weight_dst(wT_hi, m, n % 3 * 4 + j), ALU.subtract)
            ins.then_inc(wT_free, 1)
        dve.wait_ge(wT_free, 9)
        first = steps[0]
        with dve.Fori(0, NCH // 2) as n2:
            for a in range(2):
                n = n2 * 2 + a
                dve.tensor_scalar(xq[a], xnT_all[:, :, bass.ds(n * CH, CH)], c_x, None, ALU.mult).then_inc(scale_step, 1)
                dve.wait_ge(scale_step, n + first + 1)
                dve.tensor_scalar(x32[a], xq[a], 1.0 / 32, None, ALU.mult).then_inc(x32_ready, 1)
                dve.wait_ge(x32_ready, n + 1)
                dve.scalar_tensor_tensor(out=x_lo[:, :, bass.ds(n * CH, CH)], in0=x32[a], scalar=-32.0, in1=xq[a],
                                         op0=ALU.mult, op1=ALU.add).then_inc(x_lo_ready, 1)
                dve.wait_ge(gate_kept, n * PAIRS + PAIRS)
                dve.sem_inc(unit_free, PAIRS)
                dve.tensor_reduce(g_max[:, bass.ds(n, 1)], hid[:, :, bass.ds(n * CH, CH)], AX.XY, ALU.max,
                                  apply_absolute_value=True).then_inc(gate_max_done, 1)
        steps[0] += NCH
        dve.wait_ge(gate_max_done, NCH)
        whole_max(1, g_max[:, :])
        scales(1, s_x, s_gate, c_gate)
        link(dve.tensor_scalar(u_sig, s_gate, 1.0 / 65536, None, ALU.mult))
        dve.sem_inc(gate_scale, 1)
        with dve.Fori(0, NCH // 2) as n2:
            for a in range(2):
                n = n2 * 2 + a
                for j in range(PAIRS):
                    dve.wait_ge(unit_full, n * PAIRS + j + 1 + NCH * PAIRS)
                    dve.tensor_reduce(u_max[:, bass.ds(n, 1), j:j + 1], unit_ps[j][:, :, :], AX.XY, ALU.max,
                                      apply_absolute_value=True).then_inc(unit_free, 1)
                dve.wait_ge(sig_ready, n + 1)
                dve.tensor_scalar(sig16[a], sig, 65536.0, 65535.0, ALU.mult, ALU.min).then_inc(sig16_ready, 1)
                dve.wait_ge(sig16_ready, n + 2)
                dve.tensor_tensor(hid[:, :, bass.ds(n * CH, CH)], steps16[:, a], sig16[a], ALU.mult).then_inc(prod_ready, 1)
                dve.wait_ge(prod_ready, n + 3)
                dve.tensor_reduce(p_max[:, bass.ds(n, 1)], hid[:, :, bass.ds(n * CH, CH)], AX.XY, ALU.max,
                                  apply_absolute_value=True).then_inc(gate_max_done, 1)
        dve.wait_ge(gate_max_done, 2 * NCH)
        dve.tensor_reduce(sc[:, 4:5], u_max[:, :, :], AX.XY, ALU.max).then_inc(max_in, 1)
        dve.tensor_reduce(sc[:, 6:7], p_max[:, :], AX.X, ALU.max).then_inc(max_in, 1)
        scales(2, s_x, s_up, c_up)
        dve.sem_inc(up_scale, 1)
        scales(3, u_sig, s_gated, c_gated)
        link(dve.tensor_tensor(u_o, s_gated, s_up, ALU.mult))
        with dve.Fori(0, NCH // 2) as n2:
            for a in range(2):
                n = n2 * 2 + a
                dve.tensor_scalar(steps16[:, a], hid[:, :, bass.ds(n * CH, CH)], c_gated, None, ALU.mult).then_inc(gated16_ready, 1)
                dve.wait_ge(gated16_ready, n + 1)
                dve.wait_ge(up16_ready, n * PAIRS + PAIRS)
                dve.sem_inc(unit_free, PAIRS)
                dve.tensor_tensor(hid[:, :, bass.ds(n * CH, CH)], steps16[:, a], up16[a], ALU.mult).then_inc(both_ready, 1)
                dve.wait_ge(both_ready, n + 3)
                dve.tensor_reduce(q_max[:, bass.ds(n, 1)], hid[:, :, bass.ds(n * CH, CH)], AX.XY, ALU.max,
                                  apply_absolute_value=True).then_inc(gate_max_done, 1)
        dve.wait_ge(gate_max_done, 3 * NCH)
        dve.tensor_reduce(sc[:, 8:9], q_max[:, :], AX.X, ALU.max).then_inc(max_in, 1)
        scales(4, u_o, s_o, c_o)

        def join(m, g):
            dve.wait_ge(down_full, m * 2 + g + 1)
            dve.wait_ge(x3_loaded[g], m * 16 + 16)
            dve.wait_ge(y_stored[g], m * 16 + 16)
            dve.scalar_tensor_tensor(out=y_out[g], in0=down_ps[g][:, :, :], scalar=s_o, in1=x3_in[g],
                                     op0=ALU.mult, op1=ALU.add).then_inc(down_free, 1)

        with dve.Fori(0, NCH // 2) as n2:
            for a in range(2):
                n = n2 * 2 + a
                dve.tensor_scalar(steps16[:, a], hid[:, :, bass.ds(n * CH, CH)], c_o, None, ALU.mult).then_inc(o16_ready, 1)
                dve.wait_ge(o16_ready, n + 1)
                dve.tensor_scalar(up16[a], steps16[:, a], 1.0 / 32, None, ALU.mult).then_inc(o32_ready, 1)
                dve.wait_ge(o32_ready, n + 1)
                dve.wait_ge(down_done, n + 1)
                dve.scalar_tensor_tensor(out=o_lo[a], in0=up16[a], scalar=-32.0, in1=steps16[:, a],
                                         op0=ALU.mult, op1=ALU.add).then_inc(o_lo_ready, 1)
                for g in range(2):
                    join(n, g)


_INS = ["x", "ctxN", "ctxT", "mask", "WT", "COLS", "ROWS", "wg", "wu", "wd"]


def kernel(**z):
    import numpy as np
    import concourse.bacc as bacc
    from concourse.bass_utils import run_bass_kernel_spmd

    z = {k: np.asarray(v) for k, v in z.items()}
    ctx = z["ctx_1024"]
    arrays = {
        "x": z["x"], "ctxN": ctx, "ctxT": ctx.transpose(0, 2, 1), "mask": z["mask_Bx1xSxS2_ik1"].reshape(B, L, L),
        "WT": np.stack([z[n].T for n in ("L0_xattn_Wq", "L0_xattn_Wk", "L0_xattn_Wv", "L0_xattn_Wo",
                                         "L0_ffn_W_r", "L0_ffn_W_k", "L0_ffn_W_v", "L1_xattn_W_out")]),
        "COLS": np.stack([z[n].reshape(CT, P).T for n in ("L0_xattn_bq", "L0_xattn_bk", "L0_ffn_mu_r", "L0_ffn_mu_k")], 1),
        "ROWS": np.stack([z[n] for n in ("L0_xattn_bv", "L0_xattn_bo", "L1_xattn_b_out")]),
        "wg": z["L1_ffn_w_gate"], "wu": z["L1_ffn_w_up"], "wd": z["L1_ffn_w_down"],
    }
    arrays = {k: np.ascontiguousarray(v) for k, v in arrays.items()}
    nc = bacc.Bacc("TRN2", target_bir_lowering=False, num_devices=1)
    args = [nc.dram_tensor(k, arrays[k].shape, mybir.dt.from_np(arrays[k].dtype), kind="ExternalInput").ap() for k in _INS]
    args.append(nc.dram_tensor("out", [B, L, D], F32, kind="ExternalOutput").ap())
    build(nc, *args)
    r = run_bass_kernel_spmd(nc, [arrays], core_ids=[0])
    return r.results[0]["out"]
```

```python
from contextlib import ExitStack

import concourse.bass as bass
from concourse import mybir
from concourse.alu_op_type import AluOpType as ALU

F32 = mybir.dt.float32
F16 = mybir.dt.float16
I16 = mybir.dt.int16
U16 = mybir.dt.uint16
I32 = mybir.dt.int32
ACT = mybir.ActivationFunctionType
AX = mybir.AxisListType
RMAX = bass.bass_isa.ReduceOp.max

P = 128
B, L, D = 16, 256, 256
H, DH = 16, 16
TT = L // P
CT = D // P
LANES = 2
VW = 32
NEG = -60000.0
EPS = 1e-5
RING = 8
ROW_M = 3 * DH

MATS = ["q", "k", "v", "o", "r", "kk", "kv", "out"]


def prepare():
    yield from [(("stats", 0), 1.5), (("ctx_hi",), 0.5), (("rstd", 0), 0.4), (("ctx_lo",), 0.8), (("xn", 0), 0.6),
                (("proj", "k"), 0.7), (("T", 0), 0.6), (("hi", "k"), 0.5), (("lo", "k"), 0.5), (("T_hi", "xnT0"), 0.6),
                (("T_lo", "xnT0"), 0.8), (("proj", "q"), 1.6), (("hi", "q"), 0.8), (("lo", "q"), 1.0), (("proj", "v"), 1.4),
                (("v_out",), 1.0), (("values",), 0.2), (("mask",), 3.5)]


def attention(layer):
    for n in range(16):
        yield ("max", layer, n), 1.2
    yield from [(("mT", layer), 0.8), (("mneg", layer), 3.0)]
    for u in range(H):
        yield ("att", layer, u), 0.8
        if u % 4 == 1 and u > 4:
            yield ("weigh", layer, u // 4 - 1), 0.2
        if u == 11:
            yield ("gather", layer, 0), 0.1
    yield from [(("weigh", layer, 3), 1.0), (("gather", layer, 1), 0.7)]


def project(layer):
    for t in range(TT):
        yield ("oN", layer, t), 0.6
        yield ("divide", layer, t), 0.7
    yield from [(("oT", layer), 0.6), (("T_hi", f"oT{layer}"), 0.6), (("T_lo", f"oT{layer}"), 0.8), (("proj", f"ao{layer}"), 1.6), (("join", layer), 0.7)]


def middle():
    yield from project(0)
    yield from [(("stats", 1), 1.5), (("rstd", 1), 0.5), (("xn", 1), 0.7), (("T", 1), 0.6), (("xT_out",), 0.6), (("past", 0), 0.7),
                (("mix", 0), 0.7), (("past", 1), 0.1), (("mix_hi", 0), 0.6), (("mix", 1), 0.4), (("mix_lo", 0), 0.6), (("mix_hi", 1), 0.2), (("mix_lo", 1), 0.7),
                (("proj", "kk"), 1.5), (("relu",), 0.6), (("proj", "r"), 0.2), (("square",), 0.7), (("ka_hi",), 0.6), (("tanh",), 0.1), (("ka_lo",), 0.7),
                (("proj", "kv"), 0.5), (("gate",), 1.0), (("x2",), 1.5)]
    yield from [(("load",), 0.0), (("stats", 2), 1.5), (("mbT",), 0.3), (("rstd", 2), 0.5), (("mbT_out",), 0.1), (("xn", 2), 0.8), (("T", 2), 0.6), (("T_hi", "xnT2"), 0.6),
                (("T_lo", "xnT2"), 4.5)]


def finish():
    yield from project(1)
    yield from [(("store",), 0.0), (("stats", 3), 1.5), (("rstd", 3), 0.5), (("xn", 3), 0.7), (("T", 3), 0.6), (("amax",), 0.1), (("xnT_out",), 0.6)]


def of_lane(l, *stages):
    return [((l, ahead, step), length) for stage, ahead in stages for step, length in stage]


def weave(x, y):
    def starts(part):
        total, at, found = sum(length for _, length in part), 0.0, []
        for step, length in part:
            found.append((at / total, step))
            at += length
        return found
    return [step for _, step in sorted([*starts(x), *starts(y)], key=lambda a: a[0])]


PASSES = B // LANES - 1
PROLOGUE = weave(of_lane(0, (prepare(), 0)), []) + weave(of_lane(0, (attention(0), 0)), of_lane(1, (prepare(), 0)))
HALF = (weave(of_lane(0, (middle(), 0)), of_lane(1, (attention(0), 0))) +
        weave(of_lane(0, (attention(1), 0)), of_lane(1, (middle(), 0))))
BODY = (HALF + weave(of_lane(0, (finish(), 0), (prepare(), 1)), of_lane(1, (attention(1), 0))) +
        weave(of_lane(0, (attention(0), 1)), of_lane(1, (finish(), 0), (prepare(), 1))))
EPILOGUE = [e for e in HALF + weave(of_lane(0, (finish(), 0)), of_lane(1, (attention(1), 0))) + weave(of_lane(1, (finish(), 0)), [])
            if e[2] != ("load",)]

SPARE = {("T", n): f"xnT{n}" for n in range(4)}
SPARE |= {("proj", p): p for p in ("q", "k", "v", "r", "kk", "kv", "ao0", "ao1")}
SPARE |= {("oN", a, t): f"oN{a}{t}" for a in range(2) for t in range(TT)}
SPARE |= {("oT", 0): "oT0", ("oT", 1): "oT1", ("mT", 0): "mT0", ("mT", 1): "mT1", ("mbT",): "mbT"}


class At:

    def __init__(self, seg, i, l, ahead):
        self.seg, self.i, self.l, self.ahead, self.e = seg, i, l, ahead, i + ahead


class Turns:

    def __init__(self, turn_of):
        self.at = {}
        for name, seq in (("prologue", PROLOGUE), ("body", BODY), ("epilogue", EPILOGUE)):
            turns = [((l, turn_of(step)), ahead) for l, ahead, step in seq if turn_of(step) is not None]
            self.at[name] = {key: (k, ahead) for k, (key, ahead) in enumerate(turns)}
            if name == "prologue":
                self.first = len(turns)
            if name == "body":
                self.each = len(turns)

    def static(self, c, key):
        if c.seg == "prologue":
            return self.at["prologue"][c.l, key][0]
        k, ahead = self.at[c.seg].get((c.l, key), (None, 1))
        if ahead == c.ahead:
            return self.first + k
        k, ahead = self.at["body"][c.l, key]
        assert ahead == c.ahead + 1 and self.at["prologue"][c.l, key][0] == self.first - self.each + k
        return self.first - self.each + k

    def of(self, c, key):
        k = self.static(c, key)
        return k if c.seg == "prologue" else c.i * self.each + k


SPARE_TURNS = Turns(lambda step: SPARE.get(step))
MAX_TURNS = Turns(lambda step: step[1] if step[0] == "max" and step[2] == 0 else None)
ATT_TURNS = Turns(lambda step: step[1] if step[0] == "att" and step[2] == 0 else None)
OUT_TURNS = Turns(lambda step: step[1:] if step[0] == "gather" else None)
assert SPARE_TURNS.each % 2 == 0

HIS = ["c", "k", "xnT0", "q", "oT0", "xr", "xk", "ka", "xnT2", "oT1"]


BODY_LINKS = 34


def walk(eng, run):
    for l, ahead, step in PROLOGUE:
        run(At("prologue", 0, l, ahead), step)
    with eng.Fori(0, PASSES) as i:
        for l, ahead, step in BODY:
            run(At("body", i, l, ahead), step)
    for l, ahead, step in EPILOGUE:
        run(At("epilogue", PASSES, l, ahead), step)


def build(nc, x, ctxN, ctxT, mask, WT, COLS, ROWS, wg, wu, wd, out):
    scr = nc.dram_tensor("stack_scratch", [LANES, 6, D, L], F16)
    x3 = nc.dram_tensor("x3_scratch", [B, L, D], F32)
    with ExitStack() as whole:
        xnT_all = whole.enter_context(nc.sbuf_tensor("xnT_all", [P, CT, B * L], F32))
        amax = whole.enter_context(nc.sbuf_tensor("amax", [P, B], F32))
        ident = whole.enter_context(nc.sbuf_tensor("ident", [P, P], F32))
        with ExitStack() as ctx:
            layers(nc, ctx, scr, xnT_all, amax, ident, x, ctxN, ctxT, mask, WT, COLS, ROWS, x3)
        with ExitStack() as ctx:
            quantized_ffn(nc, ctx, xnT_all, amax, ident, x3, wg, wu, wd, out)


def layers(nc, ctx, scr, xnT_all, amax, ident, x, ctxN, ctxT, mask, WT, COLS, ROWS, x3):
    def sb(name, shape, dt=F32):
        return ctx.enter_context(nc.sbuf_tensor(name, shape, dt))

    def sb2(name, shape, dt=F32):
        return [sb(f"{name}{l}", shape, dt) for l in range(LANES)]

    def sem(name):
        return ctx.enter_context(nc.semaphore(name))

    def sem2(name):
        return [sem(f"{name}{l}") for l in range(LANES)]

    ident16 = sb("ident16", [P, P], F16)
    band = sb("band", [P, 2, P], F16)
    w_hi = sb("w_hi", [P, len(MATS), CT, D], F16)
    w_lo = sb("w_lo", [P, len(MATS), CT, D], F16)
    cols = sb("cols", [P, 4, CT])
    bias_q, bias_k, mu = cols[:, 0], cols[:, 1], cols[:, 2:4]
    omu = sb("omu", [P, 2, CT])
    rows = sb("rows", [P, 3, D])
    bvB, boB, boutB = rows[:, 0], rows[:, 1], rows[:, 2]
    zrow = sb("zrow", [P, H * L // P], F16)
    mhalf = sb("mhalf", [P, TT])
    xin, ctT, ctN, mk = sb2("xin", [P, TT, D]), sb2("ctT", [P, CT, L]), sb2("ctN", [P, TT, D]), sb2("mk", [P, TT, L], I32)
    xres, xb, xn = sb2("xres", [P, TT, D]), sb2("xb", [P, TT, D]), sb2("xn", [P, TT, D])
    st, mv, ve, rs = sb2("st", [P, TT, 6]), sb2("mv", [P, TT, 2]), sb2("ve", [P, TT]), sb2("rs", [P, TT])
    xh, xl = sb2("xh", [P, CT, L], F16), sb2("xl", [P, CT, L], F16)
    ch, cl = sb2("ch", [P, CT, L], F16), sb2("cl", [P, CT, L], F16)
    qh, ql = sb2("qh", [P, CT, L], F16), sb2("ql", [P, CT, L], F16)
    kh, kl = sb2("kh", [P, CT, L], F16), sb2("kl", [P, CT, L], F16)
    qst, kst0, kst1 = sb2("qst", [P, H, L], F16), sb2("kst0", [P, H, L], F16), sb2("kst1", [P, H, L], F16)
    val0, val1 = sb2("val0", [P, TT, H, VW]), sb2("val1", [P, TT, H, VW])
    anyk, anyn, mb, mbT = sb2("anyk", [P, TT]), sb2("anyn", [P, TT]), sb2("mb", [P, TT, L], F16), sb2("mbT", [P, TT, L], F16)
    mx, nm = sb2("mx", [P, TT, H]), sb2("nm", [H, L], F16)
    rc, on = sb2("rc", [P, TT, H]), sb2("on", [P, TT, D])
    xT, tm = sb2("xT", [P, CT, L + 1]), sb2("tm", [P, 2, CT, L])
    oT = [b[:, :, :, :].rearrange("p m t n -> p (m t) n") for b in tm]
    kr = sb2("kr", [P, CT, L])
    pT = sb("pT", [P, RING, TT, L])
    stage = pT[:, :, :, :].rearrange("p u t n -> p (u t n)").rearrange("p (m t n) -> p m t n", m=len(MATS), t=CT)

    score_ps = [ctx.enter_context(nc.psum_tensor(f"score_ps{j}", [P, TT, L], F32)) for j in range(3)]
    max_ps = [ctx.enter_context(nc.psum_tensor(f"max_ps{j}", [P, 2, L], F32)) for j in range(2)]
    spare_ps = [ctx.enter_context(nc.psum_tensor(f"spare_ps{j}", [P, 512], F32)) for j in range(2)]
    out_ps = ctx.enter_context(nc.psum_tensor("out_ps", [P, 2, L], F32))

    setup_loaded, id_set, id_done, band_set, consts_ready = sem("setup_loaded"), sem("id_set"), sem("id_done"), sem("band_set"), sem("consts_ready")
    w_hi_ready, w_lo_ready, zero_set = sem("w_hi_ready"), sem("w_lo_ready"), sem("zero_set")
    x_loaded, cT_loaded, cN_loaded, mk_loaded = sem2("x_loaded"), sem2("cT_loaded"), sem2("cN_loaded"), sem2("mk_loaded")
    used_act, used_dve, used_pool = sem2("used_act"), sem2("used_dve"), sem2("used_pool")
    var_ready, rstd_ready, xn_ready = sem2("var_ready"), sem2("rstd_ready"), sem2("xn_ready")
    hi_ready, cl_ready, val_ready, xb_ready, mb_ready = sem2("hi_ready"), sem2("cl_ready"), sem2("val_ready"), sem2("xb_ready"), sem2("mb_ready")
    lo_ready, mixed_ready, past_ready, kr_ready, x2_ready = sem2("lo_ready"), sem2("mixed_ready"), sem2("past_ready"), sem2("kr_ready"), sem2("x2_ready")
    v_ready = sem2("v_ready")
    scr_q, scr_k, scr_c = sem2("scr_q"), sem2("scr_k"), sem2("scr_c")
    q_stacked, k_stacked, c_stacked = sem2("q_stacked"), sem2("k_stacked"), sem2("c_stacked")
    x3_ready, x3_stored, amax_done, stats_seen = sem2("x3_ready"), sem2("x3_stored"), sem2("amax_done"), sem("stats_seen")
    max_full, max_free, score_full, exp_done, pv_done, out_free = sem("max_full"), sem("max_free"), sem("score_full"), sem("exp_done"), sem("pv_done"), sem("out_free")
    spare_full, spare_free = [sem("spare_full0"), sem("spare_full1")], [sem("spare_free0"), sem("spare_free1")]
    dve_step = sem("dve_step")

    SETUP_DMAS = len(MATS) + 2

    def spare(c, use):
        j = SPARE_TURNS.static(c, use) % 2
        before = SPARE_TURNS.static(c, use) // 2
        return spare_ps[j], j, before if c.seg == "prologue" else c.i * (SPARE_TURNS.each // 2) + before

    def wait_full(eng, c, use):
        _, j, k = spare(c, use)
        eng.wait_ge(spare_full[j], k + 1)

    def wait_evacuated(eng, c, use):
        _, j, k = spare(c, use)
        eng.wait_ge(spare_free[j], k + 2)

    def wait_hi(eng, c, name):
        eng.wait_ge(hi_ready[c.l], c.e * len(HIS) + HIS.index(name) + 1)

    def flat(ap):
        return ap[:, :, :].rearrange("p t n -> p (t n)")

    def tiled(ap):
        return ap.rearrange("p (t n) -> p t n", t=2)

    block = ctx.enter_context(nc.Block())

    @block.sync
    def _(sp):
        def load(l, e):
            b = e * LANES + l
            sp.dma_start(ctT[l][:, :, :], ctxT[b].rearrange("(t p) n -> p t n", p=P)).then_inc(cT_loaded[l], 16)
            sp.dma_start(xin[l][:, :, :], x[b].rearrange("(t p) d -> p t d", p=P)).then_inc(x_loaded[l], 16)
            sp.dma_start(mk[l][:, :, :], mask[b].rearrange("(t p) n -> p t n", p=P)).then_inc(mk_loaded[l], 16)
            sp.dma_start(ctN[l][:, :, :], ctxN[b].rearrange("(t p) d -> p t d", p=P)).then_inc(cN_loaded[l], 16)

        for m in range(len(MATS)):
            sp.dma_start(stage[:, m], WT[m].rearrange("(t p) d -> p t d", p=P)).then_inc(setup_loaded, 16)
        sp.dma_start(cols[:, :, :], COLS).then_inc(setup_loaded, 16)
        sp.dma_start(rows[:, :, :], ROWS.partition_broadcast(P)).then_inc(setup_loaded, 16)
        for l in range(LANES):
            load(l, 0)
        sp.wait_ge(zero_set, 2)

        def to_scratch(l, n, src, signal):
            sp.dma_start(scr[l, n].rearrange("(t p) n -> p t n", p=P), src[l][:, :, :]).then_inc(signal[l], 16)

        def stack_q(l):
            for row, n in ((0, 0), (DH, 0), (2 * DH, 1)):
                sp.dma_start(qst[l][row:row + DH, :, :], scr[l, n].rearrange("(h d) n -> d h n", d=DH)).then_inc(q_stacked[l], 16)
            sp.dma_start(qst[l][ROW_M:ROW_M + 1, :, :], zrow[:, :]).then_inc(q_stacked[l], 16)

        def stack_k(l, first, dst, signal):
            for row, n in ((0, first), (DH, first + 1), (2 * DH, first)):
                sp.dma_start(dst[l][row:row + DH, :, :], scr[l, n].rearrange("(h d) n -> d h n", d=DH)).then_inc(signal[l], 16)

        def run(c, step):
            l, e = c.l, c.e
            if step[0] == "load":
                sp.wait_ge(used_act[l], e + 1)
                sp.wait_ge(used_dve[l], e + 1)
                sp.wait_ge(used_pool[l], e + 1)
                load(l, e + 1)
            if step == ("ctx_lo",):
                wait_hi(sp, c, "c")
                to_scratch(l, 4, ch, scr_c)
                sp.wait_ge(cl_ready[l], e + 1)
                to_scratch(l, 5, cl, scr_c)
            if step == ("lo", "k"):
                wait_hi(sp, c, "k")
                to_scratch(l, 2, kh, scr_k)
                wait_evacuated(sp, c, "k")
                to_scratch(l, 3, kl, scr_k)
                sp.wait_ge(scr_c[l], e * 32 + 32)
                stack_k(l, 4, kst1, c_stacked)
            if step == ("lo", "q"):
                wait_hi(sp, c, "q")
                to_scratch(l, 0, qh, scr_q)
                wait_evacuated(sp, c, "q")
                to_scratch(l, 1, ql, scr_q)
                sp.wait_ge(scr_k[l], e * 32 + 32)
                stack_k(l, 2, kst0, k_stacked)
                sp.wait_ge(scr_q[l], e * 64 + 32)
                stack_q(l)
            if step == ("T_lo", "xnT2"):
                wait_hi(sp, c, "xnT2")
                to_scratch(l, 0, xh, scr_q)
                wait_evacuated(sp, c, "xnT2")
                to_scratch(l, 1, xl, scr_q)
                sp.wait_ge(scr_q[l], e * 64 + 64)
                stack_q(l)
            if step[0] == "mneg":
                wait_evacuated(sp, c, f"mT{step[1]}")
                sp.dma_start(qst[l][ROW_M:ROW_M + 1, :, :], nm[l][:, :]).then_inc(q_stacked[l], 16)
            if step[0] == "store":
                sp.wait_ge(x3_ready[l], e + 1)
                sp.dma_start(x3[e * LANES + l].rearrange("(t p) d -> p t d", p=P), xres[l][:, :, :]).then_inc(x3_stored[l], 16)

        walk(sp, run)
        for l in range(LANES):
            sp.wait_ge(x3_stored[l], 16 * (B // LANES) + 16)

    @block.gpsimd
    def _(pool):
        pool.memset(ident[:, :], 0.0).then_inc(id_set, 1)
        pool.memset(band[:, :, :], 0.0).then_inc(band_set, 1)
        pool.wait_ge(id_set, 1)
        pool.affine_select(out=ident[:, :], in_=ident[:, :], compare_op=ALU.not_equal, fill=1.0, base=0,
                           pattern=[[-1, P]], channel_multiplier=1).then_inc(id_done, 1)
        pool.wait_ge(band_set, 1)
        pool.affine_select(out=band[:, 0, :], in_=band[:, 0, :], compare_op=ALU.is_ge, fill=NEG, base=0,
                           pattern=[[-1, P]], channel_multiplier=1).then_inc(band_set, 1)
        pool.affine_select(out=band[:, 1, :], in_=band[:, 1, :], compare_op=ALU.is_ge, fill=NEG, base=0,
                           pattern=[[1, P]], channel_multiplier=-1).then_inc(band_set, 1)
        for l in range(LANES):
            pool.memset(val1[l][:, :, :, :], 0.0).then_inc(band_set, 1)
        pool.memset(mhalf[:, :], -0.5).then_inc(band_set, 1)
        pool.wait_ge(band_set, 4 + LANES)
        for l in range(LANES):
            pool.memset(val1[l][:, :, :, DH:DH + 1], 1.0).then_inc(band_set, 1)
        pool.wait_ge(band_set, 4 + 2 * LANES)
        pool.wait_ge(setup_loaded, 16 * SETUP_DMAS)

        def run(c, step):
            l, e = c.l, c.e
            if step[0] == "rstd":
                pool.wait_ge(var_ready[l], e * 4 + step[1] + 1)
                pool.tensor_tensor(rs[l][:, :], ve[l][:, :], mhalf[:, :], ALU.pow).then_inc(rstd_ready[l], 1)
            if step == ("ctx_lo",):
                wait_hi(pool, c, "c")
                pool.tensor_tensor(cl[l][:, :, :], ctT[l][:, :, :], ch[l][:, :, :], ALU.subtract).then_inc(cl_ready[l], 1)
            if step == ("values",):
                pool.wait_ge(cN_loaded[l], e * 16 + 16)
                pool.tensor_tensor(xb[l][:, :, :], xin[l][:, :, :], boB.unsqueeze(1).to_broadcast([P, TT, D]),
                                   ALU.add).then_inc(xb_ready[l], 1)
                for t in range(TT):
                    ins = pool.tensor_copy(val1[l][:, t, :, 0:DH], ctN[l][:, t, :].rearrange("p (h d) -> p h d", d=DH))
                ins.then_inc(val_ready[l], 1)
                pool.wait_ge(val_ready[l], e + 1)
                pool.sem_inc(used_pool[l], 1)
            if step == ("mbT",):
                pool.wait_ge(x2_ready[l], e + 1)
                pool.tensor_tensor(xb[l][:, :, :], xres[l][:, :, :], boutB.unsqueeze(1).to_broadcast([P, TT, D]),
                                   ALU.add).then_inc(xb_ready[l], 1)

        walk(pool, run)

    @block.scalar
    def _(act):
        act.wait_ge(setup_loaded, 16 * SETUP_DMAS)
        act.activation(w_hi[:, :, :, :].rearrange("p m t n -> p (m t n)"), stage.rearrange("p m t n -> p (m t n)"),
                       ACT.Copy).then_inc(w_hi_ready, 1)
        act.wait_ge(w_lo_ready, 1)

        def run(c, step):
            l, e, name = c.l, c.e, step[0]
            if name == "ctx_hi":
                act.wait_ge(cT_loaded[l], e * 16 + 16)
                act.activation(ch[l][:, :, :], ctT[l][:, :, :], ACT.Copy).then_inc(hi_ready[l], 1)
                act.wait_ge(hi_ready[l], e * len(HIS) + 1)
                act.sem_inc(used_act[l], 1)
            if name == "T_hi":
                wait_full(act, c, step[1])
                act.activation(flat(xh[l]), spare(c, step[1])[0][:, :], ACT.Copy).then_inc(hi_ready[l], 1)
            if name == "hi":
                dst, bias = {"q": (qh[l], bias_q), "k": (kh[l], bias_k)}[step[1]]
                wait_full(act, c, step[1])
                for t in range(CT):
                    ins = act.activation(dst[:, t, :], spare(c, step[1])[0][:, t * L:(t + 1) * L], ACT.Identity, bias=bias[:, t:t + 1])
                ins.then_inc(hi_ready[l], 1)
            if name == "mneg":
                use = f"mT{step[1]}"
                ps, j, _ = spare(c, use)
                wait_full(act, c, use)
                act.activation(nm[l][:, :], ps[0:H, 0:L], ACT.Copy, scale=-1.0).then_inc(spare_free[j], 1)
            if name == "att":
                _, layer, u = step
                scale = 1.0 / DH ** 0.5 if layer == 0 else 1.0 / D ** 0.5
                turn = ATT_TURNS.of(c, layer)
                act.wait_ge(score_full, turn * H + u + 1)
                if u % 4 == 0:
                    act.wait_ge(pv_done, turn * 4 + u // 4 + 1)
                act.activation(pT[:, u % RING], score_ps[u % 3][:, :, :], ACT.Exp, scale=scale).then_inc(exp_done, 1)
            if name == "xT_out":
                ps, j, _ = spare(c, "xnT1")
                wait_full(act, c, "xnT1")
                act.activation(xT[l][:, :, 1:L + 1], tiled(ps[:, :]), ACT.Copy).then_inc(spare_free[j], 1)
            if name == "past":
                wait_evacuated(act, c, "xnT1")
                m = step[1]
                for t in range(CT):
                    ins = act.activation(tm[l][:, m, t, :], xT[l][:, t, 0:L], ACT.Identity, scale=omu[:, m, t:t + 1])
                ins.then_inc(past_ready[l], 1)
            if name == "mix_hi":
                m = step[1]
                act.wait_ge(mixed_ready[l], e * 2 + m + 1)
                act.activation((qh, kh)[m][l][:, :, :], tm[l][:, m], ACT.Copy).then_inc(hi_ready[l], 1)
            if name == "tanh":
                ps, j, _ = spare(c, "r")
                wait_full(act, c, "r")
                act.activation(flat(on[l]), ps[:, :], ACT.Tanh, scale=0.5).then_inc(spare_free[j], 1)
            if name == "relu":
                wait_full(act, c, "kk")
                act.activation(flat(kr[l]), spare(c, "kk")[0][:, :], ACT.Relu).then_inc(kr_ready[l], 1)
            if name == "ka_hi":
                wait_evacuated(act, c, "kk")
                act.activation(xh[l][:, :, :], kr[l][:, :, :], ACT.Copy).then_inc(hi_ready[l], 1)
            if name == "mbT_out":
                ps, j, _ = spare(c, "mbT")
                wait_full(act, c, "mbT")
                act.activation(flat(mbT[l]), ps[:, :].bitcast(F16)[:, 0:TT * L], ACT.Copy).then_inc(spare_free[j], 1)
            if name == "xnT_out":
                ps, j, _ = spare(c, "xnT3")
                wait_full(act, c, "xnT3")
                act.activation(xnT_all[:, :, bass.ds((e * LANES + l) * L, L)], tiled(ps[:, :]), ACT.Copy).then_inc(spare_free[j], 1)

        walk(act, run)

    @block.tensor
    def _(pe):
        pe.wait_ge(id_done, 1)
        pe.wait_ge(consts_ready, 1)
        pe.wait_ge(w_lo_ready, 1)
        pe.wait_ge(band_set, 4 + 2 * LANES)

        def claim(c, use):
            ps, j, k = spare(c, use)
            pe.wait_ge(spare_free[j], k + 1)
            return ps, spare_full[j]

        def transposes(c, src, use):
            ps, full = claim(c, use)
            for t in range(TT):
                for k in range(CT):
                    ins = pe.transpose(ps[:, k * L + t * P:k * L + (t + 1) * P], src[:, t, k * P:(k + 1) * P], ident[:, :])
            ins.then_inc(full, 1)

        def product(c, mat, hi, lo, use, weights_first):
            m = MATS.index(mat)
            ps, full = claim(c, use)
            for t in range(2):
                n = 0
                for k in range(CT):
                    for a, w in ((hi, w_hi), (hi, w_lo), (lo, w_hi)):
                        if weights_first:
                            lhsT, rhs = w[:, m, k, t * P:(t + 1) * P], a[:, k, :]
                        else:
                            lhsT, rhs = a[:, k, t * P:(t + 1) * P], w[:, m, k, :]
                        ins = pe.matmul(ps[:, t * L:(t + 1) * L], lhsT, rhs, start=(n == 0), stop=(n == 3 * CT - 1))
                        n += 1
            ins.then_inc(full, 1)

        def proj(c, which):
            l, e = c.l, c.e
            if which == "k":
                wait_hi(pe, c, "c")
                pe.wait_ge(cl_ready[l], e + 1)
                product(c, "k", ch[l], cl[l], "k", True)
            if which == "v":
                product(c, "v", ch[l], cl[l], "v", False)
            if which == "q":
                wait_hi(pe, c, "xnT0")
                wait_evacuated(pe, c, "xnT0")
                product(c, "q", xh[l], xl[l], "q", True)
            if which == "r":
                wait_hi(pe, c, "xr")
                pe.wait_ge(lo_ready[l], e * 3 + 1)
                product(c, "r", qh[l], ql[l], "r", False)
            if which == "kk":
                wait_hi(pe, c, "xk")
                pe.wait_ge(lo_ready[l], e * 3 + 2)
                product(c, "kk", kh[l], kl[l], "kk", True)
            if which == "kv":
                wait_hi(pe, c, "ka")
                pe.wait_ge(lo_ready[l], e * 3 + 3)
                product(c, "kv", xh[l], xl[l], "kv", False)
            if which in ("ao0", "ao1"):
                layer = int(which[-1])
                wait_hi(pe, c, f"oT{layer}")
                wait_evacuated(pe, c, f"oT{layer}")
                product(c, ("o", "out")[layer], xh[l], xl[l], which, False)

        def maxima(c, layer, n):
            l, e = c.l, c.e
            kst = (kst0 if layer == 0 else kst1)[l]
            if n == 0:
                pe.wait_ge(q_stacked[l], e * 160 + 80 * layer + 64)
                pe.wait_ge((k_stacked if layer == 0 else c_stacked)[l], e * 48 + 48)
                if layer == 1:
                    pe.wait_ge(mb_ready[l], e + 1)
            t, h = n // 8, n % 8 * 2
            ps = max_ps[n % 2]
            pe.wait_ge(max_free, MAX_TURNS.of(c, layer) * 16 + n + 1)
            if layer == 0:
                off = (1 - t) * P
                pe.matmul(ps[:, :, off:off + P], ident16[:, :], band[:, t, :].unsqueeze(1).to_broadcast([P, 2, P]),
                          start=True, stop=False, skip_group_check=True)
            else:
                pe.matmul(ps[:, :, :], ident16[:, :], mb[l][:, t, :].unsqueeze(1).to_broadcast([P, 2, L]),
                          start=True, stop=False, skip_group_check=True)
            for a in range(2):
                ins = pe.matmul(ps[:, a, :], qst[l][:, h + a, t * P:(t + 1) * P], kst[:, h + a, :],
                                start=False, stop=(a == 1), skip_group_check=True)
            ins.then_inc(max_full, 1)

        def score(c, layer, u):
            l, e = c.l, c.e
            kst = (kst0 if layer == 0 else kst1)[l]
            if u == 0:
                pe.wait_ge(q_stacked[l], e * 160 + 80 * layer + 80)
                if layer == 1:
                    wait_evacuated(pe, c, "mbT")
            ps = score_ps[u % 3]
            pe.wait_ge(exp_done, ATT_TURNS.of(c, layer) * H + (u + 1 if u else 3))
            if layer == 0:
                pe.matmul(flat(ps)[:, P:3 * P], ident16[:, :], band[:, :, :].rearrange("p a n -> p (a n)"),
                          start=True, stop=False, skip_group_check=True)
            else:
                pe.matmul(flat(ps), ident16[:, :], flat(mbT[l]), start=True, stop=False, skip_group_check=True)
            for t in range(TT):
                ins = pe.matmul(ps[:, t, :], kst[:, u, t * P:(t + 1) * P], qst[l][:, u, :],
                                start=False, stop=(t == TT - 1), skip_group_check=True)
            ins.then_inc(score_full, 1)

        def weigh(c, layer, g):
            l, e = c.l, c.e
            val = (val0 if layer == 0 else val1)[l]
            if g == 0:
                if layer == 0:
                    pe.wait_ge(v_ready[l], e + 1)
                else:
                    pe.wait_ge(val_ready[l], e + 1)
            if g % 2 == 0:
                pe.wait_ge(out_free, OUT_TURNS.of(c, (layer, g // 2)) + 1)
            pe.wait_ge(exp_done, ATT_TURNS.of(c, layer) * H + 4 * g + 4 + 3)
            for t in range(TT):
                for r in range(4):
                    ins = pe.matmul(out_ps[VW * r:VW * (r + 1), g % 2, :], val[:, t, 4 * g + r, :],
                                    pT[:, (4 * g + r) % RING, t, :], start=(t == 0), stop=(t == TT - 1),
                                    skip_group_check=True, tile_position=(0, VW * r))
            ins.then_inc(pv_done, 1)

        def run(c, step):
            l, e, name = c.l, c.e, step[0]
            if name == "T":
                pe.wait_ge(xn_ready[l], e * 4 + step[1] + 1)
                transposes(c, xn[l], f"xnT{step[1]}")
            if name == "proj":
                proj(c, step[1])
            if name == "max":
                maxima(c, step[1], step[2])
            if name == "mT":
                layer = step[1]
                ps, full = claim(c, f"mT{layer}")
                pe.wait_ge(max_free, MAX_TURNS.of(c, layer) * 16 + 16 + 2)
                for t in range(TT):
                    ins = pe.transpose(ps[0:H, t * P:(t + 1) * P], mx[l][:, t, :], ident[:, :])
                ins.then_inc(full, 1)
            if name == "att":
                score(c, step[1], step[2])
            if name == "weigh":
                weigh(c, step[1], step[2])
            if name == "oN":
                _, layer, t = step
                pe.wait_ge(out_free, OUT_TURNS.of(c, (layer, 1)) + 2)
                ps, full = claim(c, f"oN{layer}{t}")
                for g in range(4):
                    ins = pe.transpose(ps[:, g * P:(g + 1) * P], oT[l][:, g, t * P:(t + 1) * P], ident[:, :])
                ins.then_inc(full, 1)
            if name == "oT":
                layer = step[1]
                for t in range(TT):
                    wait_evacuated(pe, c, f"oN{layer}{t}")
                transposes(c, on[l], f"oT{layer}")
            if name == "mbT":
                pe.wait_ge(mb_ready[l], e + 1)
                ps, full = claim(c, "mbT")
                for k in range(TT):
                    for t in range(TT):
                        ins = pe.transpose(ps[:, :].bitcast(F16)[:, k * L + t * P:k * L + (t + 1) * P],
                                           mb[l][:, t, k * P:(k + 1) * P], ident16[:, :])
                ins.then_inc(full, 1)

        walk(pe, run)

    @block.vector
    def _(dve):
        dve.memset(zrow[:, :], 0.0)
        for l in range(LANES):
            dve.memset(qst[l][:, :, :], 0.0)
            for kst in (kst0[l], kst1[l]):
                dve.memset(kst[:, :, :], 0.0)
            dve.memset(xT[l][:, :, 0:1], 0.0)
            dve.memset(val0[l][:, :, :, :], 0.0)
        dve.memset(amax[:, :], 0.0).then_inc(zero_set, 1)
        dve.wait_ge(zero_set, 1)
        for l in range(LANES):
            dve.memset(val0[l][:, :, :, DH:DH + 1], 1.0)
            for kst in (kst0[l], kst1[l]):
                ins = dve.memset(kst[32:64, :, :], 1.0)
        ins.then_inc(zero_set, 1)
        dve.wait_ge(id_done, 1)
        dve.tensor_copy(ident16[:, :], ident[:, :]).then_inc(consts_ready, 1)
        dve.wait_ge(consts_ready, 1)
        for s, ahead in ((spare_free[0], 1), (spare_free[1], 1), (max_free, 2), (exp_done, 3), (pv_done, 2), (out_free, 1),
                         (x3_stored[0], 16), (x3_stored[1], 16)):
            dve.sem_inc(s, ahead)
        dve.wait_ge(setup_loaded, 16 * SETUP_DMAS)
        dve.tensor_scalar(omu[:, :, :], mu, -1.0, 1.0, ALU.mult, ALU.add)
        dve.wait_ge(w_hi_ready, 1)
        dve.tensor_tensor(w_lo[:, :, :, :].rearrange("p m t n -> p (m t n)"), stage.rearrange("p m t n -> p (m t n)"),
                          w_hi[:, :, :, :].rearrange("p m t n -> p (m t n)"), ALU.subtract).then_inc(w_lo_ready, 1)
        dve.wait_ge(w_lo_ready, 1)

        links = {"prologue": 0, "body": 0, "epilogue": 0}

        def link(c, ins):
            links[c.seg] += 1
            ins.then_inc(dve_step, 1)
            before = 0 if c.seg == "prologue" else links["prologue"] + c.i * BODY_LINKS
            dve.wait_ge(dve_step, before + links[c.seg])

        def low(c, use, hi, lo, name):
            ps, j, _ = spare(c, use)
            wait_full(dve, c, use)
            wait_hi(dve, c, name)
            dve.tensor_tensor(flat(lo[c.l]), ps[:, :], flat(hi[c.l]), ALU.subtract).then_inc(spare_free[j], 1)

        def run(c, step):
            l, e, name = c.l, c.e, step[0]
            if name == "stats":
                n = step[1]
                src = xin[l] if n == 0 else xres[l]
                if n == 0:
                    dve.wait_ge(x_loaded[l], e * 16 + 16)
                for t in range(TT):
                    ins = dve.bn_stats(st[l][:, t, :], src[:, t, :])
                link(c, ins)
                dve.sem_inc(stats_seen, 1)
                for t in range(TT):
                    ins = dve.bn_aggr(mv[l][:, t, :], st[l][:, t, :])
                link(c, ins)
                dve.tensor_scalar(ve[l][:, :], mv[l][:, :, 1], EPS, None, ALU.add).then_inc(var_ready[l], 1)
            if name == "xn":
                n = step[1]
                src = xin[l] if n == 0 else xres[l]
                dve.wait_ge(rstd_ready[l], e * 4 + n + 1)
                if n == 2:
                    link(c, dve.tensor_tensor(rs[l][:, :], rs[l][:, :], anyk[l][:, :], ALU.mult))
                for t in range(TT):
                    ins = dve.tensor_scalar(xn[l][:, t, :], src[:, t, :], mv[l][:, t, 0:1], rs[l][:, t:t + 1], ALU.subtract, ALU.mult)
                ins.then_inc(xn_ready[l], 1)
            if name == "mask":
                dve.wait_ge(mk_loaded[l], e * 16 + 16)
                link(c, dve.tensor_scalar(kr[l][:, :, :], mk[l][:, :, :], 0.0, None, ALU.not_equal))
                link(c, dve.tensor_reduce(anyk[l][:, :], kr[l][:, :, :], AX.X, ALU.max))
                link(c, dve.tensor_scalar(anyn[l][:, :], anyk[l][:, :], NEG, None, ALU.mult))
                for t in range(TT):
                    ins = dve.tensor_scalar(mb[l][:, t, :], mk[l][:, t, :], 0.0, anyn[l][:, t:t + 1], ALU.is_equal, ALU.mult)
                ins.then_inc(mb_ready[l], 1)
                dve.wait_ge(mb_ready[l], e + 1)
                dve.wait_ge(xn_ready[l], e * 4 + 1)
                dve.sem_inc(used_dve[l], 1)
            if name == "T_lo":
                low(c, step[1], xh, xl, step[1])
            if name == "lo":
                hi, lo, bias = {"q": (qh[l], ql[l], bias_q), "k": (kh[l], kl[l], bias_k)}[step[1]]
                ps, j, _ = spare(c, step[1])
                wait_full(dve, c, step[1])
                wait_hi(dve, c, step[1])
                for t in range(CT):
                    ins = dve.scalar_tensor_tensor(out=lo[:, t, :], in0=ps[:, t * L:(t + 1) * L], scalar=bias[:, t:t + 1],
                                                   in1=hi[:, t, :], op0=ALU.add, op1=ALU.subtract)
                ins.then_inc(spare_free[j], 1)
            if name == "v_out":
                ps, j, _ = spare(c, "v")
                wait_full(dve, c, "v")
                for t in range(TT):
                    ins = dve.tensor_tensor(val0[l][:, t, :, 0:DH], ps[:, t * D:(t + 1) * D].rearrange("p (h d) -> p h d", d=DH),
                                            bvB.rearrange("p (h d) -> p h d", d=DH), ALU.add)
                ins.then_inc(spare_free[j], 1)
                wait_evacuated(dve, c, "v")
                dve.sem_inc(v_ready[l], 1)
            if name == "max":
                _, layer, n = step
                t, h = n // 8, n % 8 * 2
                dve.wait_ge(max_full, MAX_TURNS.of(c, layer) * 16 + n + 1)
                dve.tensor_reduce(mx[l][:, t, h:h + 2], max_ps[n % 2][:, :, :], AX.X, ALU.max).then_inc(max_free, 1)
            if name == "gather":
                _, layer, a = step
                dve.wait_ge(pv_done, ATT_TURNS.of(c, layer) * 4 + 2 * a + 2 + 2)
                dve.tensor_copy(oT[l][:, 2 * a:2 * a + 2, :], out_ps[:, :, :]).then_inc(out_free, 1)
            if name == "divide":
                _, layer, t = step
                use = f"oN{layer}{t}"
                ps, j, _ = spare(c, use)
                wait_full(dve, c, use)
                heads = ps[:, :].rearrange("p (h w) -> p h w", w=VW)
                link(c, dve.reciprocal(rc[l][:, t, :], heads[:, :, DH]))
                dve.tensor_tensor(on[l][:, t, :].rearrange("p (h d) -> p h d", d=DH), heads[:, :, 0:DH],
                                  rc[l][:, t, :].unsqueeze(2).to_broadcast([P, H, DH]), ALU.mult).then_inc(spare_free[j], 1)
            if name == "join":
                layer = step[1]
                use = f"ao{layer}"
                ps, j, _ = spare(c, use)
                wait_full(dve, c, use)
                dve.wait_ge(xb_ready[l], e * 2 + layer + 1)
                if layer == 0:
                    dve.wait_ge(x3_stored[l], e * 16 + 16)
                dve.tensor_tensor(flat(xres[l]), ps[:, :], flat(xb[l]), ALU.add).then_inc(spare_free[j], 1)
                wait_evacuated(dve, c, use)
                if layer == 1:
                    dve.sem_inc(x3_ready[l], 1)
            if name == "mix":
                m = step[1]
                dve.wait_ge(past_ready[l], e * 2 + m + 1)
                for t in range(CT):
                    ins = dve.scalar_tensor_tensor(out=tm[l][:, m, t, :], in0=xT[l][:, t, 1:L + 1], scalar=mu[:, m, t:t + 1],
                                                   in1=tm[l][:, m, t, :], op0=ALU.mult, op1=ALU.add)
                ins.then_inc(mixed_ready[l], 1)
            if name == "mix_lo":
                m = step[1]
                wait_hi(dve, c, ("xr", "xk")[m])
                dve.tensor_tensor((ql, kl)[m][l][:, :, :], tm[l][:, m], (qh, kh)[m][l][:, :, :], ALU.subtract).then_inc(lo_ready[l], 1)
            if name == "square":
                ps, j, _ = spare(c, "kk")
                dve.wait_ge(kr_ready[l], e + 1)
                dve.scalar_tensor_tensor(out=flat(kr[l]), in0=ps[:, :], scalar=0.0, in1=flat(kr[l]),
                                         op0=ALU.max, op1=ALU.mult).then_inc(spare_free[j], 1)
            if name == "ka_lo":
                wait_hi(dve, c, "ka")
                wait_evacuated(dve, c, "kk")
                dve.tensor_tensor(xl[l][:, :, :], kr[l][:, :, :], xh[l][:, :, :], ALU.subtract).then_inc(lo_ready[l], 1)
            if name == "gate":
                wait_evacuated(dve, c, "r")
                link(c, dve.tensor_scalar(on[l][:, :, :], on[l][:, :, :], 0.5, 0.5, ALU.mult, ALU.add))
            if name == "x2":
                ps, j, _ = spare(c, "kv")
                wait_full(dve, c, "kv")
                dve.tensor_tensor(flat(on[l]), ps[:, :], flat(on[l]), ALU.mult).then_inc(spare_free[j], 1)
                wait_evacuated(dve, c, "kv")
                dve.tensor_tensor(xres[l][:, :, :], xres[l][:, :, :], on[l][:, :, :], ALU.add).then_inc(x2_ready[l], 1)
                dve.wait_ge(x2_ready[l], e + 1)
            if name == "amax":
                dve.wait_ge(xn_ready[l], e * 4 + 4)
                dve.tensor_reduce(amax[:, bass.ds(e * LANES + l, 1)], xn[l][:, :, :], AX.XY, ALU.max,
                                  apply_absolute_value=True).then_inc(amax_done[l], 1)

        walk(dve, run)
        assert links["body"] == BODY_LINKS, links
        for l in range(LANES):
            dve.wait_ge(amax_done[l], B // LANES)


I = 768
OT = I // P
PAIRS = OT // 2
BLK = 32
N = B * L
CH = 512
NCH = N // CH
QA, QW = 32767.0, 7.0


def quantized_ffn(nc, ctx, xnT_all, amax, ident, x3, wg, wu, wd, out):
    def sb(name, shape, dt=F32):
        return ctx.enter_context(nc.sbuf_tensor(name, shape, dt))

    def sem(name):
        return ctx.enter_context(nc.semaphore(name))

    hid = sb("hid", [P, OT, N])
    x_hi, x_lo = sb("x_hi", [P, CT, N], F16), sb("x_lo", [P, CT, N], F16)
    wT_hi = [sb(f"wT_hi{m}", [P, CT * I], F16) for m in range(3)]
    wT_lo = [sb(f"wT_lo{m}", [P, CT * I], F16) for m in range(3)]
    steps16 = sb("steps16", [P, 2, OT, CH], I16)
    blk_s, blk_r = sb("blk_s", [P, 3, I * CT // BLK]), sb("blk_r", [P, 3, I * CT // BLK])
    sc = sb("sc", [P, 32])
    g_max, p_max, u_max, q_max = sb("g_max", [P, NCH]), sb("p_max", [P, NCH]), sb("u_max", [P, NCH, PAIRS]), sb("q_max", [P, NCH])

    w_nat = [hid[:, m, 0:CT * I] for m in range(3)]
    w_step = [hid[:, 3, m * CT * I // 2:(m + 1) * CT * I // 2].bitcast(I16) for m in range(2)] + [hid[:, 4, 0:CT * I // 2].bitcast(I16)]
    work = xnT_all[:, :, :].rearrange("p t n -> p (t n)")
    sig = work[:, 0:OT * CH].rearrange("p (o n) -> p o n", o=OT)
    half = [work[:, OT * CH + j * OT * CH // 2:OT * CH + (j + 1) * OT * CH // 2] for j in range(2)]
    sig16 = [h.bitcast(U16).rearrange("p (o n) -> p o n", o=OT) for h in half]
    up16 = [h.bitcast(I16).rearrange("p (o n) -> p o n", o=OT) for h in half]
    rest = work[:, 2 * OT * CH:2 * OT * CH + 4 * 2 * D].rearrange("p (j t d) -> p j t d", j=4, d=D)
    x3_in, y_out = [rest[:, j] for j in range(2)], [rest[:, 2 + j] for j in range(2)]
    tokens = x_hi[:, :, :].rearrange("p t n -> p (t n)"), x_lo[:, :, :].rearrange("p t n -> p (t n)")
    o_hi, o_lo = [[half[:, j * OT * CH:(j + 1) * OT * CH].rearrange("p (o n) -> p o n", o=OT) for j in range(2)] for half in tokens]
    xq = [steps16[:, 0, 2 * j:2 * j + 2, :] for j in range(2)]
    x32 = [steps16[:, 1, 2 * j:2 * j + 2, :] for j in range(2)]

    s_x, c_x, s_gate, c_gate, s_gated, c_gated, s_up, c_up, s_o, c_o = [sc[:, 12 + k:13 + k] for k in range(10)]
    u_sig, u_o, tmp = [sc[:, 22 + k:23 + k] for k in range(3)]

    unit_ps = [ctx.enter_context(nc.psum_tensor(f"unit_ps{j}", [P, 2, CH], F32)) for j in range(PAIRS)]
    down_ps = [ctx.enter_context(nc.psum_tensor(f"down_ps{j}", [P, 2, D], F32)) for j in range(2)]

    w_loaded, w_quantized, wT_full, wT_hi_done, wT_free = sem("w_loaded"), sem("w_quantized"), sem("wT_full"), sem("wT_hi_done"), sem("wT_free")
    amax_ready, max_in, max_out, scale_step = sem("amax_ready"), sem("max_in"), sem("max_out"), sem("scale_step")
    x32_ready, x_hi_ready, x_lo_ready = sem("x32_ready"), sem("x_hi_ready"), sem("x_lo_ready")
    unit_full, unit_free, gate_kept, gate_max_done = sem("unit_full"), sem("unit_free"), sem("gate_kept"), sem("gate_max_done")
    gate_scale, gate16_ready, sig_ready, sig16_ready, prod_ready = sem("gate_scale"), sem("gate16_ready"), sem("sig_ready"), sem("sig16_ready"), sem("prod_ready")
    up_scale, up16_ready, gated16_ready, both_ready = sem("up_scale"), sem("up16_ready"), sem("gated16_ready"), sem("both_ready")
    o16_ready, o32_ready, o_hi_ready, o_lo_ready = sem("o16_ready"), sem("o32_ready"), sem("o_hi_ready"), sem("o_lo_ready")
    down_full, down_free, down_done = sem("down_full"), sem("down_free"), sem("down_done")
    x3_loaded, y_stored = [sem("x3_loaded0"), sem("x3_loaded1")], [sem("y_stored0"), sem("y_stored1")]

    x3_v = x3.rearrange("b l d -> (b l) d").rearrange("(g t p) d -> g p t d", t=2, p=P)
    out_v = out.rearrange("b l d -> (b l) d").rearrange("(g t p) d -> g p t d", t=2, p=P)

    block = ctx.enter_context(nc.Block())

    @block.sync
    def _(sp):
        for m, w in enumerate((wg, wu)):
            sp.dma_start(w_nat[m].rearrange("p (t c) -> p t c", c=D), w.rearrange("(t p) c -> p t c", p=P)).then_inc(w_loaded, 16)
        sp.dma_start(w_nat[2].rearrange("p (t c) -> p t c", c=I), wd.rearrange("(t p) c -> p t c", p=P)).then_inc(w_loaded, 16)
        with sp.Fori(0, NCH) as n:
            for g in range(2):
                sp.wait_ge(down_free, n * 2 + g + 3)
                sp.dma_start(out_v[n * 2 + g], y_out[g]).then_inc(y_stored[g], 16)
        for g in range(2):
            sp.wait_ge(y_stored[g], 16 * NCH + 16)

    @block.gpsimd
    def _(pool):
        for k in range(5):
            pool.wait_ge(max_in, k + 1)
            pool.partition_all_reduce(sc[:, 2 * k + 1:2 * k + 2], sc[:, 2 * k:2 * k + 1], P, RMAX).then_inc(max_out, 1)
        with pool.Fori(0, NCH) as n:
            for g in range(2):
                pool.wait_ge(down_free, n * 2 + g + 1)
                pool.dma_start(x3_in[g], x3_v[n * 2 + g]).then_inc(x3_loaded[g], 16)

    def weight_block(m, k):
        if m < 2:
            o, c = k // CT, k % CT
            return w_nat[m][:, o * D + c * P:o * D + (c + 1) * P], c * I + o * P
        h, t = k % CT, k // CT
        return w_nat[m][:, h * I + t * P:h * I + (t + 1) * P], t * D + h * P

    def weight_dst(w, m, k):
        _, at = weight_block(m, k)
        return w[m][:, at:at + P]

    @block.scalar
    def _(act):
        for n in range(9):
            m, ps = n // 3, unit_ps[n % 3]
            act.wait_ge(wT_full, n + 1)
            for j in range(4):
                ins = act.activation(weight_dst(wT_hi, m, n % 3 * 4 + j), ps[:, 0, j * P:(j + 1) * P], ACT.Copy)
            ins.then_inc(wT_hi_done, 1)
        with act.Fori(0, NCH // 2) as n2:
            for a in range(2):
                n = n2 * 2 + a
                act.wait_ge(x32_ready, n + 1)
                act.activation(x_hi[:, :, bass.ds(n * CH, CH)], x32[a], ACT.Copy, scale=32.0).then_inc(x_hi_ready, 1)
                for j in range(PAIRS):
                    act.wait_ge(unit_full, n * PAIRS + j + 1)
                    act.activation(hid[:, 2 * j:2 * j + 2, bass.ds(n * CH, CH)], unit_ps[j][:, :, :], ACT.Copy).then_inc(gate_kept, 1)
        act.wait_ge(gate_scale, 1)
        with act.Fori(0, NCH // 2) as n2:
            for a in range(2):
                n = n2 * 2 + a
                act.wait_ge(prod_ready, n + 1)
                act.activation(steps16[:, a], hid[:, :, bass.ds(n * CH, CH)], ACT.Identity, scale=c_gate).then_inc(gate16_ready, 1)
                act.wait_ge(gate16_ready, n + 1)
                act.wait_ge(sig16_ready, n + 1)
                act.activation(sig, steps16[:, a], ACT.Sigmoid, scale=s_gate).then_inc(sig_ready, 1)
        act.wait_ge(up_scale, 1)
        with act.Fori(0, NCH // 2) as n2:
            for a in range(2):
                n = n2 * 2 + a
                act.wait_ge(both_ready, n + 1)
                for j in range(PAIRS):
                    act.wait_ge(unit_full, n * PAIRS + j + 1 + 2 * NCH * PAIRS)
                    act.activation(up16[a][:, 2 * j:2 * j + 2, :], unit_ps[j][:, :, :], ACT.Identity, scale=c_up).then_inc(up16_ready, 1)
        with act.Fori(0, NCH // 2) as n2:
            for a in range(2):
                n = n2 * 2 + a
                act.wait_ge(o32_ready, n + 1)
                act.wait_ge(down_done, n + 1)
                act.activation(o_hi[a], up16[a], ACT.Copy, scale=32.0).then_inc(o_hi_ready, 1)

    @block.tensor
    def _(pe):
        for n in range(9):
            m, ps = n // 3, unit_ps[n % 3]
            pe.wait_ge(w_quantized, m + 1)
            if n >= 3:
                pe.wait_ge(wT_free, n - 2)
            for j in range(4):
                src, _ = weight_block(m, n % 3 * 4 + j)
                ins = pe.transpose(ps[:, 0, j * P:(j + 1) * P], src, ident[:, :])
            ins.then_inc(wT_full, 1)
        pe.wait_ge(wT_free, 9)

        def units(n, m, first):
            for j in range(PAIRS):
                done_before = first + j
                pe.wait_ge(unit_free, n * PAIRS + done_before + 1)
                for a in range(2):
                    o, k = 2 * j + a, 0
                    for c in range(CT):
                        for w, xx in ((wT_hi, x_hi), (wT_lo, x_hi), (wT_hi, x_lo)):
                            ins = pe.matmul(unit_ps[j][:, a, :], w[m][:, c * I + o * P:c * I + (o + 1) * P],
                                            xx[:, c, bass.ds(n * CH, CH)], start=(k == 0), stop=(k == 3 * CT - 1))
                            k += 1
                ins.then_inc(unit_full, 1)

        for p, m in enumerate((0, 1, 1)):
            with pe.Fori(0, NCH) as n:
                if p == 0:
                    pe.wait_ge(x_hi_ready, n + 1)
                    pe.wait_ge(x_lo_ready, n + 1)
                units(n, m, p * NCH * PAIRS)
        with pe.Fori(0, NCH // 2) as n2:
            for a in range(2):
                n = n2 * 2 + a
                pe.wait_ge(o_hi_ready, n + 1)
                pe.wait_ge(o_lo_ready, n + 1)
                for g in range(2):
                    pe.wait_ge(down_free, n * 2 + g + 1)
                    for t in range(2):
                        k = 0
                        tok = slice((2 * g + t) * P, (2 * g + t + 1) * P)
                        for o in range(OT):
                            for w, hh in ((wT_hi, o_hi), (wT_lo, o_hi), (wT_hi, o_lo)):
                                ins = pe.matmul(down_ps[g][:, t, :], hh[a][:, o, tok], w[2][:, o * D:(o + 1) * D],
                                                start=(k == 0), stop=(k == 3 * OT - 1))
                                k += 1
                    ins.then_inc(down_full, 1)
                pe.drain().then_inc(down_done, 1)

    @block.vector
    def _(dve):
        for s, v in ((y_stored[0], 16), (y_stored[1], 16), (unit_free, PAIRS), (prod_ready, 2), (sig16_ready, 1), (both_ready, 2), (down_done, 2), (down_free, 2)):
            dve.sem_inc(s, v)
        steps = [0]

        def link(ins):
            steps[0] += 1
            ins.then_inc(scale_step, 1)
            dve.wait_ge(scale_step, steps[0])

        def whole_max(k, parts):
            dve.tensor_reduce(sc[:, 2 * k:2 * k + 1], parts, AX.X if len(parts.shape) == 2 else AX.XY, ALU.max).then_inc(max_in, 1)

        def scales(k, unit, s, c):
            dve.wait_ge(max_out, k + 1)
            if unit is None:
                link(dve.tensor_scalar(s, sc[:, 2 * k + 1:2 * k + 2], 1.0 / QA, 1e-12, ALU.mult, ALU.max))
                link(dve.reciprocal(c, s))
                return
            link(dve.tensor_tensor(tmp, sc[:, 2 * k + 1:2 * k + 2], unit, ALU.mult))
            link(dve.tensor_scalar(s, tmp, 1.0 / QA, 1e-12, ALU.mult, ALU.max))
            link(dve.reciprocal(tmp, s))
            link(dve.tensor_tensor(c, tmp, unit, ALU.mult))

        whole_max(0, amax[:, :])
        dve.wait_ge(w_loaded, 48)
        nb = CT * I // BLK
        for m in range(3):
            blocks = w_nat[m].rearrange("p (b e) -> p b e", e=BLK)
            s, r = blk_s[:, m], blk_r[:, m]
            link(dve.tensor_reduce(r, blocks, AX.X, ALU.max, apply_absolute_value=True))
            link(dve.tensor_scalar(s, r, 1.0 / QW, 1e-12, ALU.mult, ALU.max))
            link(dve.reciprocal(r, s))
            step = w_step[m].rearrange("p (b e) -> p b e", e=BLK)
            link(dve.tensor_tensor(step, blocks, r.unsqueeze(2).to_broadcast([P, nb, BLK]), ALU.mult))
            link(dve.tensor_scalar(w_step[m], w_step[m], QW, -QW - 1.0, ALU.min, ALU.max))
            dve.tensor_tensor(blocks, step, s.unsqueeze(2).to_broadcast([P, nb, BLK]), ALU.mult).then_inc(w_quantized, 1)
        scales(0, None, s_x, c_x)
        for n in range(9):
            m, ps = n // 3, unit_ps[n % 3]
            dve.wait_ge(wT_hi_done, n + 1)
            for j in range(4):
                ins = dve.tensor_tensor(weight_dst(wT_lo, m, n % 3 * 4 + j), ps[:, 0, j * P:(j + 1) * P],
                                        weight_dst(wT_hi, m, n % 3 * 4 + j), ALU.subtract)
            ins.then_inc(wT_free, 1)
        dve.wait_ge(wT_free, 9)
        first = steps[0]
        with dve.Fori(0, NCH // 2) as n2:
            for a in range(2):
                n = n2 * 2 + a
                dve.tensor_scalar(xq[a], xnT_all[:, :, bass.ds(n * CH, CH)], c_x, None, ALU.mult).then_inc(scale_step, 1)
                dve.wait_ge(scale_step, n + first + 1)
                dve.tensor_scalar(x32[a], xq[a], 1.0 / 32, None, ALU.mult).then_inc(x32_ready, 1)
                dve.wait_ge(x32_ready, n + 1)
                dve.scalar_tensor_tensor(out=x_lo[:, :, bass.ds(n * CH, CH)], in0=x32[a], scalar=-32.0, in1=xq[a],
                                         op0=ALU.mult, op1=ALU.add).then_inc(x_lo_ready, 1)
                dve.wait_ge(gate_kept, n * PAIRS + PAIRS)
                dve.sem_inc(unit_free, PAIRS)
                dve.tensor_reduce(g_max[:, bass.ds(n, 1)], hid[:, :, bass.ds(n * CH, CH)], AX.XY, ALU.max,
                                  apply_absolute_value=True).then_inc(gate_max_done, 1)
        steps[0] += NCH
        dve.wait_ge(gate_max_done, NCH)
        whole_max(1, g_max[:, :])
        scales(1, s_x, s_gate, c_gate)
        link(dve.tensor_scalar(u_sig, s_gate, 1.0 / 65536, None, ALU.mult))
        dve.sem_inc(gate_scale, 1)
        with dve.Fori(0, NCH // 2) as n2:
            for a in range(2):
                n = n2 * 2 + a
                for j in range(PAIRS):
                    dve.wait_ge(unit_full, n * PAIRS + j + 1 + NCH * PAIRS)
                    dve.tensor_reduce(u_max[:, bass.ds(n, 1), j:j + 1], unit_ps[j][:, :, :], AX.XY, ALU.max,
                                      apply_absolute_value=True).then_inc(unit_free, 1)
                dve.wait_ge(sig_ready, n + 1)
                dve.tensor_scalar(sig16[a], sig, 65536.0, 65535.0, ALU.mult, ALU.min).then_inc(sig16_ready, 1)
                dve.wait_ge(sig16_ready, n + 2)
                dve.tensor_tensor(hid[:, :, bass.ds(n * CH, CH)], steps16[:, a], sig16[a], ALU.mult).then_inc(prod_ready, 1)
                dve.wait_ge(prod_ready, n + 3)
                dve.tensor_reduce(p_max[:, bass.ds(n, 1)], hid[:, :, bass.ds(n * CH, CH)], AX.XY, ALU.max,
                                  apply_absolute_value=True).then_inc(gate_max_done, 1)
        dve.wait_ge(gate_max_done, 2 * NCH)
        dve.tensor_reduce(sc[:, 4:5], u_max[:, :, :], AX.XY, ALU.max).then_inc(max_in, 1)
        dve.tensor_reduce(sc[:, 6:7], p_max[:, :], AX.X, ALU.max).then_inc(max_in, 1)
        scales(2, s_x, s_up, c_up)
        dve.sem_inc(up_scale, 1)
        scales(3, u_sig, s_gated, c_gated)
        link(dve.tensor_tensor(u_o, s_gated, s_up, ALU.mult))
        with dve.Fori(0, NCH // 2) as n2:
            for a in range(2):
                n = n2 * 2 + a
                dve.tensor_scalar(steps16[:, a], hid[:, :, bass.ds(n * CH, CH)], c_gated, None, ALU.mult).then_inc(gated16_ready, 1)
                dve.wait_ge(gated16_ready, n + 1)
                dve.wait_ge(up16_ready, n * PAIRS + PAIRS)
                dve.sem_inc(unit_free, PAIRS)
                dve.tensor_tensor(hid[:, :, bass.ds(n * CH, CH)], steps16[:, a], up16[a], ALU.mult).then_inc(both_ready, 1)
                dve.wait_ge(both_ready, n + 3)
                dve.tensor_reduce(q_max[:, bass.ds(n, 1)], hid[:, :, bass.ds(n * CH, CH)], AX.XY, ALU.max,
                                  apply_absolute_value=True).then_inc(gate_max_done, 1)
        dve.wait_ge(gate_max_done, 3 * NCH)
        dve.tensor_reduce(sc[:, 8:9], q_max[:, :], AX.X, ALU.max).then_inc(max_in, 1)
        scales(4, u_o, s_o, c_o)

        def join(m, g):
            dve.wait_ge(down_full, m * 2 + g + 1)
            dve.wait_ge(x3_loaded[g], m * 16 + 16)
            dve.wait_ge(y_stored[g], m * 16 + 16)
            dve.scalar_tensor_tensor(out=y_out[g], in0=down_ps[g][:, :, :], scalar=s_o, in1=x3_in[g],
                                     op0=ALU.mult, op1=ALU.add).then_inc(down_free, 1)

        with dve.Fori(0, NCH // 2) as n2:
            for a in range(2):
                n = n2 * 2 + a
                dve.tensor_scalar(steps16[:, a], hid[:, :, bass.ds(n * CH, CH)], c_o, None, ALU.mult).then_inc(o16_ready, 1)
                dve.wait_ge(o16_ready, n + 1)
                dve.tensor_scalar(up16[a], steps16[:, a], 1.0 / 32, None, ALU.mult).then_inc(o32_ready, 1)
                dve.wait_ge(o32_ready, n + 1)
                dve.wait_ge(down_done, n + 1)
                dve.scalar_tensor_tensor(out=o_lo[a], in0=up16[a], scalar=-32.0, in1=steps16[:, a],
                                         op0=ALU.mult, op1=ALU.add).then_inc(o_lo_ready, 1)
                for g in range(2):
                    join(n, g)


_INS = ["x", "ctxN", "ctxT", "mask", "WT", "COLS", "ROWS", "wg", "wu", "wd"]


def kernel(**z):
    import numpy as np
    import concourse.bacc as bacc
    from concourse.bass_utils import run_bass_kernel_spmd

    z = {k: np.asarray(v) for k, v in z.items()}
    ctx = z["ctx_1024"]
    arrays = {
        "x": z["x"], "ctxN": ctx, "ctxT": ctx.transpose(0, 2, 1), "mask": z["mask_Bx1xSxS2_ik1"].reshape(B, L, L),
        "WT": np.stack([z[n].T for n in ("L0_xattn_Wq", "L0_xattn_Wk", "L0_xattn_Wv", "L0_xattn_Wo",
                                         "L0_ffn_W_r", "L0_ffn_W_k", "L0_ffn_W_v", "L1_xattn_W_out")]),
        "COLS": np.stack([z[n].reshape(CT, P).T for n in ("L0_xattn_bq", "L0_xattn_bk", "L0_ffn_mu_r", "L0_ffn_mu_k")], 1),
        "ROWS": np.stack([z[n] for n in ("L0_xattn_bv", "L0_xattn_bo", "L1_xattn_b_out")]),
        "wg": z["L1_ffn_w_gate"], "wu": z["L1_ffn_w_up"], "wd": z["L1_ffn_w_down"],
    }
    arrays = {k: np.ascontiguousarray(v) for k, v in arrays.items()}
    nc = bacc.Bacc("TRN2", target_bir_lowering=False, num_devices=1)
    args = [nc.dram_tensor(k, arrays[k].shape, mybir.dt.from_np(arrays[k].dtype), kind="ExternalInput").ap() for k in _INS]
    args.append(nc.dram_tensor("out", [B, L, D], F32, kind="ExternalOutput").ap())
    build(nc, *args)
    r = run_bass_kernel_spmd(nc, [arrays], core_ids=[0])
    return r.results[0]["out"]
```

```python
from contextlib import ExitStack

import concourse.bass as bass
from concourse import mybir
from concourse.alu_op_type import AluOpType as ALU

F32 = mybir.dt.float32
F16 = mybir.dt.float16
I16 = mybir.dt.int16
U16 = mybir.dt.uint16
I32 = mybir.dt.int32
ACT = mybir.ActivationFunctionType
AX = mybir.AxisListType
RMAX = bass.bass_isa.ReduceOp.max

P = 128
B, L, D = 16, 256, 256
H, DH = 16, 16
TT = L // P
CT = D // P
LANES = 2
VW = 32
NEG = -60000.0
EPS = 1e-5
HALF_H = H // 2
RING = 8
ROW_M = 3 * DH

MATS = ["q", "k", "v", "o", "r", "kk", "kv", "out"]
SCALED = ["r", "kk"]
PAST = len(MATS)
BIASED = {"v": 0, "ao0": 1, "ao1": 2}
GAP = 2



def prepare():
    return [(("stats", 0), 1.3), (("ctx_hi",), 0.1), (("rstd", 0), 0.62), (("ctx_lo",), 0.11), (("xn", 0), 2.17),
            (("proj", "k"), 1.5), (("hi", "k"), 1.37), (("lo", "k"), 0.6), (("T", 0), 0.00), (("T_hi", "xnT0"), 0.69),
            (("T_lo", "xnT0"), 1.26), (("proj", "q"), 1.5), (("hi", "q"), 0.8), (("lo", "q"), 0.98), (("proj", "v"), 1.62),
            (("v_out",), 0.72), (("values",), 0.10), (("mask",), 1.7)]


def attention(layer):
    steps = [(("max", layer, n), 0.62) for n in range(8)] + [(("mT", layer, 0), 0.35), (("mneg", layer, 0), 0.00)]
    steps += [(("max", layer, n), 0.53) for n in range(8, 12)]
    for u in range(H):
        steps += [(("att", layer, u), 0.5)]
        if u < 2:
            steps += [(("max", layer, 12 + 2 * u), 0.37), (("max", layer, 13 + 2 * u), 0.52)]
        if u == 2:
            steps += [(("mT", layer, 1), 0.00), (("mneg", layer, 1), 0.28)]
        if u % 4 == 1 and u > 4:
            steps += [(("weigh", layer, u // 4 - 1), 0.3)]
        if u == 11:
            steps += [(("gather", layer, 0), 1.05)]
    return steps + [(("weigh", layer, 3), 0.96), (("gather", layer, 1), 1.18)]


def project(layer):
    return [(("oN", layer, 0), 0.51), (("divide", layer, 0), 0.09), (("oN", layer, 1), 1.06), (("divide", layer, 1), 0.7),
            (("oT", layer), 0.54), (("T_hi", f"oT{layer}"), 0.64), (("T_lo", f"oT{layer}"), 1.92), (("proj", f"ao{layer}"), 0.54), (("join", layer), 0.57)]


def middle():
    return project(0) + [(("stats", 1), 1.09), (("rstd", 1), 0.00), (("xn", 1), 1.52), (("T", 1), 0.63), (("T_hi", "xnT1"), 0.6), (("T_lo", "xnT1"), 0.8),
                         (("proj", "kk"), 3.40), (("relu",), 0.00), (("square",), 1.26), (("proj", "r"), 0.1), (("ka_hi",), 0.51), (("tanh",), 0.11), (("ka_lo",), 0.81),
                         (("proj", "kv"), 1.5), (("x2",), 1.13),
                         (("load",), 0.00), (("stats", 2), 0.95), (("mbT",), 0.16), (("rstd", 2), 0.97), (("mbT_out",), 0.12), (("xn", 2), 0.76),
                         (("T", 2), 0.36), (("T_hi", "xnT2"), 0.21), (("T_lo", "xnT2"), 5.63)]


def finish():
    return project(1) + [(("store",), 0.00), (("stats", 3), 1.3), (("rstd", 3), 0.76), (("xn", 3), 0.81), (("T", 3), 1.95), (("amax",), 0.1), (("xnT_out",), 0.52)]


HELD = {"stats": "V1.22", "xn": "V0.77", "mask": "V1.82", "T_lo": "V0.59", "lo": "V0.73", "gather": "V0.61", "divide": "V0.66", "join": "V1.76",
        "square": "V0.71", "ka_lo": "V0.55", "x2": "V1.3", "amax": "V0.71", "ctx_hi": "S0.45", "T_hi": "S.5", "hi": "S1.46", "mneg": "S0.32",
        "v_out": "S0.89", "xnT_out": "S0.46", "mbT_out": "S0.43", "relu": "S0.87", "ka_hi": "S0.52", "tanh": "S0.46", "T": "T.45", "oN": "T0.57",
        "oT": "T0.29", "mT": "T.25", "mbT": "T.25", "weigh": "T1.60", "proj": "T0.46", "rstd": "P.6", "ctx_lo": "P1.1", "values": "P2.16",
        "max": "T.4 V0.62", "att": "T0.00 S.5"}
LONG = {("proj", "kk"): "T3.90", ("proj", "r"): "T1.89"}
LAG = 0.53
BEHIND = {"max": 0.30, "att": 0.33, "weigh": 0.22, "gather": 0.02, "stats": 0.01, "mask": 0.31, "values": 0.01, "proj": 0.01, "lo": 0.01, "hi": 0.01,
          "join": 0.01, "T_lo": 0.01, "T_hi": 0.01, "mT": 0.63, "mneg": 0.01, "divide": 0.01, "xn": 0.01, "T": 0.01, "oN": 0.01}


SPARE = {("T", n): f"xnT{n}" for n in range(4)}
SPARE |= {("proj", p): p for p in ("q", "k", "v", "r", "kk", "kv", "ao0", "ao1")}
SPARE |= {("oN", a, t): f"oN{a}{t}" for a in range(2) for t in range(TT)}
SPARE |= {("mT", a, g): f"mT{a}{g}" for a in range(2) for g in range(2)}
SPARE |= {("oT", 0): "oT0", ("oT", 1): "oT1", ("mbT",): "mbT"}
OVER = {"k": ("lo", "k"), "q": ("lo", "q"), "v": ("v_out",), "r": ("tanh",), "kk": ("square",), "kv": ("x2",), "mbT": ("mbT_out",),
        "xnT3": ("xnT_out",), "xnT0": ("T_lo", "xnT0"), "xnT1": ("T_lo", "xnT1"), "xnT2": ("T_lo", "xnT2")}
OVER |= {f"mT{a}{g}": ("mneg", a, g) for a in range(2) for g in range(2)} | {f"oT{a}": ("T_lo", f"oT{a}") for a in range(2)} | {f"ao{a}": ("join", a) for a in range(2)}
OVER |= {f"oN{a}{t}": ("divide", a, t) for a in range(2) for t in range(TT)}


def chain(l, ahead, steps):
    return [((l, ahead, step), length) for step, length in steps]


def after(*keys):
    return [(key, None) for key in keys]


def weave(*chains):
    chains, clock, free = [list(part) for part in chains], [0.0] * len(chains), {e: 0.0 for e in "VSTP"}
    found, claims, now = [], [], 0.0
    while any(chains):
        best = None
        for k, part in enumerate(chains):
            while part and part[0][1] is None and part[0][0] in found:
                part.pop(0)
                clock[k] = max(clock[k], now)
            if not part or part[0][1] is None:
                continue
            step = part[0][0][2]
            if step in SPARE and len(claims) > 1 and (claims[-2][0], claims[-2][1], OVER[claims[-2][2]]) not in found:
                continue
            held = [(h[0], float(h[1:])) for h in LONG.get(step, HELD.get(step[0], "")).split()]
            start = max([clock[k]] + [free[e] - LAG * i for i, (e, _) in enumerate(held)])
            rank = start + BEHIND.get(step[0], 0.0)
            if best is None or rank < best[0]:
                best = rank, k, start, held
        _, k, start, held = best
        key, length = chains[k].pop(0)
        for i, (e, time) in enumerate(held):
            free[e] = start + LAG * i + time
        now, clock[k] = max(now, start), start + length
        found.append(key)
        if key[2] in SPARE:
            claims.append((key[0], key[1], SPARE[key[2]]))
    return found


PASSES = B // LANES - 1


def attend(l, ahead, layer, last, part=slice(None)):
    chained = []
    for step, length in attention(layer)[part]:
        if last and step in (("max", layer, 0), ("att", layer, 0)):
            other, other_ahead, other_layer = last
            chained += after((other, other_ahead, ("max", other_layer, 15) if step[0] == "max" else ("gather", other_layer, 1)))
        chained += chain(l, ahead, [(step, length)])
    return chained


def attended(l, ahead, layer):
    return after((l, ahead, ("gather", layer, 1)))


def prepared(l, ahead):
    return after((l, ahead, ("mask",)))


CUT = [step for step, _ in attention(0)].index(("att", 0, 0))
OPENING, REST = slice(0, CUT), slice(CUT, None)
PROLOGUE = weave(chain(0, 0, prepare()) + attend(0, 0, 0, None), after((0, 0, ("mask",))) + chain(1, 0, prepare()) + attend(1, 0, 0, (0, 0, 0), OPENING))


def main_part(last):
    chains = [chain(0, 0, middle()) + attend(0, 0, 1, (1, 0, 0)),
              attend(1, 0, 0, None, REST) + chain(1, 0, middle()) + attend(1, 0, 1, (0, 0, 1)),
              attended(0, 0, 1) + chain(0, 0, finish()), attended(1, 0, 1) + chain(1, 0, finish())]
    if not last:
        chains += [attended(0, 0, 1) + chain(0, 1, prepare()) + attend(0, 1, 0, (1, 0, 1)),
                   attended(1, 0, 1) + chain(1, 1, prepare()) + attend(1, 1, 0, (0, 1, 0), OPENING)]
    return weave(*chains)


BODY, EPILOGUE = main_part(False), main_part(True)


class At:

    def __init__(self, seg, i, l, ahead):
        self.seg, self.i, self.l, self.ahead, self.e = seg, i, l, ahead, i + ahead


class Turns:

    def __init__(self, turn_of):
        self.at = {}
        for name, seq in (("prologue", PROLOGUE), ("body", BODY), ("epilogue", EPILOGUE)):
            turns = [((l, turn_of(step)), ahead) for l, ahead, step in seq if turn_of(step) is not None]
            self.at[name] = {key: (k, ahead) for k, (key, ahead) in enumerate(turns)}
            if name == "prologue":
                self.first = len(turns)
            if name == "body":
                self.each = len(turns)

    def static(self, c, key):
        if c.seg == "prologue":
            return self.at["prologue"][c.l, key][0]
        k, ahead = self.at[c.seg].get((c.l, key), (None, 1))
        if ahead == c.ahead:
            return self.first + k
        k, ahead = self.at["body"][c.l, key]
        assert ahead == c.ahead + 1 and self.at["prologue"][c.l, key][0] == self.first - self.each + k
        return self.first - self.each + k

    def of(self, c, key):
        k = self.static(c, key)
        return k if c.seg == "prologue" else c.i * self.each + k


SPARE_TURNS = Turns(lambda step: SPARE.get(step))
MAX_TURNS = Turns(lambda step: step[1] if step[0] == "max" and step[2] == 0 else None)
ATT_TURNS = Turns(lambda step: step[1] if step[0] == "att" and step[2] == 0 else None)
OUT_TURNS = Turns(lambda step: step[1:] if step[0] == "gather" else None)
assert SPARE_TURNS.each % 2 == 0

PREPARED, HIS = ["c", "k", "xnT0", "q"], ["oT0", "xnT1", "ka", "xnT2", "oT1"]
BODY_LINKS = 32


def walk(eng, run):
    for l, ahead, step in PROLOGUE:
        run(At("prologue", 0, l, ahead), step)
    with eng.Fori(0, PASSES) as i:
        for l, ahead, step in BODY:
            run(At("body", i, l, ahead), step)
    for l, ahead, step in EPILOGUE:
        run(At("epilogue", PASSES, l, ahead), step)


def build(nc, x, ctxN, ctxT, mask, WT, COLS, ROWS, wg, wu, wd, out):
    scr = nc.dram_tensor("stack_scratch", [LANES, 6, D, L], F16)
    x3 = nc.dram_tensor("x3_scratch", [B, L, D], F32)
    with ExitStack() as whole:
        xnT_all = whole.enter_context(nc.sbuf_tensor("xnT_all", [P, CT, B * L], F32))
        amax = whole.enter_context(nc.sbuf_tensor("amax", [P, B], F32))
        ident = whole.enter_context(nc.sbuf_tensor("ident", [P, P], F32))
        with ExitStack() as ctx:
            layers(nc, ctx, scr, xnT_all, amax, ident, x, ctxN, ctxT, mask, WT, COLS, ROWS, x3)
        with ExitStack() as ctx:
            quantized_ffn(nc, ctx, xnT_all, amax, ident, x3, wg, wu, wd, out)


def layers(nc, ctx, scr, xnT_all, amax, ident, x, ctxN, ctxT, mask, WT, COLS, ROWS, x3):
    def sb(name, shape, dt=F32):
        return ctx.enter_context(nc.sbuf_tensor(name, shape, dt))

    def sb2(name, shape, dt=F32):
        return [sb(f"{name}{l}", shape, dt) for l in range(LANES)]

    def sem(name):
        return ctx.enter_context(nc.semaphore(name))

    def sem2(name):
        return [sem(f"{name}{l}") for l in range(LANES)]

    ident16 = sb("ident16", [P, P], F16)
    band = sb("band", [P, 2, P], F16)
    w_hi = sb("w_hi", [P, PAST + len(SCALED), CT, D], F16)
    w_lo = sb("w_lo", [P, PAST + len(SCALED), CT, D], F16)
    cols = sb("cols", [P, 4, CT])
    bias_q, bias_k, mu = cols[:, 0], cols[:, 1], cols[:, 2:4]
    omu = sb("omu", [P, 2, CT])
    bias_rows = sb("bias_rows", [P, 3, D], F16)
    ones = sb("ones", [P, P], F16)
    zrow = sb("zrow", [P, H * L // P], F16)
    xin, ctT, ctN, mk = sb2("xin", [P, TT, D]), sb2("ctT", [P, CT, L]), sb2("ctN", [P, TT, D]), sb2("mk", [P, TT, L], I32)
    xres, xn, xn0 = sb2("xres", [P, TT, D]), sb2("xn", [P, TT, D]), sb2("xn0", [P, TT, D])
    mhalf, ve = sb("mhalf", [P, TT]), sb2("ve", [P, 2, TT])
    st, mv, rs = sb2("st", [P, 2, TT, 6]), sb2("mv", [P, 2, TT, 2]), sb2("rs", [P, 2, TT])
    xh, xl = sb2("xh", [P, CT, GAP + L], F16), sb2("xl", [P, CT, GAP + L], F16)
    x0h, x0l = sb2("x0h", [P, CT, L], F16), sb2("x0l", [P, CT, L], F16)
    ch, cl = sb2("ch", [P, CT, L], F16), sb2("cl", [P, CT, L], F16)
    qh, ql = sb2("qh", [P, CT, L], F16), sb2("ql", [P, CT, L], F16)
    kh, kl = sb2("kh", [P, CT, L], F16), sb2("kl", [P, CT, L], F16)
    qst, kst0, kst1 = sb2("qst", [P, H, L], F16), sb2("kst0", [P, H, L], F16), sb2("kst1", [P, H, L], F16)
    val0, val1 = sb2("val0", [P, TT, H, VW]), sb2("val1", [P, TT, H, VW])
    anyk, anyn, mb, mbT = sb2("anyk", [P, TT]), sb2("anyn", [P, TT]), sb2("mb", [P, TT, L], F16), sb2("mbT", [P, TT, L], F16)
    mx, nm = sb2("mx", [P, TT, H]), sb2("nm", [HALF_H, 2, L], F16)
    rc, on = sb2("rc", [P, TT, H]), sb2("on", [P, TT, D])
    oT = sb2("oT", [P, 4, L])
    kr = [b[:, 0:CT, :] for b in oT]
    rows, rows_hi = oT[0][:, 0:3, :], oT[1][:, 0:3, :]
    pT = sb("pT", [P, RING, TT, L])
    stage = pT[:, :, :, :].rearrange("p u t n -> p (u t n)").rearrange("p (m t n) -> p m t n", m=len(MATS), t=CT)

    score_ps = [ctx.enter_context(nc.psum_tensor(f"score_ps{j}", [P, TT, L], F32)) for j in range(3)]
    max_ps = [ctx.enter_context(nc.psum_tensor(f"max_ps{j}", [P, 2, L], F32)) for j in range(2)]
    spare_ps = [ctx.enter_context(nc.psum_tensor(f"spare_ps{j}", [P, 512], F32)) for j in range(2)]
    out_ps = ctx.enter_context(nc.psum_tensor("out_ps", [P, 2, L], F32))

    setup_loaded, id_set, id_done, band_set, consts_ready = sem("setup_loaded"), sem("id_set"), sem("id_done"), sem("band_set"), sem("consts_ready")
    w_hi_ready, w_lo_ready, zero_set, ones_set, omu_ready, bias_step = sem("w_hi_ready"), sem("w_lo_ready"), sem("zero_set"), sem("ones_set"), sem("omu_ready"), sem("bias_step")
    x_loaded, cT_loaded, cN_loaded, mk_loaded = sem2("x_loaded"), sem2("cT_loaded"), sem2("cN_loaded"), sem2("mk_loaded")
    used_act, used_dve, used_pool = sem2("used_act"), sem2("used_dve"), sem2("used_pool")
    var0_ready, rstd0_ready, xn0_ready = sem2("var0_ready"), sem2("rstd0_ready"), sem2("xn0_ready")
    var_ready, rstd_ready, xn_ready = sem2("var_ready"), sem2("rstd_ready"), sem2("xn_ready")
    prepared_hi, hi_ready, cl_ready, val_ready, mb_ready = sem2("prepared_hi"), sem2("hi_ready"), sem2("cl_ready"), sem2("val_ready"), sem2("mb_ready")
    ka_lo_ready, kr_ready, x2_ready, val1_free = sem2("ka_lo_ready"), sem2("kr_ready"), sem2("x2_ready"), sem2("val1_free")
    v_ready = sem2("v_ready")
    m_cleared, scr_qh, scr_ql, scr_k, scr_c = sem2("m_cleared"), sem2("scr_qh"), sem2("scr_ql"), sem2("scr_k"), sem2("scr_c")
    m_stacked = [[sem(f"m_stacked{l}{g}") for g in range(2)] for l in range(LANES)]
    q_stacked, k_stacked, c_stacked = sem2("q_stacked"), sem2("k_stacked"), sem2("c_stacked")
    x3_ready, x3_stored, amax_done, stats_seen = sem2("x3_ready"), sem2("x3_stored"), sem2("amax_done"), sem("stats_seen")
    max_full, max_free, score_full, exp_done, pv_done, out_free = sem("max_full"), sem("max_free"), sem("score_full"), sem("exp_done"), sem("pv_done"), sem("out_free")
    spare_full, spare_free = [sem("spare_full0"), sem("spare_full1")], [sem("spare_free0"), sem("spare_free1")]
    dve_step = sem("dve_step")

    SETUP_DMAS = len(MATS) + 2

    def spare(c, use):
        j = SPARE_TURNS.static(c, use) % 2
        before = SPARE_TURNS.static(c, use) // 2
        return spare_ps[j], j, before if c.seg == "prologue" else c.i * (SPARE_TURNS.each // 2) + before

    def wait_full(eng, c, use):
        _, j, k = spare(c, use)
        eng.wait_ge(spare_full[j], k + 1)

    def wait_evacuated(eng, c, use):
        _, j, k = spare(c, use)
        eng.wait_ge(spare_free[j], k + 2)

    def wait_hi(eng, c, name):
        if name in PREPARED:
            eng.wait_ge(prepared_hi[c.l], c.e * len(PREPARED) + PREPARED.index(name) + 1)
        else:
            eng.wait_ge(hi_ready[c.l], c.e * len(HIS) + HIS.index(name) + 1)

    def wait_normal(eng, c, n, first, others):
        if n == 0:
            eng.wait_ge(first[c.l], c.e + 1)
        else:
            eng.wait_ge(others[c.l], c.e * 3 + n)

    def halves(l, name):
        if name == "ka":
            return kh[l], kl[l]
        return (x0h[l], x0l[l]) if name == "xnT0" else (xh[l][:, :, GAP:], xl[l][:, :, GAP:])

    def tile_heads(n):
        return n // 4 % 2, n // 8 * HALF_H + n % 4 * 2

    def flat(ap):
        return ap[:, :, :].rearrange("p t n -> p (t n)")

    def tiled(ap):
        return ap.rearrange("p (t n) -> p t n", t=2)

    block = ctx.enter_context(nc.Block())

    @block.sync
    def _(sp):
        def load(l, e):
            b = e * LANES + l
            sp.dma_start(ctT[l][:, :, :], ctxT[b].rearrange("(t p) n -> p t n", p=P)).then_inc(cT_loaded[l], 16)
            sp.dma_start(xin[l][:, :, :], x[b].rearrange("(t p) d -> p t d", p=P)).then_inc(x_loaded[l], 16)
            sp.dma_start(mk[l][:, :, :], mask[b].rearrange("(t p) n -> p t n", p=P)).then_inc(mk_loaded[l], 16)
            sp.dma_start(ctN[l][:, :, :], ctxN[b].rearrange("(t p) d -> p t d", p=P)).then_inc(cN_loaded[l], 16)

        for m in range(len(MATS)):
            sp.dma_start(stage[:, m], WT[m].rearrange("(t p) d -> p t d", p=P)).then_inc(setup_loaded, 16)
        sp.dma_start(cols[:, :, :], COLS).then_inc(setup_loaded, 16)
        sp.dma_start(rows, ROWS.partition_broadcast(P)).then_inc(setup_loaded, 16)
        for l in range(LANES):
            load(l, 0)
        sp.wait_ge(zero_set, 1)
        sp.wait_ge(ones_set, 1)

        def to_scratch(l, n, src, signal):
            sp.dma_start(scr[l, n].rearrange("(t p) n -> p t n", p=P), src).then_inc(signal[l], 16)

        def clear_m(l):
            sp.dma_start(qst[l][ROW_M:ROW_M + 1, :, :], zrow[:, :]).then_inc(m_cleared[l], 16)

        def stack_q(l, e, layer):
            for row, n in ((0, 0), (DH, 0), (2 * DH, 1)):
                if row != DH:
                    sp.wait_ge((scr_qh, scr_ql)[n][l], e * 32 + 16 * layer + 16)
                sp.dma_start(qst[l][row:row + DH, :, :], scr[l, n].rearrange("(h d) n -> d h n", d=DH)).then_inc(q_stacked[l], 16)

        def stack_k(l, first, dst, signal):
            for row, n in ((0, first), (DH, first + 1), (2 * DH, first)):
                sp.dma_start(dst[l][row:row + DH, :, :], scr[l, n].rearrange("(h d) n -> d h n", d=DH)).then_inc(signal[l], 16)

        def run(c, step):
            l, e = c.l, c.e
            if step[0] == "load":
                sp.wait_ge(used_act[l], e + 1)
                sp.wait_ge(used_dve[l], e + 1)
                sp.wait_ge(used_pool[l], e + 1)
                if c.seg != "epilogue":
                    load(l, e + 1)
                clear_m(l)
            if step == ("ctx_lo",):
                wait_hi(sp, c, "c")
                clear_m(l)
                to_scratch(l, 4, ch[l][:, :, :], scr_c)
                sp.wait_ge(cl_ready[l], e + 1)
                to_scratch(l, 5, cl[l][:, :, :], scr_c)
            if step == ("T", 0):
                sp.wait_ge(scr_k[l], e * 32 + 32)
                stack_k(l, 2, kst0, k_stacked)
            if step == ("lo", "k"):
                wait_hi(sp, c, "k")
                to_scratch(l, 2, kh[l][:, :, :], scr_k)
                wait_evacuated(sp, c, "k")
                to_scratch(l, 3, kl[l][:, :, :], scr_k)
                sp.wait_ge(scr_c[l], e * 32 + 32)
                stack_k(l, 4, kst1, c_stacked)
            if step == ("lo", "q"):
                wait_hi(sp, c, "q")
                to_scratch(l, 0, qh[l][:, :, :], scr_qh)
                wait_evacuated(sp, c, "q")
                to_scratch(l, 1, ql[l][:, :, :], scr_ql)
                stack_q(l, e, 0)
            if step == ("T_lo", "xnT2"):
                wait_hi(sp, c, "xnT2")
                to_scratch(l, 0, halves(l, "xnT2")[0], scr_qh)
                wait_evacuated(sp, c, "xnT2")
                to_scratch(l, 1, halves(l, "xnT2")[1], scr_ql)
                stack_q(l, e, 1)
            if step[0] == "mneg":
                _, layer, g = step
                wait_evacuated(sp, c, f"mT{layer}{g}")
                sp.dma_start(qst[l][ROW_M:ROW_M + 1, g * HALF_H:(g + 1) * HALF_H, :], nm[l][:, g, :]).then_inc(m_stacked[l][g], 16)
            if step[0] == "store":
                sp.wait_ge(x3_ready[l], e + 1)
                sp.dma_start(x3[e * LANES + l].rearrange("(t p) d -> p t d", p=P), xres[l][:, :, :]).then_inc(x3_stored[l], 16)

        walk(sp, run)
        for l in range(LANES):
            sp.wait_ge(x3_stored[l], 16 * (B // LANES) + 16)

    @block.gpsimd
    def _(pool):
        pool.memset(ident[:, :], 0.0).then_inc(id_set, 1)
        pool.memset(band[:, :, :], 0.0).then_inc(band_set, 1)
        pool.wait_ge(id_set, 1)
        pool.affine_select(out=ident[:, :], in_=ident[:, :], compare_op=ALU.not_equal, fill=1.0, base=0,
                           pattern=[[-1, P]], channel_multiplier=1).then_inc(id_done, 1)
        pool.wait_ge(band_set, 1)
        pool.affine_select(out=band[:, 0, :], in_=band[:, 0, :], compare_op=ALU.is_ge, fill=NEG, base=0,
                           pattern=[[-1, P]], channel_multiplier=1).then_inc(band_set, 1)
        pool.affine_select(out=band[:, 1, :], in_=band[:, 1, :], compare_op=ALU.is_ge, fill=NEG, base=0,
                           pattern=[[1, P]], channel_multiplier=-1).then_inc(band_set, 1)
        for l in range(LANES):
            pool.memset(val1[l][:, :, :, :], 0.0).then_inc(band_set, 1)
        pool.memset(ones[:, :], 1.0)
        pool.memset(mhalf[:, :], -0.5).then_inc(band_set, 1)
        pool.wait_ge(band_set, 4 + LANES)
        for l in range(LANES):
            pool.memset(val1[l][:, :, :, DH:DH + 1], 1.0).then_inc(band_set, 1)
        pool.wait_ge(band_set, 4 + 2 * LANES)
        for l in range(LANES):
            for kst in (kst0[l], kst1[l]):
                ins = pool.memset(kst[:, :, :], 1.0)
        ins.then_inc(ones_set, 1)

        def run(c, step):
            l, e = c.l, c.e
            if step[0] == "rstd":
                n = step[1]
                wait_normal(pool, c, n, var0_ready, var_ready)
                pool.tensor_tensor(rs[l][:, int(n > 0)], ve[l][:, int(n > 0)], mhalf[:, :], ALU.pow).then_inc((rstd0_ready if n == 0 else rstd_ready)[l], 1)
            if step == ("ctx_lo",):
                wait_hi(pool, c, "c")
                pool.tensor_tensor(cl[l][:, :, :], ctT[l][:, :, :], ch[l][:, :, :], ALU.subtract).then_inc(cl_ready[l], 1)
            if step == ("values",):
                pool.wait_ge(cN_loaded[l], e * 16 + 16)
                pool.wait_ge(val1_free[l], e + 1)
                pool.sem_inc(stats_seen, 1)
                for t in range(TT):
                    ins = pool.tensor_copy(val1[l][:, t, :, 0:DH], ctN[l][:, t, :].rearrange("p (h d) -> p h d", d=DH))
                ins.then_inc(val_ready[l], 1)
                pool.wait_ge(val_ready[l], e + 1)
                pool.sem_inc(used_pool[l], 1)

        walk(pool, run)

    @block.scalar
    def _(act):
        act.wait_ge(setup_loaded, 16 * SETUP_DMAS)
        act.wait_ge(omu_ready, 1)
        for m, mat in enumerate(MATS):
            if mat not in SCALED:
                act.activation(w_hi[:, m, :, :], stage[:, m], ACT.Copy).then_inc(w_hi_ready, 1)
        for s, mat in enumerate(SCALED):
            for t in range(CT):
                for m, factor in ((MATS.index(mat), mu), (PAST + s, omu)):
                    act.activation(w_hi[:, m, t, :], stage[:, MATS.index(mat), t], ACT.Identity,
                                   scale=factor[:, s, t:t + 1]).then_inc(w_hi_ready, 1)
        act.wait_ge(w_lo_ready, 1)

        def run(c, step):
            l, e, name = c.l, c.e, step[0]
            if name == "ctx_hi":
                act.wait_ge(cT_loaded[l], e * 16 + 16)
                act.activation(ch[l][:, :, :], ctT[l][:, :, :], ACT.Copy).then_inc(prepared_hi[l], 1)
                wait_hi(act, c, "c")
                act.sem_inc(used_act[l], 1)
            if name == "T_hi":
                wait_full(act, c, step[1])
                act.activation(halves(l, step[1])[0][:, :, :], tiled(spare(c, step[1])[0][:, :]),
                               ACT.Copy).then_inc((prepared_hi if step[1] in PREPARED else hi_ready)[l], 1)
            if name == "hi":
                dst, bias = {"q": (qh[l], bias_q), "k": (kh[l], bias_k)}[step[1]]
                wait_full(act, c, step[1])
                for t in range(CT):
                    ins = act.activation(dst[:, t, :], spare(c, step[1])[0][:, t * L:(t + 1) * L], ACT.Identity, bias=bias[:, t:t + 1])
                ins.then_inc(prepared_hi[l], 1)
            if name == "mneg":
                _, layer, g = step
                use = f"mT{layer}{g}"
                ps, j, _ = spare(c, use)
                wait_full(act, c, use)
                act.activation(nm[l][:, g, :], ps[0:HALF_H, 0:L], ACT.Copy, scale=-1.0).then_inc(spare_free[j], 1)
            if name == "att":
                _, layer, u = step
                scale = 1.0 / DH ** 0.5 if layer == 0 else 1.0 / D ** 0.5
                turn = ATT_TURNS.of(c, layer)
                act.wait_ge(score_full, turn * H + u + 1)
                if u % 4 == 0:
                    act.wait_ge(pv_done, turn * 4 + u // 4 + 1)
                act.activation(pT[:, u % RING], score_ps[u % 3][:, :, :], ACT.Exp, scale=scale).then_inc(exp_done, 1)
            if name == "v_out":
                ps, j, _ = spare(c, "v")
                wait_full(act, c, "v")
                act.activation(val0[l][:, :, :, 0:DH].rearrange("p t h d -> p (t h) d"), ps[:, :].rearrange("p (a d) -> p a d", d=DH),
                               ACT.Copy).then_inc(spare_free[j], 1)
                wait_evacuated(act, c, "v")
                act.sem_inc(v_ready[l], 1)
            if name == "tanh":
                ps, j, _ = spare(c, "r")
                wait_full(act, c, "r")
                act.activation(flat(on[l]), ps[:, :], ACT.Tanh, scale=0.5).then_inc(spare_free[j], 1)
            if name == "relu":
                wait_full(act, c, "kk")
                act.activation(kr[l].rearrange("p t n -> p (t n)"), spare(c, "kk")[0][:, :], ACT.Relu).then_inc(kr_ready[l], 1)
            if name == "ka_hi":
                wait_evacuated(act, c, "kk")
                act.activation(halves(l, "ka")[0][:, :, :], kr[l], ACT.Copy).then_inc(hi_ready[l], 1)
            if name == "mbT_out":
                ps, j, _ = spare(c, "mbT")
                wait_full(act, c, "mbT")
                act.activation(flat(mbT[l]), ps[:, :].bitcast(F16)[:, 0:TT * L], ACT.Copy).then_inc(spare_free[j], 1)
            if name == "xnT_out":
                ps, j, _ = spare(c, "xnT3")
                wait_full(act, c, "xnT3")
                act.activation(xnT_all[:, :, bass.ds((e * LANES + l) * L, L)], tiled(ps[:, :]), ACT.Copy).then_inc(spare_free[j], 1)

        walk(act, run)

    @block.tensor
    def _(pe):
        pe.wait_ge(id_done, 1)
        pe.wait_ge(consts_ready, 1)
        pe.wait_ge(w_lo_ready, 1)
        pe.wait_ge(band_set, 4 + 2 * LANES)

        def claim(c, use):
            ps, j, k = spare(c, use)
            pe.wait_ge(spare_free[j], k + 1)
            return ps, spare_full[j]

        def transposes(c, src, use):
            ps, full = claim(c, use)
            for t in range(TT):
                for k in range(CT):
                    ins = pe.transpose(ps[:, k * L + t * P:k * L + (t + 1) * P], src[:, t, k * P:(k + 1) * P], ident[:, :])
            ins.then_inc(full, 1)

        def product(c, mat, hi, lo, use, weights_first):
            m = MATS.index(mat)
            ps, full = claim(c, use)
            terms = [(a, w, m, k, 0) for k in range(CT) for a, w in ((hi, w_hi), (hi, w_lo), (lo, w_hi))]
            if mat in SCALED:
                terms += [(a, w, PAST + SCALED.index(mat), k, 1) for k in range(CT) for a, w in ((hi, w_hi), (hi, w_lo), (lo, w_hi))]
            for t in range(2):
                for n, (a, w, wm, k, back) in enumerate(terms):
                    at = (GAP if mat in ("r", "kk", "o", "out") else 0) - back
                    if weights_first:
                        lhsT, rhs = w[:, wm, k, t * P:(t + 1) * P], a[:, k, at:at + L]
                    else:
                        lhsT, rhs = a[:, k, at + t * P:at + (t + 1) * P], w[:, wm, k, :]
                    ins = pe.matmul(ps[:, t * L:(t + 1) * L], lhsT, rhs, start=(n == 0), stop=(n == len(terms) - 1 and use not in BIASED))
                if use in BIASED:
                    ins = pe.matmul(ps[:, t * L:(t + 1) * L], ones[0:2, :], bias_rows[0:2, BIASED[use], :], start=False, stop=True)
            ins.then_inc(full, 1)

        def proj(c, which):
            l, e = c.l, c.e
            if which == "k":
                wait_hi(pe, c, "c")
                pe.wait_ge(cl_ready[l], e + 1)
                product(c, "k", ch[l], cl[l], "k", True)
            if which == "v":
                product(c, "v", ch[l], cl[l], "v", False)
            if which == "q":
                wait_hi(pe, c, "xnT0")
                wait_evacuated(pe, c, "xnT0")
                product(c, "q", x0h[l], x0l[l], "q", True)
            if which == "kk":
                wait_hi(pe, c, "xnT1")
                wait_evacuated(pe, c, "xnT1")
                product(c, "kk", xh[l], xl[l], "kk", True)
            if which == "r":
                product(c, "r", xh[l], xl[l], "r", False)
            if which == "kv":
                wait_hi(pe, c, "ka")
                pe.wait_ge(ka_lo_ready[l], e + 1)
                product(c, "kv", kh[l], kl[l], "kv", False)
            if which in ("ao0", "ao1"):
                layer = int(which[-1])
                wait_hi(pe, c, f"oT{layer}")
                wait_evacuated(pe, c, f"oT{layer}")
                product(c, ("o", "out")[layer], xh[l], xl[l], which, False)

        def maxima(c, layer, n):
            l, e = c.l, c.e
            kst = (kst0 if layer == 0 else kst1)[l]
            if n == 0:
                pe.wait_ge(q_stacked[l], e * 96 + 48 * layer + 48)
                pe.wait_ge(m_cleared[l], e * 32 + 16 * layer + 16)
                pe.wait_ge((k_stacked if layer == 0 else c_stacked)[l], e * 48 + 48)
                if layer == 1:
                    pe.wait_ge(mb_ready[l], e + 1)
            t, h = tile_heads(n)
            ps = max_ps[n % 2]
            pe.wait_ge(max_free, MAX_TURNS.of(c, layer) * 16 + n + 1)
            if layer == 0:
                off = (1 - t) * P
                pe.matmul(ps[:, :, off:off + P], ident16[:, :], band[:, t, :].unsqueeze(1).to_broadcast([P, 2, P]),
                          start=True, stop=False, skip_group_check=True)
            else:
                pe.matmul(ps[:, :, :], ident16[:, :], mb[l][:, t, :].unsqueeze(1).to_broadcast([P, 2, L]),
                          start=True, stop=False, skip_group_check=True)
            for a in range(2):
                ins = pe.matmul(ps[:, a, :], qst[l][:, h + a, t * P:(t + 1) * P], kst[:, h + a, :],
                                start=False, stop=(a == 1), skip_group_check=True)
            ins.then_inc(max_full, 1)

        def score(c, layer, u):
            l, e = c.l, c.e
            kst = (kst0 if layer == 0 else kst1)[l]
            if u % HALF_H == 0:
                pe.wait_ge(m_stacked[l][u // HALF_H], e * 32 + 16 * layer + 16)
                if layer == 1 and u == 0:
                    wait_evacuated(pe, c, "mbT")
            ps = score_ps[u % 3]
            pe.wait_ge(exp_done, ATT_TURNS.of(c, layer) * H + (u + 1 if u else 3))
            if layer == 0:
                pe.matmul(flat(ps)[:, P:3 * P], ident16[:, :], band[:, :, :].rearrange("p a n -> p (a n)"),
                          start=True, stop=False, skip_group_check=True)
            else:
                pe.matmul(flat(ps), ident16[:, :], flat(mbT[l]), start=True, stop=False, skip_group_check=True)
            for t in range(TT):
                ins = pe.matmul(ps[:, t, :], kst[:, u, t * P:(t + 1) * P], qst[l][:, u, :],
                                start=False, stop=(t == TT - 1), skip_group_check=True)
            ins.then_inc(score_full, 1)

        def weigh(c, layer, g):
            l, e = c.l, c.e
            val = (val0 if layer == 0 else val1)[l]
            if g == 0:
                if layer == 0:
                    pe.wait_ge(v_ready[l], e + 1)
                else:
                    pe.wait_ge(val_ready[l], e + 1)
            if g % 2 == 0:
                pe.wait_ge(out_free, OUT_TURNS.of(c, (layer, g // 2)) + 1)
            pe.wait_ge(exp_done, ATT_TURNS.of(c, layer) * H + 4 * g + 4 + 3)
            for t in range(TT):
                for r in range(4):
                    ins = pe.matmul(out_ps[VW * r:VW * (r + 1), g % 2, :], val[:, t, 4 * g + r, :],
                                    pT[:, (4 * g + r) % RING, t, :], start=(t == 0), stop=(t == TT - 1),
                                    skip_group_check=True, tile_position=(0, VW * r))
            ins.then_inc(pv_done, 1)

        def run(c, step):
            l, e, name = c.l, c.e, step[0]
            if name == "T":
                wait_normal(pe, c, step[1], xn0_ready, xn_ready)
                transposes(c, xn0[l] if step[1] == 0 else xn[l], f"xnT{step[1]}")
            if name == "proj":
                proj(c, step[1])
            if name == "max":
                maxima(c, step[1], step[2])
            if name == "mT":
                _, layer, g = step
                ps, full = claim(c, f"mT{layer}{g}")
                pe.wait_ge(max_free, MAX_TURNS.of(c, layer) * 16 + 8 * (g + 1) + 2)
                for t in range(TT):
                    ins = pe.transpose(ps[0:HALF_H, t * P:(t + 1) * P], mx[l][:, t, g * HALF_H:(g + 1) * HALF_H], ident[:, :])
                ins.then_inc(full, 1)
            if name == "att":
                score(c, step[1], step[2])
            if name == "weigh":
                weigh(c, step[1], step[2])
            if name == "oN":
                _, layer, t = step
                pe.wait_ge(out_free, OUT_TURNS.of(c, (layer, 1)) + 2)
                ps, full = claim(c, f"oN{layer}{t}")
                for g in range(4):
                    ins = pe.transpose(ps[:, g * P:(g + 1) * P], oT[l][:, g, t * P:(t + 1) * P], ident[:, :])
                ins.then_inc(full, 1)
            if name == "oT":
                layer = step[1]
                for t in range(TT):
                    wait_evacuated(pe, c, f"oN{layer}{t}")
                transposes(c, on[l], f"oT{layer}")
            if name == "mbT":
                pe.wait_ge(mb_ready[l], e + 1)
                ps, full = claim(c, "mbT")
                for k in range(TT):
                    for t in range(TT):
                        ins = pe.transpose(ps[:, :].bitcast(F16)[:, k * L + t * P:k * L + (t + 1) * P],
                                           mb[l][:, t, k * P:(k + 1) * P], ident16[:, :])
                ins.then_inc(full, 1)

        walk(pe, run)

    @block.vector
    def _(dve):
        dve.memset(zrow[:, :], 0.0)
        for l in range(LANES):
            dve.memset(qst[l][:, :, :], 0.0)
            dve.memset(xh[l][:, :, 0:GAP], 0.0)
            dve.memset(xl[l][:, :, 0:GAP], 0.0)
            dve.memset(val0[l][:, :, :, :], 0.0)
        dve.memset(amax[:, :], 0.0).then_inc(zero_set, 1)
        dve.wait_ge(zero_set, 1)
        for l in range(LANES):
            dve.memset(val0[l][:, :, :, DH:DH + 1], 1.0)
        dve.wait_ge(id_done, 1)
        dve.tensor_copy(ident16[:, :], ident[:, :]).then_inc(consts_ready, 1)
        dve.wait_ge(consts_ready, 1)
        for s, ahead in ((spare_free[0], 1), (spare_free[1], 1), (max_free, 2), (exp_done, 3), (pv_done, 2), (out_free, 1),
                         (x3_stored[0], 16), (x3_stored[1], 16), (val1_free[0], 1), (val1_free[1], 1)):
            dve.sem_inc(s, ahead)
        dve.wait_ge(setup_loaded, 16 * SETUP_DMAS)
        dve.tensor_scalar(omu[:, :, :], mu, -1.0, 1.0, ALU.mult, ALU.add).then_inc(omu_ready, 1)
        dve.tensor_copy(bias_rows[:, :, :], rows).then_inc(bias_step, 1)
        dve.wait_ge(bias_step, 1)
        dve.tensor_copy(rows_hi, bias_rows[:, :, :]).then_inc(bias_step, 1)
        dve.wait_ge(bias_step, 2)
        dve.tensor_tensor(rows, rows, rows_hi, ALU.subtract).then_inc(bias_step, 1)
        dve.wait_ge(bias_step, 3)
        dve.tensor_scalar(rows_hi, rows_hi, ident[:, 0:1], None, ALU.mult).then_inc(bias_step, 1)
        dve.wait_ge(bias_step, 4)
        dve.scalar_tensor_tensor(out=bias_rows[:, :, :], in0=rows, scalar=ident[:, 1:2], in1=rows_hi, op0=ALU.mult, op1=ALU.add)
        halved = 0
        for m, mat in enumerate(MATS):
            if mat not in SCALED:
                halved += 1
                dve.wait_ge(w_hi_ready, halved)
                dve.tensor_tensor(w_lo[:, m, :, :], stage[:, m], w_hi[:, m, :, :], ALU.subtract)
        for s, mat in enumerate(SCALED):
            for t in range(CT):
                for m, factor in ((MATS.index(mat), mu), (PAST + s, omu)):
                    halved += 1
                    dve.wait_ge(w_hi_ready, halved)
                    ins = dve.scalar_tensor_tensor(out=w_lo[:, m, t, :], in0=stage[:, MATS.index(mat), t], scalar=factor[:, s, t:t + 1],
                                                   in1=w_hi[:, m, t, :], op0=ALU.mult, op1=ALU.subtract)
        ins.then_inc(w_lo_ready, 1)
        dve.wait_ge(w_lo_ready, 1)

        links = {"prologue": 0, "body": 0, "epilogue": 0}

        def link(c, ins):
            links[c.seg] += 1
            ins.then_inc(dve_step, 1)
            before = 0 if c.seg == "prologue" else links["prologue"] + c.i * BODY_LINKS
            dve.wait_ge(dve_step, before + links[c.seg])

        def low(c, use):
            ps, j, _ = spare(c, use)
            hi, lo = halves(c.l, use)
            wait_full(dve, c, use)
            wait_hi(dve, c, use)
            dve.tensor_tensor(lo[:, :, :], tiled(ps[:, :]), hi[:, :, :], ALU.subtract).then_inc(spare_free[j], 1)

        def run(c, step):
            l, e, name = c.l, c.e, step[0]
            if name == "stats":
                n = step[1]
                src = xin[l] if n == 0 else xres[l]
                if n == 0:
                    dve.wait_ge(x_loaded[l], e * 16 + 16)
                for t in range(TT):
                    ins = dve.bn_stats(st[l][:, int(n > 0), t, :], src[:, t, :])
                link(c, ins)
                dve.sem_inc(stats_seen, 1)
                for t in range(TT):
                    ins = dve.bn_aggr(mv[l][:, int(n > 0), t, :], st[l][:, int(n > 0), t, :])
                link(c, ins)
                dve.tensor_scalar(ve[l][:, int(n > 0)], mv[l][:, int(n > 0), :, 1], EPS, None, ALU.add).then_inc((var0_ready if n == 0 else var_ready)[l], 1)
            if name == "xn":
                n = step[1]
                src, dst = (xin[l], xn0[l]) if n == 0 else (xres[l], xn[l])
                wait_normal(dve, c, n, rstd0_ready, rstd_ready)
                if n == 2:
                    link(c, dve.tensor_tensor(rs[l][:, 1], rs[l][:, 1], anyk[l][:, :], ALU.mult))
                for t in range(TT):
                    ins = dve.tensor_scalar(dst[:, t, :], src[:, t, :], mv[l][:, int(n > 0), t, 0:1], rs[l][:, int(n > 0), t:t + 1], ALU.subtract, ALU.mult)
                ins.then_inc((xn0_ready if n == 0 else xn_ready)[l], 1)
            if name == "mask":
                dve.wait_ge(mk_loaded[l], e * 16 + 16)
                link(c, dve.tensor_scalar(mb[l][:, :, :], mk[l][:, :, :], 0.0, None, ALU.not_equal))
                link(c, dve.tensor_reduce(anyk[l][:, :], mb[l][:, :, :], AX.X, ALU.max))
                link(c, dve.tensor_scalar(anyn[l][:, :], anyk[l][:, :], NEG, None, ALU.mult))
                for t in range(TT):
                    ins = dve.tensor_scalar(mb[l][:, t, :], mk[l][:, t, :], 0.0, anyn[l][:, t:t + 1], ALU.is_equal, ALU.mult)
                ins.then_inc(mb_ready[l], 1)
            if name == "T_lo":
                low(c, step[1])
            if name == "lo":
                hi, lo, bias = {"q": (qh[l], ql[l], bias_q), "k": (kh[l], kl[l], bias_k)}[step[1]]
                ps, j, _ = spare(c, step[1])
                wait_full(dve, c, step[1])
                wait_hi(dve, c, step[1])
                for t in range(CT):
                    ins = dve.scalar_tensor_tensor(out=lo[:, t, :], in0=ps[:, t * L:(t + 1) * L], scalar=bias[:, t:t + 1],
                                                   in1=hi[:, t, :], op0=ALU.add, op1=ALU.subtract)
                ins.then_inc(spare_free[j], 1)
            if name == "max":
                _, layer, n = step
                t, h = tile_heads(n)
                dve.wait_ge(max_full, MAX_TURNS.of(c, layer) * 16 + n + 1)
                dve.tensor_reduce(mx[l][:, t, h:h + 2], max_ps[n % 2][:, :, :], AX.X, ALU.max).then_inc(max_free, 1)
            if name == "gather":
                _, layer, a = step
                dve.wait_ge(pv_done, ATT_TURNS.of(c, layer) * 4 + 2 * a + 2 + 2)
                dve.tensor_copy(oT[l][:, 2 * a:2 * a + 2, :], out_ps[:, :, :]).then_inc(out_free, 1)
                if (layer, a) == (1, 1):
                    dve.sem_inc(val1_free[l], 1)
            if name == "divide":
                _, layer, t = step
                use = f"oN{layer}{t}"
                ps, j, _ = spare(c, use)
                wait_full(dve, c, use)
                heads = ps[:, :].rearrange("p (h w) -> p h w", w=VW)
                link(c, dve.reciprocal(rc[l][:, t, :], heads[:, :, DH]))
                dve.tensor_tensor(on[l][:, t, :].rearrange("p (h d) -> p h d", d=DH), heads[:, :, 0:DH],
                                  rc[l][:, t, :].unsqueeze(2).to_broadcast([P, H, DH]), ALU.mult).then_inc(spare_free[j], 1)
            if name == "join":
                layer = step[1]
                use = f"ao{layer}"
                ps, j, _ = spare(c, use)
                wait_full(dve, c, use)
                if layer == 0:
                    dve.wait_ge(x3_stored[l], e * 16 + 16)
                dve.tensor_tensor(flat(xres[l]), ps[:, :], flat(xin[l] if layer == 0 else xres[l]), ALU.add).then_inc(spare_free[j], 1)
                wait_evacuated(dve, c, use)
                dve.sem_inc((used_dve if layer == 0 else x3_ready)[l], 1)
            if name == "square":
                ps, j, _ = spare(c, "kk")
                dve.wait_ge(kr_ready[l], e + 1)
                keys = kr[l].rearrange("p t n -> p (t n)")
                dve.scalar_tensor_tensor(out=keys, in0=ps[:, :], scalar=0.0, in1=keys,
                                         op0=ALU.max, op1=ALU.mult).then_inc(spare_free[j], 1)
            if name == "ka_lo":
                wait_hi(dve, c, "ka")
                wait_evacuated(dve, c, "kk")
                hi, lo = halves(l, "ka")
                dve.tensor_tensor(lo[:, :, :], kr[l], hi[:, :, :], ALU.subtract).then_inc(ka_lo_ready[l], 1)
            if name == "x2":
                ps, j, _ = spare(c, "kv")
                wait_full(dve, c, "kv")
                wait_evacuated(dve, c, "r")
                dve.scalar_tensor_tensor(out=flat(on[l]), in0=flat(on[l]), scalar=1.0, in1=ps[:, :],
                                         op0=ALU.add, op1=ALU.mult).then_inc(spare_free[j], 1)
                wait_evacuated(dve, c, "kv")
                dve.scalar_tensor_tensor(out=flat(xres[l]), in0=flat(on[l]), scalar=0.5, in1=flat(xres[l]),
                                         op0=ALU.mult, op1=ALU.add).then_inc(x2_ready[l], 1)
                dve.wait_ge(x2_ready[l], e + 1)
            if name == "amax":
                wait_normal(dve, c, 3, None, xn_ready)
                dve.tensor_reduce(amax[:, bass.ds(e * LANES + l, 1)], xn[l][:, :, :], AX.XY, ALU.max,
                                  apply_absolute_value=True).then_inc(amax_done[l], 1)

        walk(dve, run)
        assert links["body"] == BODY_LINKS, links
        for l in range(LANES):
            dve.wait_ge(amax_done[l], B // LANES)


I = 768
OT = I // P
PAIRS = OT // 2
BLK = 32
N = B * L
CH = 512
NCH = N // CH
QA, QW = 32767.0, 7.0


def quantized_ffn(nc, ctx, xnT_all, amax, ident, x3, wg, wu, wd, out):
    def sb(name, shape, dt=F32):
        return ctx.enter_context(nc.sbuf_tensor(name, shape, dt))

    def sem(name):
        return ctx.enter_context(nc.semaphore(name))

    hid = sb("hid", [P, OT, N])
    x_hi, x_lo = sb("x_hi", [P, CT, N], F16), sb("x_lo", [P, CT, N], F16)
    wT_hi = [sb(f"wT_hi{m}", [P, CT * I], F16) for m in range(3)]
    wT_lo = [sb(f"wT_lo{m}", [P, CT * I], F16) for m in range(3)]
    steps16 = sb("steps16", [P, 2, OT, CH], I16)
    blk_s, blk_r = sb("blk_s", [P, 3, I * CT // BLK]), sb("blk_r", [P, 3, I * CT // BLK])
    sc = sb("sc", [P, 32])
    g_max, p_max, u_max, q_max = sb("g_max", [P, NCH]), sb("p_max", [P, NCH]), sb("u_max", [P, NCH, PAIRS]), sb("q_max", [P, NCH])

    w_nat = [hid[:, 0, :]] + [sb(f"w_nat{m}", [P, CT * I]) for m in (1, 2)]
    w_step = sb("w_step", [P, CT * I], I16)
    work = xnT_all[:, :, :].rearrange("p t n -> p (t n)")
    sig = work[:, 0:OT * CH].rearrange("p (o n) -> p o n", o=OT)
    half = [work[:, OT * CH + j * OT * CH // 2:OT * CH + (j + 1) * OT * CH // 2] for j in range(2)]
    sig16 = [h.bitcast(U16).rearrange("p (o n) -> p o n", o=OT) for h in half]
    up16 = [h.bitcast(I16).rearrange("p (o n) -> p o n", o=OT) for h in half]
    rest = work[:, 2 * OT * CH:2 * OT * CH + 4 * 2 * D].rearrange("p (j t d) -> p j t d", j=4, d=D)
    x3_in, y_out = [rest[:, j] for j in range(2)], [rest[:, 2 + j] for j in range(2)]
    tokens = x_hi[:, :, :].rearrange("p t n -> p (t n)"), x_lo[:, :, :].rearrange("p t n -> p (t n)")
    o_hi, o_lo = [[half[:, j * OT * CH:(j + 1) * OT * CH].rearrange("p (o n) -> p o n", o=OT) for j in range(2)] for half in tokens]
    xq = [steps16[:, 0, 2 * j:2 * j + 2, :] for j in range(2)]
    x32 = [steps16[:, 1, 2 * j:2 * j + 2, :] for j in range(2)]

    s_x, c_x, s_gate, c_gate, s_gated, c_gated, s_up, c_up, s_o, c_o = [sc[:, 12 + k:13 + k] for k in range(10)]
    u_sig, u_o, tmp = [sc[:, 22 + k:23 + k] for k in range(3)]

    unit_ps = [ctx.enter_context(nc.psum_tensor(f"unit_ps{j}", [P, 2, CH], F32)) for j in range(PAIRS)]
    down_ps = [ctx.enter_context(nc.psum_tensor(f"down_ps{j}", [P, 2, D], F32)) for j in range(2)]

    w_loaded = [sem(f"w_loaded{m}") for m in range(3)]
    w_quantized, wT_full, wT_hi_done, wT_free = sem("w_quantized"), sem("wT_full"), sem("wT_hi_done"), sem("wT_free")
    max_in, max_out, scale_step = sem("max_in"), sem("max_out"), sem("scale_step")
    xq_ready, x32_ready, x_hi_ready, x_lo_ready = sem("xq_ready"), sem("x32_ready"), sem("x_hi_ready"), sem("x_lo_ready")
    unit_full, unit_free, gate_max_done = sem("unit_full"), sem("unit_free"), sem("gate_max_done")
    gated_scale, o_scale = sem("gated_scale"), sem("o_scale")
    gate_scale, gate16_ready, sig_ready, sig16_ready, prod_ready = sem("gate_scale"), sem("gate16_ready"), sem("sig_ready"), sem("sig16_ready"), sem("prod_ready")
    up_scale, gated16_ready, both_ready = sem("up_scale"), sem("gated16_ready"), sem("both_ready")
    o16_ready, o32_ready, o_hi_ready, o_lo_ready = sem("o16_ready"), sem("o32_ready"), sem("o_hi_ready"), sem("o_lo_ready")
    down_full, down_free, down_done = sem("down_full"), sem("down_free"), sem("down_done")
    x3_loaded, y_stored = [sem("x3_loaded0"), sem("x3_loaded1")], [sem("y_stored0"), sem("y_stored1")]

    x3_v = x3.rearrange("b l d -> (b l) d").rearrange("(g t p) d -> g p t d", t=2, p=P)
    out_v = out.rearrange("b l d -> (b l) d").rearrange("(g t p) d -> g p t d", t=2, p=P)

    block = ctx.enter_context(nc.Block())

    @block.sync
    def _(sp):
        for m, w in enumerate((wg, wu)):
            sp.dma_start(w_nat[m][:, 0:CT * I].rearrange("p (t c) -> p t c", c=D), w.rearrange("(t p) c -> p t c", p=P)).then_inc(w_loaded[m], 16)
        sp.dma_start(w_nat[2][:, 0:CT * I].rearrange("p (t c) -> p t c", c=I), wd.rearrange("(t p) c -> p t c", p=P)).then_inc(w_loaded[2], 16)
        with sp.Fori(0, NCH) as n:
            for g in range(2):
                sp.wait_ge(down_free, n * 2 + g + 3)
                sp.dma_start(out_v[n * 2 + g], y_out[g]).then_inc(y_stored[g], 16)
        for g in range(2):
            sp.wait_ge(y_stored[g], 16 * NCH + 16)

    @block.gpsimd
    def _(pool):
        for k in range(5):
            pool.wait_ge(max_in, k + 1)
            pool.partition_all_reduce(sc[:, 2 * k + 1:2 * k + 2], sc[:, 2 * k:2 * k + 1], P, RMAX).then_inc(max_out, 1)
        with pool.Fori(0, NCH) as n:
            for g in range(2):
                pool.wait_ge(down_free, n * 2 + g + 1)
                pool.dma_start(x3_in[g], x3_v[n * 2 + g]).then_inc(x3_loaded[g], 16)

    def weight_block(m, k):
        if m < 2:
            o, c = k // CT, k % CT
            return w_nat[m][:, o * D + c * P:o * D + (c + 1) * P], c * I + o * P
        h, t = k % CT, k // CT
        return w_nat[m][:, h * I + t * P:h * I + (t + 1) * P], t * D + h * P

    def turned(n):
        return down_ps[n % 2][:, :, :].rearrange("p t d -> p (t d)")

    def weight_dst(w, m, k):
        _, at = weight_block(m, k)
        return w[m][:, at:at + P]

    @block.scalar
    def _(act):
        def weight_highs(m):
            for n in range(3 * m, 3 * m + 3):
                act.wait_ge(wT_full, n + 1)
                for j in range(4):
                    ins = act.activation(weight_dst(wT_hi, m, n % 3 * 4 + j), turned(n)[:, j * P:(j + 1) * P], ACT.Copy)
                ins.then_inc(wT_hi_done, 1)

        def token_highs(n, a):
            act.wait_ge(x32_ready, n + 1)
            act.activation(x_hi[:, :, bass.ds(n * CH, CH)], x32[a], ACT.Copy, scale=32.0).then_inc(x_hi_ready, 1)

        def keep_gate(n):
            for j in range(PAIRS):
                act.wait_ge(unit_full, n * PAIRS + j + 1)
                act.activation(hid[:, 2 * j:2 * j + 2, bass.ds(n * CH, CH)], unit_ps[j][:, :, :], ACT.Copy).then_inc(unit_free, 1)

        weight_highs(0)
        token_highs(0, 0)
        for n in range(3):
            token_highs(n + 1, (n + 1) % 2)
            keep_gate(n)
            if n in (0, 2):
                weight_highs(1 + n // 2)
        with act.Fori(0, (NCH - 4) // 2) as n2:
            for a in range(2):
                token_highs(n2 * 2 + a + 4, a)
                keep_gate(n2 * 2 + a + 3)
        keep_gate(NCH - 1)
        act.wait_ge(gate_scale, 1)
        with act.Fori(0, NCH // 2) as n2:
            for a in range(2):
                n = n2 * 2 + a
                act.wait_ge(prod_ready, n + 1)
                act.activation(steps16[:, a], hid[:, :, bass.ds(n * CH, CH)], ACT.Identity, scale=c_gate).then_inc(gate16_ready, 1)
                act.wait_ge(gate16_ready, n + 1)
                act.wait_ge(sig16_ready, n + 1)
                act.activation(sig, steps16[:, a], ACT.Sigmoid, scale=s_gate).then_inc(sig_ready, 1)
                act.wait_ge(sig_ready, n + 1)
                act.activation(sig16[a], sig, ACT.Copy, scale=65536.0).then_inc(sig16_ready, 1)
        act.wait_ge(up_scale, 1)
        act.wait_ge(gated_scale, 1)
        with act.Fori(0, NCH // 2) as n2:
            for a in range(2):
                n = n2 * 2 + a
                act.wait_ge(both_ready, n + 1)
                for j in range(PAIRS):
                    act.wait_ge(unit_full, n * PAIRS + j + 1 + 2 * NCH * PAIRS)
                    act.activation(up16[a][:, 2 * j:2 * j + 2, :], unit_ps[j][:, :, :], ACT.Identity, scale=c_up).then_inc(unit_free, 1)
                act.activation(steps16[:, a], hid[:, :, bass.ds(n * CH, CH)], ACT.Identity, scale=c_gated).then_inc(gated16_ready, 1)

        def hidden_steps(n, a):
            act.activation(steps16[:, a], hid[:, :, bass.ds(n * CH, CH)], ACT.Identity, scale=c_o).then_inc(o16_ready, 1)

        def hidden_highs(n, a):
            act.wait_ge(o32_ready, n + 1)
            act.wait_ge(down_done, n + 1)
            act.activation(o_hi[a], up16[a], ACT.Copy, scale=32.0).then_inc(o_hi_ready, 1)

        act.wait_ge(o_scale, 1)
        hidden_steps(0, 0)
        hidden_highs(0, 0)
        hidden_steps(1, 1)
        with act.Fori(0, NCH // 2 - 1) as n2:
            for a in range(2):
                act.wait_ge(o_lo_ready, n2 * 2 + a + 1)
                hidden_steps(n2 * 2 + a + 2, a)
                hidden_highs(n2 * 2 + a + 1, 1 - a)
        hidden_highs(NCH - 1, 1)

    @block.tensor
    def _(pe):
        def turn_weights(m):
            for n in range(3 * m, 3 * m + 3):
                pe.wait_ge(w_quantized, m + 1)
                if n >= 2:
                    pe.wait_ge(wT_free, n - 1)
                for j in range(4):
                    src, _ = weight_block(m, n % 3 * 4 + j)
                    ins = pe.transpose(turned(n)[:, j * P:(j + 1) * P], src, ident[:, :])
                ins.then_inc(wT_full, 1)

        def units(n, m, first):
            for j in range(PAIRS):
                done_before = first + j
                pe.wait_ge(unit_free, n * PAIRS + done_before + 1)
                for a in range(2):
                    o, k = 2 * j + a, 0
                    for c in range(CT):
                        for w, xx in ((wT_hi, x_hi), (wT_lo, x_hi), (wT_hi, x_lo)):
                            ins = pe.matmul(unit_ps[j][:, a, :], w[m][:, c * I + o * P:c * I + (o + 1) * P],
                                            xx[:, c, bass.ds(n * CH, CH)], start=(k == 0), stop=(k == 3 * CT - 1))
                            k += 1
                ins.then_inc(unit_full, 1)

        def gate(n):
            pe.wait_ge(x_hi_ready, n + 1)
            pe.wait_ge(x_lo_ready, n + 1)
            units(n, 0, 0)

        turn_weights(0)
        pe.wait_ge(wT_free, 3)
        for n in range(3):
            gate(n)
            if n in (0, 2):
                turn_weights(1 + n // 2)
        with pe.Fori(3, NCH) as n:
            gate(n)
        pe.wait_ge(wT_free, 9)
        for p in (1, 2):
            with pe.Fori(0, NCH) as n:
                units(n, 1, p * NCH * PAIRS)
        with pe.Fori(0, NCH // 2) as n2:
            for a in range(2):
                n = n2 * 2 + a
                pe.wait_ge(o_hi_ready, n + 1)
                pe.wait_ge(o_lo_ready, n + 1)
                for g in range(2):
                    pe.wait_ge(down_free, n * 2 + g + 1)
                    for t in range(2):
                        k = 0
                        tok = slice((2 * g + t) * P, (2 * g + t + 1) * P)
                        for o in range(OT):
                            for w, hh in ((wT_hi, o_hi), (wT_lo, o_hi), (wT_hi, o_lo)):
                                ins = pe.matmul(down_ps[g][:, t, :], hh[a][:, o, tok], w[2][:, o * D:(o + 1) * D],
                                                start=(k == 0), stop=(k == 3 * OT - 1))
                                k += 1
                    ins.then_inc(down_full, 1)
                pe.drain().then_inc(down_done, 1)

    @block.vector
    def _(dve):
        for s, v in ((y_stored[0], 16), (y_stored[1], 16), (unit_free, PAIRS), (prod_ready, 2), (sig16_ready, 1), (both_ready, 2), (down_done, 2), (down_free, 2)):
            dve.sem_inc(s, v)
        steps = [0]

        def link(ins):
            steps[0] += 1
            ins.then_inc(scale_step, 1)
            dve.wait_ge(scale_step, steps[0])

        def whole_max(k, parts):
            dve.tensor_reduce(sc[:, 2 * k:2 * k + 1], parts, AX.X if len(parts.shape) == 2 else AX.XY, ALU.max).then_inc(max_in, 1)

        def scales(k, unit, s, c):
            dve.wait_ge(max_out, k + 1)
            if unit is None:
                link(dve.tensor_scalar(s, sc[:, 2 * k + 1:2 * k + 2], 1.0 / QA, 1e-12, ALU.mult, ALU.max))
                link(dve.reciprocal(c, s))
                return
            link(dve.tensor_tensor(tmp, sc[:, 2 * k + 1:2 * k + 2], unit, ALU.mult))
            link(dve.tensor_scalar(s, tmp, 1.0 / QA, 1e-12, ALU.mult, ALU.max))
            link(dve.reciprocal(tmp, s))
            link(dve.tensor_tensor(c, tmp, unit, ALU.mult))

        def split_tokens(n, a):
            if not isinstance(n, int) or n >= 2:
                dve.wait_ge(x_hi_ready, n - 1)
            dve.tensor_scalar(xq[a], xnT_all[:, :, bass.ds(n * CH, CH)], c_x, None, ALU.mult).then_inc(xq_ready, 1)
            dve.wait_ge(xq_ready, n + 1)
            dve.tensor_scalar(x32[a], xq[a], 1.0 / 32, None, ALU.mult).then_inc(x32_ready, 1)
            dve.wait_ge(x32_ready, n + 1)
            dve.scalar_tensor_tensor(out=x_lo[:, :, bass.ds(n * CH, CH)], in0=x32[a], scalar=-32.0, in1=xq[a],
                                     op0=ALU.mult, op1=ALU.add).then_inc(x_lo_ready, 1)

        def gate_maximum(n):
            dve.wait_ge(unit_free, n * PAIRS + 2 * PAIRS)
            dve.tensor_reduce(g_max[:, bass.ds(n, 1)], hid[:, :, bass.ds(n * CH, CH)], AX.XY, ALU.max,
                              apply_absolute_value=True).then_inc(gate_max_done, 1)

        whole_max(0, amax[:, :])
        nb = CT * I // BLK

        def quantize_weights(m):
            dve.wait_ge(w_loaded[m], 16)
            blocks = w_nat[m][:, 0:CT * I].rearrange("p (b e) -> p b e", e=BLK)
            s, r = blk_s[:, m], blk_r[:, m]
            link(dve.tensor_reduce(r, blocks, AX.X, ALU.max, apply_absolute_value=True))
            link(dve.tensor_scalar(s, r, 1.0 / QW, 1e-12, ALU.mult, ALU.max))
            link(dve.reciprocal(r, s))
            step = w_step[:, :].rearrange("p (b e) -> p b e", e=BLK)
            link(dve.tensor_tensor(step, blocks, r.unsqueeze(2).to_broadcast([P, nb, BLK]), ALU.mult))
            link(dve.tensor_scalar(w_step[:, :], w_step[:, :], QW, -QW - 1.0, ALU.min, ALU.max))
            dve.tensor_tensor(blocks, step, s.unsqueeze(2).to_broadcast([P, nb, BLK]), ALU.mult).then_inc(w_quantized, 1)
            dve.wait_ge(w_quantized, m + 1)

        def weight_lows(m):
            for n in range(3 * m, 3 * m + 3):
                dve.wait_ge(wT_hi_done, n + 1)
                for j in range(4):
                    ins = dve.tensor_tensor(weight_dst(wT_lo, m, n % 3 * 4 + j), turned(n)[:, j * P:(j + 1) * P],
                                            weight_dst(wT_hi, m, n % 3 * 4 + j), ALU.subtract)
                ins.then_inc(wT_free, 1)

        quantize_weights(0)
        scales(0, None, s_x, c_x)
        split_tokens(0, 0)
        weight_lows(0)
        split_tokens(1, 1)
        quantize_weights(1)
        split_tokens(2, 0)
        weight_lows(1)
        gate_maximum(0)
        split_tokens(3, 1)
        quantize_weights(2)
        gate_maximum(1)
        weight_lows(2)
        gate_maximum(2)
        with dve.Fori(0, (NCH - 4) // 2) as n2:
            for a in range(2):
                split_tokens(n2 * 2 + a + 4, a)
                gate_maximum(n2 * 2 + a + 3)
        gate_maximum(NCH - 1)
        dve.wait_ge(gate_max_done, NCH)
        whole_max(1, g_max[:, :])
        scales(1, s_x, s_gate, c_gate)
        link(dve.tensor_scalar(u_sig, s_gate, 1.0 / 65536, None, ALU.mult))
        dve.sem_inc(gate_scale, 1)
        def up_maximum(n):
            for j in range(PAIRS):
                dve.wait_ge(unit_full, n * PAIRS + j + 1 + NCH * PAIRS)
                dve.tensor_reduce(u_max[:, bass.ds(n, 1), j:j + 1], unit_ps[j][:, :, :], AX.XY, ALU.max,
                                  apply_absolute_value=True).then_inc(unit_free, 1)

        def gated_maximum(n, a):
            dve.wait_ge(sig16_ready, n + 2)
            dve.tensor_tensor(hid[:, :, bass.ds(n * CH, CH)], steps16[:, a], sig16[a], ALU.mult).then_inc(prod_ready, 1)
            dve.wait_ge(prod_ready, n + 3)
            dve.tensor_reduce(p_max[:, bass.ds(n, 1)], hid[:, :, bass.ds(n * CH, CH)], AX.XY, ALU.max,
                              apply_absolute_value=True).then_inc(gate_max_done, 1)

        up_maximum(0)
        up_maximum(1)
        with dve.Fori(0, NCH // 2 - 1) as n2:
            for a in range(2):
                gated_maximum(n2 * 2 + a, a)
                up_maximum(n2 * 2 + a + 2)
        gated_maximum(NCH - 2, 0)
        gated_maximum(NCH - 1, 1)
        dve.wait_ge(gate_max_done, 2 * NCH)
        dve.tensor_reduce(sc[:, 4:5], u_max[:, :, :], AX.XY, ALU.max).then_inc(max_in, 1)
        dve.tensor_reduce(sc[:, 6:7], p_max[:, :], AX.X, ALU.max).then_inc(max_in, 1)
        scales(2, s_x, s_up, c_up)
        dve.sem_inc(up_scale, 1)
        scales(3, u_sig, s_gated, c_gated)
        dve.sem_inc(gated_scale, 1)
        link(dve.tensor_tensor(u_o, s_gated, s_up, ALU.mult))
        with dve.Fori(0, NCH // 2) as n2:
            for a in range(2):
                n = n2 * 2 + a
                dve.wait_ge(gated16_ready, n + 1)
                dve.wait_ge(unit_free, n * PAIRS + 2 * PAIRS + 2 * NCH * PAIRS)
                dve.tensor_tensor(hid[:, :, bass.ds(n * CH, CH)], steps16[:, a], up16[a], ALU.mult).then_inc(both_ready, 1)
                dve.wait_ge(both_ready, n + 3)
                dve.tensor_reduce(q_max[:, bass.ds(n, 1)], hid[:, :, bass.ds(n * CH, CH)], AX.XY, ALU.max,
                                  apply_absolute_value=True).then_inc(gate_max_done, 1)
        dve.wait_ge(gate_max_done, 3 * NCH)
        dve.tensor_reduce(sc[:, 8:9], q_max[:, :], AX.X, ALU.max).then_inc(max_in, 1)
        scales(4, u_o, s_o, c_o)
        dve.sem_inc(o_scale, 1)

        def join(m, g):
            dve.wait_ge(down_full, m * 2 + g + 1)
            dve.wait_ge(x3_loaded[g], m * 16 + 16)
            dve.wait_ge(y_stored[g], m * 16 + 16)
            dve.scalar_tensor_tensor(out=y_out[g], in0=down_ps[g][:, :, :], scalar=s_o, in1=x3_in[g],
                                     op0=ALU.mult, op1=ALU.add).then_inc(down_free, 1)

        def split_hidden(n, a):
            dve.wait_ge(o16_ready, n + 1)
            dve.tensor_scalar(up16[a], steps16[:, a], 1.0 / 32, None, ALU.mult).then_inc(o32_ready, 1)
            dve.wait_ge(o32_ready, n + 1)
            dve.wait_ge(down_done, n + 1)
            dve.scalar_tensor_tensor(out=o_lo[a], in0=up16[a], scalar=-32.0, in1=steps16[:, a],
                                     op0=ALU.mult, op1=ALU.add).then_inc(o_lo_ready, 1)

        split_hidden(0, 0)
        with dve.Fori(0, NCH // 2 - 1) as n2:
            for a in range(2):
                split_hidden(n2 * 2 + a + 1, 1 - a)
                for g in range(2):
                    join(n2 * 2 + a, g)
        split_hidden(NCH - 1, 1)
        for n in (NCH - 2, NCH - 1):
            for g in range(2):
                join(n, g)


_INS = ["x", "ctxN", "ctxT", "mask", "WT", "COLS", "ROWS", "wg", "wu", "wd"]


def kernel(**z):
    import numpy as np
    import concourse.bacc as bacc
    from concourse.bass_utils import run_bass_kernel_spmd

    z = {k: np.asarray(v) for k, v in z.items()}
    ctx = z["ctx_1024"]
    arrays = {
        "x": z["x"], "ctxN": ctx, "ctxT": ctx.transpose(0, 2, 1), "mask": z["mask_Bx1xSxS2_ik1"].reshape(B, L, L),
        "WT": np.stack([z[n].T for n in ("L0_xattn_Wq", "L0_xattn_Wk", "L0_xattn_Wv", "L0_xattn_Wo",
                                         "L0_ffn_W_r", "L0_ffn_W_k", "L0_ffn_W_v", "L1_xattn_W_out")]),
        "COLS": np.stack([z[n].reshape(CT, P).T for n in ("L0_xattn_bq", "L0_xattn_bk", "L0_ffn_mu_r", "L0_ffn_mu_k")], 1),
        "ROWS": np.stack([z[n] for n in ("L0_xattn_bv", "L0_xattn_bo", "L1_xattn_b_out")]),
        "wg": z["L1_ffn_w_gate"], "wu": z["L1_ffn_w_up"], "wd": z["L1_ffn_w_down"],
    }
    arrays = {k: np.ascontiguousarray(v) for k, v in arrays.items()}
    nc = bacc.Bacc("TRN2", target_bir_lowering=False, num_devices=1)
    args = [nc.dram_tensor(k, arrays[k].shape, mybir.dt.from_np(arrays[k].dtype), kind="ExternalInput").ap() for k in _INS]
    args.append(nc.dram_tensor("out", [B, L, D], F32, kind="ExternalOutput").ap())
    build(nc, *args)
    r = run_bass_kernel_spmd(nc, [arrays], core_ids=[0])
    return r.results[0]["out"]
```
